# Optimizing a Trainium2 kernel written in Bass

```python
import numpy as np
import jax
import jax.numpy as jnp

def _softmax(x, axis=-1):
    return jax.nn.softmax(x, axis=axis)

def _gelu(x):
    return jax.nn.gelu(x, approximate=True)

def _silu(x):
    return jax.nn.silu(x)

def _sigmoid(x):
    return jax.nn.sigmoid(x)

def _layernorm(x, axis=-1, eps=1e-05):
    m = jnp.mean(x, axis=axis, keepdims=True)
    v = jnp.var(x, axis=axis, keepdims=True)
    return (x - m) / jnp.sqrt(v + eps)

def _scatter_add(tgt, idx, src, axis=0):
    return tgt.at[idx].add(src)

def _segment_sum(src, seg, n):
    return jax.ops.segment_sum(src, seg, n)
kernel_name = 'mk_adaln_d2_jaxref_r8_aecc3e'

def setup_inputs(seed: int=0):
    np.random.seed(seed)
    _w = jnp.asarray

    def _L0_attn_setup():
        import jax, jax.numpy as jnp
        import numpy as np
        B, S, DIM = (2, 256, 128)
        H, DH = (16, 64)
        WIN = 64
        key = jax.random.key(seed)
        k1, k2, k3 = jax.random.split(key, 3)
        x = jax.random.normal(k1, (B, S, DIM), dtype=jnp.float32)
        Wqkv = jax.random.normal(k2, (DIM, 3 * H * DH), dtype=jnp.float32) * DIM ** (-0.5)
        Wout = jax.random.normal(k3, (H * DH, DIM), dtype=jnp.float32) * (H * DH) ** (-0.5)
        return {'x': x, 'Wqkv': Wqkv, 'Wout': Wout}
    _L0_attn_in = _L0_attn_setup()

    def _L0_ffn_setup():
        import jax, jax.numpy as jnp
        import numpy as np
        H = 128
        I = 256
        E = 8
        B, S = (2, 512)
        EPS = 1e-05
        INIT = 0.02

        def _layernorm(x, w, b):
            mu = jnp.mean(x, axis=-1, keepdims=True)
            var = jnp.mean(jnp.square(x - mu), axis=-1, keepdims=True)
            return (x - mu) * jax.lax.rsqrt(var + EPS) * w + b
        key = jax.random.key(seed)
        ks = jax.random.split(key, 9)
        return {'hidden_states': jax.random.normal(ks[0], (B, S, H), jnp.float32), 'ln_w': jnp.ones((H,), jnp.float32), 'ln_b': jnp.zeros((H,), jnp.float32), 'router_w': jax.random.normal(ks[1], (H, E), jnp.float32) * INIT, 'gate_w': jax.random.normal(ks[2], (E, H, I), jnp.float32) * INIT, 'up_w': jax.random.normal(ks[3], (E, H, I), jnp.float32) * INIT, 'down_w': jax.random.normal(ks[4], (E, I, H), jnp.float32) * INIT, 'sh_gate': jax.random.normal(ks[5], (H, I), jnp.float32) * INIT, 'sh_up': jax.random.normal(ks[6], (H, I), jnp.float32) * INIT, 'sh_down': jax.random.normal(ks[7], (I, H), jnp.float32) * INIT}
    _L0_ffn_in = _L0_ffn_setup()
    _L0_c = _w((lambda *s: np.random.randn(*s).astype(np.float32) * 0.05)(32, 128))
    _L0_wmod = _w((lambda *s: np.random.randn(*s).astype(np.float32) * 0.05)(128, 6 * 128) * 128 ** (-0.5))

    def _L1_attn_setup():
        import jax, jax.numpy as jnp
        import numpy as np
        DIM = 128
        QK_DIM = 128
        HIDDEN = 256
        B, N = (4, 512)

        def _layernorm(x, g, b, eps=1e-05):
            mu = jnp.mean(x, axis=-1, keepdims=True)
            var = jnp.var(x, axis=-1, keepdims=True)
            return (x - mu) * jax.lax.rsqrt(var + eps) * g + b
        key = jax.random.key(seed)
        ks = jax.random.split(key, 10)
        std = 0.02
        return {'x': jax.random.normal(ks[0], (B, N, DIM), dtype=jnp.float32), 'ln_g': jnp.ones((DIM,), jnp.float32), 'ln_b': jnp.zeros((DIM,), jnp.float32), 'W_hidden': jax.random.normal(ks[1], (DIM, 2 * HIDDEN), jnp.float32) * (1.0 / np.sqrt(DIM)), 'b_hidden': jnp.zeros((2 * HIDDEN,), jnp.float32), 'W_qk': jax.random.normal(ks[2], (DIM, QK_DIM), jnp.float32) * (1.0 / np.sqrt(DIM)), 'b_qk': jnp.zeros((QK_DIM,), jnp.float32), 'os_gamma': jax.random.normal(ks[3], (2, QK_DIM), jnp.float32) * std, 'os_beta': jnp.zeros((2, QK_DIM), jnp.float32), 'W_out': jax.random.normal(ks[4], (HIDDEN, DIM), jnp.float32) * (1.0 / np.sqrt(HIDDEN)), 'b_out': jnp.zeros((DIM,), jnp.float32)}
    _L1_attn_in = _L1_attn_setup()

    def _L1_ffn_setup():
        import jax, jax.numpy as jnp
        import numpy as np
        B, S, D, F, E = (4, 512, 128, 256, 8)
        key = jax.random.key(seed)
        ks = jax.random.split(key, 8)
        x = jax.random.normal(ks[0], (B, S, D), dtype=jnp.float32)
        Wr = jax.random.normal(ks[1], (D, E), dtype=jnp.float32) * 0.02
        br = jnp.zeros((E,), dtype=jnp.float32)
        W1 = jax.random.normal(ks[2], (E, D, F), dtype=jnp.float32) * (1.0 / np.sqrt(D))
        b1 = jnp.zeros((E, F), dtype=jnp.float32)
        W2 = jax.random.normal(ks[3], (E, F, D), dtype=jnp.float32) * (1.0 / np.sqrt(F))
        b2 = jnp.zeros((E, D), dtype=jnp.float32)
        return {'x': x, 'Wr': Wr, 'br': br, 'W1': W1, 'b1': b1, 'W2': W2, 'b2': b2}
    _L1_ffn_in = _L1_ffn_setup()
    _L1_c = _w((lambda *s: np.random.randn(*s).astype(np.float32) * 0.05)(32, 128))
    _L1_wmod = _w((lambda *s: np.random.randn(*s).astype(np.float32) * 0.05)(128, 6 * 128) * 128 ** (-0.5))
    _d = {'L0_attn_x': _L0_attn_in['x'], 'L0_attn_Wqkv': _L0_attn_in['Wqkv'], 'L0_attn_Wout': _L0_attn_in['Wout'], 'L0_ffn_ln_w': _L0_ffn_in['ln_w'], 'L0_ffn_ln_b': _L0_ffn_in['ln_b'], 'L0_ffn_router_w': _L0_ffn_in['router_w'], 'L0_ffn_gate_w': _L0_ffn_in['gate_w'], 'L0_ffn_up_w': _L0_ffn_in['up_w'], 'L0_ffn_down_w': _L0_ffn_in['down_w'], 'L0_ffn_sh_gate': _L0_ffn_in['sh_gate'], 'L0_ffn_sh_up': _L0_ffn_in['sh_up'], 'L0_ffn_sh_down': _L0_ffn_in['sh_down'], 'L0_c': _L0_c, 'L0_wmod': _L0_wmod, 'L1_attn_ln_g': _L1_attn_in['ln_g'], 'L1_attn_ln_b': _L1_attn_in['ln_b'], 'L1_attn_W_hidden': _L1_attn_in['W_hidden'], 'L1_attn_b_hidden': _L1_attn_in['b_hidden'], 'L1_attn_W_qk': _L1_attn_in['W_qk'], 'L1_attn_b_qk': _L1_attn_in['b_qk'], 'L1_attn_os_gamma': _L1_attn_in['os_gamma'], 'L1_attn_os_beta': _L1_attn_in['os_beta'], 'L1_attn_W_out': _L1_attn_in['W_out'], 'L1_attn_b_out': _L1_attn_in['b_out'], 'L1_ffn_Wr': _L1_ffn_in['Wr'], 'L1_ffn_br': _L1_ffn_in['br'], 'L1_ffn_W1': _L1_ffn_in['W1'], 'L1_ffn_b1': _L1_ffn_in['b1'], 'L1_ffn_W2': _L1_ffn_in['W2'], 'L1_ffn_b2': _L1_ffn_in['b2'], 'L1_c': _L1_c, 'L1_wmod': _L1_wmod}
    _x0 = _d['L0_attn_x']
    _d['L0_attn_x'] = jax.random.normal(jax.random.fold_in(jax.random.key(seed), 1), (32, 256, 128), dtype=_x0.dtype)
    del _x0
    return _d

def reference(L0_attn_x, L0_attn_Wqkv, L0_attn_Wout, L0_ffn_ln_w, L0_ffn_ln_b, L0_ffn_router_w, L0_ffn_gate_w, L0_ffn_up_w, L0_ffn_down_w, L0_ffn_sh_gate, L0_ffn_sh_up, L0_ffn_sh_down, L0_c, L0_wmod, L1_attn_ln_g, L1_attn_ln_b, L1_attn_W_hidden, L1_attn_b_hidden, L1_attn_W_qk, L1_attn_b_qk, L1_attn_os_gamma, L1_attn_os_beta, L1_attn_W_out, L1_attn_b_out, L1_ffn_Wr, L1_ffn_br, L1_ffn_W1, L1_ffn_b1, L1_ffn_W2, L1_ffn_b2, L1_c, L1_wmod):

    def _L0_attn_ref(x, Wqkv, Wout):
        import jax, jax.numpy as jnp
        import numpy as np
        B, S, DIM = (2, 256, 128)
        H, DH = (16, 64)
        WIN = 64
        b, s, _ = x.shape
        qkv = jnp.einsum('bsd,de->bse', x, Wqkv)
        q, k, v = jnp.split(qkv, 3, axis=-1)
        q = q.reshape(b, s, H, DH).transpose(0, 2, 1, 3)
        k = k.reshape(b, s, H, DH).transpose(0, 2, 1, 3)
        v = v.reshape(b, s, H, DH).transpose(0, 2, 1, 3)
        scale = DH ** (-0.5)
        scores = jnp.einsum('bhsd,bhtd->bhst', q, k) * scale
        i = jnp.arange(s)[:, None]
        j = jnp.arange(s)[None, :]
        mask = (j >= i - WIN + 1) & (j <= i)
        mask_value = -jnp.finfo(scores.dtype).max
        scores = jnp.where(mask[None, None], scores, mask_value)
        attn = jax.nn.softmax(scores, axis=-1)
        out = jnp.einsum('bhst,bhtd->bhsd', attn, v)
        out = out.transpose(0, 2, 1, 3).reshape(b, s, H * DH)
        return jnp.einsum('bse,ed->bsd', out, Wout)

    def _L0_ffn_ref(hidden_states, ln_w, ln_b, router_w, gate_w, up_w, down_w, sh_gate, sh_up, sh_down):
        import jax, jax.numpy as jnp
        import numpy as np
        H = 128
        I = 256
        E = 8
        B, S = (2, 512)
        EPS = 1e-05
        INIT = 0.02

        def _layernorm(x, w, b):
            mu = jnp.mean(x, axis=-1, keepdims=True)
            var = jnp.mean(jnp.square(x - mu), axis=-1, keepdims=True)
            return (x - mu) * jax.lax.rsqrt(var + EPS) * w + b
        b, s, h = hidden_states.shape
        normed = _layernorm(hidden_states, ln_w, ln_b)
        xf = normed.reshape(-1, h)
        logits = xf @ router_w
        top_idx = jnp.argmax(logits, axis=-1)
        top_score = jax.nn.sigmoid(jnp.max(logits, axis=-1))

        def body(acc, ew):
            g, u, d, e = ew
            w = jnp.where(top_idx == e, top_score, 0.0)[:, None]
            xe = xf * w
            hmid = jax.nn.silu(xe @ g) * (xe @ u)
            return (acc + hmid @ d, None)
        routed, _ = jax.lax.scan(body, jnp.zeros_like(xf), (gate_w, up_w, down_w, jnp.arange(E)))
        shared = jax.nn.silu(xf @ sh_gate) * (xf @ sh_up) @ sh_down
        moe_out = (routed + shared).reshape(b, s, h)
        return hidden_states + moe_out

    def _L1_attn_ref(x, ln_g, ln_b, W_hidden, b_hidden, W_qk, b_qk, os_gamma, os_beta, W_out, b_out):
        import jax, jax.numpy as jnp
        import numpy as np
        DIM = 128
        QK_DIM = 128
        HIDDEN = 256
        B, N = (4, 512)

        def _layernorm(x, g, b, eps=1e-05):
            mu = jnp.mean(x, axis=-1, keepdims=True)
            var = jnp.var(x, axis=-1, keepdims=True)
            return (x - mu) * jax.lax.rsqrt(var + eps) * g + b
        n = x.shape[-2]
        normed = _layernorm(x, ln_g, ln_b)
        hidden = jax.nn.silu(normed @ W_hidden + b_hidden)
        v, gate = jnp.split(hidden, 2, axis=-1)
        qk = jax.nn.silu(normed @ W_qk + b_qk)
        q = qk * os_gamma[0] + os_beta[0]
        k = qk * os_gamma[1] + os_beta[1]
        sim = jnp.einsum('bid,bjd->bij', q, k)
        denom = (jnp.arange(n, dtype=x.dtype) + 1.0)[:, None]
        sim = sim / denom
        attn = jnp.square(jax.nn.relu(sim))
        causal_mask = jnp.triu(jnp.ones((n, n), dtype=bool), k=1)
        attn = jnp.where(causal_mask, 0.0, attn)
        out = jnp.einsum('bij,bjd->bid', attn, v)
        out = out * gate
        out = out @ W_out + b_out
        return out + x

    def _L1_ffn_ref(x, Wr, br, W1, b1, W2, b2):
        import jax, jax.numpy as jnp
        import numpy as np
        B, S, D, F, E = (4, 512, 128, 256, 8)
        logits = jnp.einsum('bsd,de->bse', x, Wr) + br
        probs = jax.nn.softmax(logits, axis=-1)
        expert_weights = jnp.max(probs, axis=-1)
        expert_indices = jnp.argmax(probs, axis=-1)
        num_experts = W1.shape[0]
        out = jnp.zeros_like(x)
        for e in range(num_experts):
            h = jax.nn.gelu(jnp.einsum('bsd,df->bsf', x, W1[e]) + b1[e], approximate=False)
            y = jnp.einsum('bsf,fd->bsd', h, W2[e]) + b2[e]
            out = jnp.where((expert_indices == e)[..., None], y, out)
        return out * expert_weights[..., None]
    x = L0_attn_x
    mod = (_silu(L0_c) @ L0_wmod).reshape(L0_c.shape[0], 6, 1, -1)
    sa, ca, ga, sb, cb, gb = (mod[:, 0], mod[:, 1], mod[:, 2], mod[:, 3], mod[:, 4], mod[:, 5])
    ga = (2 * (ga >= 0) - 1) * jnp.maximum(jnp.abs(ga), 0.25)
    gb = (2 * (gb >= 0) - 1) * jnp.maximum(jnp.abs(gb), 0.25)
    h = _layernorm(x, axis=-1) * (1 + ca) + sa
    x = x + ga * _L0_attn_ref(h, L0_attn_Wqkv, L0_attn_Wout)
    h = _layernorm(x, axis=-1) * (1 + cb) + sb
    x = x + gb * _L0_ffn_ref(h, L0_ffn_ln_w, L0_ffn_ln_b, L0_ffn_router_w, L0_ffn_gate_w, L0_ffn_up_w, L0_ffn_down_w, L0_ffn_sh_gate, L0_ffn_sh_up, L0_ffn_sh_down)
    mod = (_silu(L1_c) @ L1_wmod).reshape(L1_c.shape[0], 6, 1, -1)
    sa, ca, ga, sb, cb, gb = (mod[:, 0], mod[:, 1], mod[:, 2], mod[:, 3], mod[:, 4], mod[:, 5])
    ga = (2 * (ga >= 0) - 1) * jnp.maximum(jnp.abs(ga), 0.25)
    gb = (2 * (gb >= 0) - 1) * jnp.maximum(jnp.abs(gb), 0.25)
    h = _layernorm(x, axis=-1) * (1 + ca) + sa
    x = x + ga * _L1_attn_ref(h, L1_attn_ln_g, L1_attn_ln_b, L1_attn_W_hidden, L1_attn_b_hidden, L1_attn_W_qk, L1_attn_b_qk, L1_attn_os_gamma, L1_attn_os_beta, L1_attn_W_out, L1_attn_b_out)
    h = _layernorm(x, axis=-1) * (1 + cb) + sb
    x = x + gb * _L1_ffn_ref(h, L1_ffn_Wr, L1_ffn_br, L1_ffn_W1, L1_ffn_b1, L1_ffn_W2, L1_ffn_b2)
    return x

_drawn_inputs = setup_inputs


def setup_inputs(seed=0):
    import zlib

    import numpy as np

    out = dict(_drawn_inputs(seed))
    spreads = {'L0_ffn_ln_w': (1.0, 0.6),
     'L0_ffn_ln_b': (0.0, 0.8),
     'L1_attn_ln_g': (1.0, 0.2),
     'L1_attn_ln_b': (0.0, 0.1),
     'L1_attn_b_hidden': (0.0, 0.1),
     'L1_attn_b_qk': (0.0, 0.1),
     'L1_attn_os_beta': (0.0, 2.0),
     'L1_attn_b_out': (0.0, 1.833),
     'L1_ffn_br': (0.0, 2.0),
     'L1_ffn_b1': (0.0, 2.0),
     'L1_ffn_b2': (0.0, 2.0)}
    factors = {'L0_ffn_router_w': 8.0,
     'L0_ffn_gate_w': 8.0,
     'L0_ffn_up_w': 8.0,
     'L0_ffn_down_w': 8.0,
     'L0_ffn_sh_gate': 8.0,
     'L0_ffn_sh_up': 8.0,
     'L0_ffn_sh_down': 8.0,
     'L1_ffn_Wr': 5.872,
     'L1_ffn_W1': 8.0,
     'L1_ffn_W2': 6.865}
    for name, (base, spread) in spreads.items():
        noise = np.random.default_rng([zlib.crc32(name.encode()), seed]).standard_normal(out[name].shape)
        drawn = base * np.exp(spread * noise) if base else spread * noise
        out[name] = jnp.asarray(drawn.astype(out[name].dtype))
    for name, factor in factors.items():
        out[name] = (out[name] * factor).astype(out[name].dtype)
    return out
```

```python
from contextlib import ExitStack

import concourse.bass as bass
import concourse.mybir as mybir
from concourse.alu_op_type import AluOpType as ALU

F32 = mybir.dt.float32
F32R = mybir.dt.float32r
BF16 = mybir.dt.bfloat16
U32 = mybir.dt.uint32
ACT = mybir.ActivationFunctionType
AX = mybir.AxisListType

B, S, D = 32, 256, 128
TILES = B * S // 128
HEADS, DH = 16, 64
UNITS = 4
E, F = 8, 256
EPS = 1e-5
GATE_MIN = 0.25
MASKED = -1e30
CAP = B * S + 128
SLOTS = TILES + E
SENT = 132
NEWTON = 3
LOADS = 16
SA, CA, GA, SB, CB, GB = range(6)

C_IDENT, C_WINDOW, C_BEFORE, C_ONES, C_REGION, C_INDEX, C_CAUSAL, C_SLOT, C_ROW, C_EPS = 0, 128, 384, 512, 640, 648, 656, 1040, 1112, 1113
C_ALL = 1120


def constants():
    import numpy as np
    c = np.zeros((128, C_ALL), np.float32)
    p, j = np.arange(128)[:, None], np.arange(128)[None, :]
    c[:, C_IDENT:C_IDENT + 128] = p == j
    first = (j <= p) & (j >= p - 63)
    r = p % 64
    second = (j >= r + 1) & (j <= r + 64)
    c[:, C_WINDOW:C_WINDOW + 128] = np.where(first, 0, MASKED)
    c[:, C_WINDOW + 128:C_WINDOW + 256] = np.where(second, 0, MASKED)
    c[:, C_BEFORE:C_BEFORE + 128] = p < j
    c[:, C_ONES:C_ONES + 128] = 1
    c[:, C_REGION:C_REGION + E] = np.arange(E) * CAP
    c[:, C_INDEX:C_INDEX + E] = np.arange(E)
    i = np.arange(256)[None, :]
    c[:, C_CAUSAL:C_CAUSAL + 256] = (i >= p) / (i + 1.0)
    c[:, C_CAUSAL + 256:C_CAUSAL + 384] = (j >= p) / (j + 129.0)
    c[:, C_SLOT:C_SLOT + SLOTS] = np.arange(SLOTS)
    c[:, C_ROW] = np.arange(128)
    c[:, C_EPS] = EPS
    return c


def need(engine, semaphore, value):
    if not (isinstance(value, int) and value <= 0):
        engine.wait_ge(semaphore, value)


def wait_apart(engine, semaphore, value, passed):
    if not (isinstance(value, int) and value <= 0):
        engine.wait_ge(semaphore, value)
        engine.sem_inc(passed, 1)


def last(owner):
    return min(owner, B - 1) if isinstance(owner, int) else owner


def real(owner, count=B):
    return not isinstance(owner, int) or 0 <= owner < count


def turns(engine, body, count=B, unroll=1, ahead=1, behind=2):
    start = -(-(behind + 1) // unroll) * unroll
    end = (count - ahead) // unroll * unroll
    for n in range(-ahead, start):
        body(n, n % unroll, n // unroll)
    with engine.Fori(start // unroll, end // unroll) as i:
        for k in range(unroll):
            body(unroll * i + k, k, i)
    for n in range(end, count + behind):
        body(n, n % unroll, n // unroll)


def clear(nc, semaphores):
    with nc.Block() as block:
        @block.gpsimd
        def _(pool):
            for semaphore in semaphores:
                pool.sem_clear(semaphore)


def cols(start, size):
    return bass.ds(start, size)


def program(nc, t, out):
    ctx = ExitStack()
    with ctx:
        def sb(name, columns, kind=F32, rows=128):
            return ctx.enter_context(nc.sbuf_tensor(name, [rows, columns], kind))

        def sem(name):
            return ctx.enter_context(nc.semaphore(name))

        sent_done = [sem(f"sent_done{n}") for n in range(2)]
        got_in = [sem(f"got_in{n}") for n in range(3)]

        x = sb("x", TILES * D)
        const = sb("const", C_ALL)
        ident = const[:, C_IDENT:C_IDENT + 128]
        mod_col = [sb(f"mod_col{n}", 6 * B) for n in range(2)]
        rows_at = [sb(f"rows_at{n}", TILES) for n in range(2)]
        back_at = [sb(f"back_at{n}", TILES, U32) for n in range(2)]
        shifted = sb("shifted", TILES * E)
        counts = [sb(f"counts{n}", E) for n in range(2)]
        mod_row = [nc.dram_tensor(f"mod_row{n}", [B, 6 * D], F32, kind="Internal").ap() for n in range(2)]
        sent = [nc.dram_tensor(f"sent{n}", [(E + 1) * CAP, (SENT, D)[n]], F32, kind="Internal").ap() for n in range(2)]
        back = [nc.dram_tensor(f"back{n}", [SLOTS * 128, D], F32, kind="Internal").ap() for n in range(2)]
        banks = [ctx.enter_context(nc.psum_tensor(f"bank{n}", [128, 512], F32)) for n in range(8)]

        setup_and_attention0(nc, t, out, x, const, ident, mod_col, rows_at, counts, mod_row, sent, sent_done[0], banks)
        experts(nc, t, 0, counts[0], rows_at[0], back_at[0], sent[0], back[0], banks, const, ident)
        attention1(nc, t, x, const, ident, mod_col, mod_row, rows_at[1], back_at[0], counts[1], shifted, back[0], sent[1], got_in[0], sent_done[1], banks)
        experts(nc, t, 1, counts[1], rows_at[1], back_at[1], sent[1], back[1], banks, const, ident)
        combine(nc, out, x, mod_row[1], back_at[1], back[1], shifted, got_in[1:3])


def setup_and_attention0(nc, t, out, x, const, ident, mod_col, rows_at, counts, mod_row, sent, sent_done, banks):
    ctx = ExitStack()
    with ctx:
        def sb(name, columns, kind=F32, rows=128):
            return ctx.enter_context(nc.sbuf_tensor(name, [rows, columns], kind))

        used = []

        def sem(name):
            used.append(ctx.enter_context(nc.semaphore(name)))
            return used[-1]

        WQKV = 3 * HEADS * DH
        w_high, w_low = sb("w_high", WQKV, F32R), sb("w_low", WQKV, F32R)
        w_out = sb("w_out", HEADS * DH)
        router = sb("router", E)
        c_col = [sb(f"c_col{n}", B) for n in range(2)]
        w_mod = [sb(f"w_mod{n}", 6 * D) for n in range(2)]
        mod_stage = [sb(f"mod_stage{n}", 6 * D, rows=B) for n in range(2)]
        mod_tmp = sb("mod_tmp", 4 * D)
        ident_b, window_b, before_b, ones_b = sb("ident_b", 128, BF16), sb("window_b", 256, BF16), sb("before_b", 128, BF16), sb("ones_b", 128, BF16)
        ln_row = sb("ln_row", 2 * D)
        hT = sb("hT", 256)
        h_high, h_low = sb("h_high", 256, F32R), sb("h_low", 256, F32R)
        qk = [sb(f"qk{n}", 1024) for n in range(2)]
        v = [sb(f"v{n}", 768) for n in range(4)]
        probs = [sb(f"probs{n}", 1024) for n in range(2)]
        probsT = [sb(f"probsT{n}", 1024) for n in range(2)]
        neg_max, sums, inverse = sb("neg_max", 16), sb("sums", 16), sb("inverse", 16)
        attn = sb("attn", 8 * 256)
        yT = sb("yT", 256)
        stats, moments = sb("stats", 3 * 12), sb("moments", 3 * 4)
        log_var, rstd = sb("log_var", 3 * 2), sb("rstd", 3 * 2)
        z_a, z_b, z_c, h_b, g_b = (sb(n, 256) for n in ("z_a", "z_b", "z_c", "h_b", "g_b"))
        mod_b = sb("mod_b", 3 * D)
        send = sb("send", 2 * SENT)
        nT = sb("nT", 256)
        logits, top, top_at, hot, hot_b = sb("logits", 16), sb("top", 16), sb("top_at", 16, U32), sb("hot", 16), sb("hot_b", 16, BF16)
        expert = sb("expert", 2)
        low_top, exp_top = sb("low_top", 2), sb("exp_top", 2)
        place, picked, place_f = sb("place", 16), sb("picked", 16), sb("place_f", 2)
        rows_now = sb("rows_now", 2, U32)

        names = """passed_dve passed_pool consts_in small_in weights_in x_in mod_sent  c_silu mod_made mod_taken mod_rows_made
              split_done consts_cast
            scores_ready negmax_ready exp_done inverse_ready norm_done pt_ready pt_taken
            qk0_ready qk1_ready v_ready qk0_taken qk1_taken v_taken attn_ready attn_taken
            y_ready y_taken yt_ready yt_taken zt_ready zt_taken split_ready nt_ready nt_taken
            lg_ready lg_taken log_a log_b log_c parts_a parts_b parts_c setup_steps high_done top_done top_at_done low_top_done expert_done hot_done place_made picked_done place_summed score_steps scaled_b scaled_c gated_b hot_ready rk_ready rk_taken
            stats_a stats_b stats_c rstd_a rstd_b rstd_c z_a_done z_b_done z_c_done h_b_done x_b_done send_done
            mod_b_in  exp_top_done score_done place_done
                     """.split()
        s = {n: sem("a_" + n) for n in names}
        v_shifted = [sem(f"a_v_shifted{n}") for n in range(4)]
        scores_bank, pt_bank, proj_bank = banks[0:2], banks[2:4], banks[4:6]
        attn_bank, misc = banks[6], banks[7]

        ctx_block = ExitStack()
        block = ctx_block.enter_context(nc.Block())

        @block.sync
        def _(sp):
            sp.dma_start(const[:], t["consts"]).then_inc(s["consts_in"], 16)
            for n in range(2):
                sp.dma_start(c_col[n][:], t[f"c{n}T"]).then_inc(s["small_in"], 16)
                sp.dma_start(w_mod[n][:], t[f"L{n}_wmod"]).then_inc(s["small_in"], 16)
            sp.dma_start(router[:], t["L0_ffn_router_w"]).then_inc(s["small_in"], 16)
            for n, name in enumerate(("L0_ffn_ln_w", "L0_ffn_ln_b")):
                sp.dma_start(ln_row[:, n * D:(n + 1) * D], t[name].partition_broadcast(128)).then_inc(s["small_in"], 16)
            for n in range(3):
                for half in range(2):
                    sp.dma_start((probs, probsT, qk)[n][half][:, 0:512], t["L0_attn_Wqkv"][:, n * 1024 + half * 512:n * 1024 + half * 512 + 512]).then_inc(s["weights_in"], 16)
            sp.dma_start(w_out[:].rearrange("p (c n) -> p c n", n=D), t["L0_attn_Wout"].rearrange("(c p) n -> p c n", p=128)).then_inc(s["small_in"], 16)
            x_dram = t["L0_attn_x"].rearrange("b (i p) d -> p (b i) d", p=128)
            x_view = x[:].rearrange("p (n d) -> p n d", d=D)
            for n in range(4):
                sp.dma_start(x_view[:, n * 16:(n + 1) * 16], x_dram[:, n * 16:(n + 1) * 16]).then_inc(s["x_in"], 16)
            for n in range(2):
                sp.wait_ge(s["mod_rows_made"], n + 1)
                sp.dma_start(mod_row[n], mod_stage[n][:]).then_inc(s["mod_sent"], 16)
            sp.wait_ge(s["mod_sent"], 32)

            def body(b, _, __):
                for step in range(4):
                    g = 4 * b + step
                    if step == 0 and real(b - 1):
                        need(sp, s["x_b_done"], b - 1)
                        sp.dma_start(mod_b[:], mod_row[0][cols(b - 1, 1), SB * D:6 * D].broadcast_to([128, 3 * D])).then_inc(s["mod_b_in"], 16)
                    if real(b + 1 if step == 3 else b):
                        n = (step + 1) % 4
                        sp.wait_ge(s["v_taken"], g + 2)
                        sp.dma_start(v[n][0:64, 512:768], v[n][64:128, 0:256]).then_inc(v_shifted[n], 16)
                        sp.dma_start(v[n][64:128, 512:768], v[n][0:64, 256:512]).then_inc(v_shifted[n], 16)

            turns(sp, body)

        @block.tensor
        def _(pe):
            pe.wait_ge(s["small_in"], 128)
            pe.wait_ge(s["c_silu"], 2)
            for n in range(2):
                for j in range(6):
                    nc.tensor.matmul(banks[4 + n][:, j * B:(j + 1) * B], w_mod[n][:, j * D:(j + 1) * D], c_col[n][:], start=True, stop=True)
                nc.tensor.matmul(banks[2 * n][0:B, 0:384], c_col[n][:], w_mod[n][:, 0:384], start=True, stop=True)
                nc.tensor.matmul(banks[2 * n + 1][0:B, 0:384], c_col[n][:], w_mod[n][:, 384:768], start=True, stop=True).then_inc(s["mod_made"], 1)
            pe.wait_ge(s["consts_cast"], 1)
            pe.wait_ge(s["mod_taken"], 2)
            pe.wait_ge(s["split_done"], 1)

            def window(g, step, parity):
                need(pe, s["exp_done"], 2 * (g - 1) + parity + 1)
                bank, rows = scores_bank[parity], slice(64 * parity, 64 * parity + 64)
                nc.tensor.matmul(bank[:].rearrange("p (j w) -> p j w", j=2), ident_b[:], window_b[:].unsqueeze(1).broadcast_to([128, 2, 256]), start=True, stop=False, skip_group_check=True)
                for j in range(2):
                    q, k = qk[step % 2][rows, j * 512:j * 512 + 256], qk[step % 2][rows, j * 512 + 256:j * 512 + 512]
                    at = bank[:, j * 256:j * 256 + 256]
                    nc.tensor.matmul(at[:, 0:128], q[:, 0:128], k[:, 0:128], start=False, stop=True, skip_group_check=True)
                    nc.tensor.matmul(at[0:64, 128:256], q[:, 128:192], k[:, 64:192], start=False, stop=True, skip_group_check=True)
                    done = nc.tensor.matmul(at[64:128, 128:256], q[:, 192:256], k[:, 128:256], start=False, stop=True, skip_group_check=True)
                done.then_inc(s["scores_ready"], 1)

            def transpose_probs(g, step, parity):
                need(pe, s["norm_done"], 2 * g + parity + 1)
                need(pe, s["pt_taken"], 2 * (g - 1) + parity + 1)
                for n in range(4):
                    at = parity * 512 + n * 128
                    done = nc.tensor.transpose(pt_bank[parity][:, n * 128:n * 128 + 128], probs[step % 2][:, at:at + 128], ident)
                done.then_inc(s["pt_ready"], 1)

            def project(bank, parts):
                for n, (left_high, left_low, right_high, right_low, at) in enumerate(parts):
                    nc.tensor.matmul(at, left_high, right_high, start=True, stop=False)
                    nc.tensor.matmul(at, left_high, right_low, start=False, stop=False)
                    done = nc.tensor.matmul(at, left_low, right_high, start=False, stop=True)
                return done

            def project_qk(g, step, pair):
                n = (3 * step + pair) % 2
                need(pe, s["v_taken" if pair else "qk1_taken"], g)
                parts = []
                for i in range(2):
                    c = i * HEADS * DH + (2 * step + pair) * 128
                    parts.append((w_high[:, c:c + 128], w_low[:, c:c + 128], h_high[:], h_low[:], proj_bank[n][:, i * 256:i * 256 + 256]))
                project(proj_bank[n], parts).then_inc(s["qk1_ready" if pair else "qk0_ready"], 1)

            def project_v(g, step):
                n = (3 * step + 2) % 2
                need(pe, s["qk0_taken"], g + 1)
                c = 2 * HEADS * DH + step * 256
                parts = [(h_high[:, i * 128:i * 128 + 128], h_low[:, i * 128:i * 128 + 128], w_high[:, c:c + 256], w_low[:, c:c + 256], proj_bank[n][:, i * 256:i * 256 + 256]) for i in range(2)]
                project(proj_bank[n], parts).then_inc(s["v_ready"], 1)

            def apply_probs(g, step, owner):
                pe.wait_ge(s["pt_taken"], 2 * g + 2)
                pe.wait_ge(v_shifted[step], 32 * (owner + 1))
                need(pe, s["attn_taken"], g)
                for j in range(2):
                    for parity in range(2):
                        rows = slice(64 * parity, 64 * parity + 64)
                        head = (2 * j + parity) * DH
                        p = probsT[step % 2][:, parity * 512 + j * 256:parity * 512 + j * 256 + 256]
                        for value, a, e in ((0, 0, 128), (2, 128, 192), (1, 192, 256)):
                            done = nc.tensor.matmul(attn_bank[rows, j * 256 + a:j * 256 + e], v[step % 4][:, value * 256 + head:value * 256 + head + DH], p[:, a:e], start=True, stop=True, skip_group_check=True)
                done.then_inc(s["attn_ready"], 1)

            def body(b, _, __):
                for step in range(4):
                    g = 4 * b + step
                    before = b if step else b - 1
                    after = b + 1 if step == 3 else b
                    if real(b):
                        pe.wait_ge(s["qk0_taken"], g + 1)
                        pe.wait_ge(s["qk1_taken"], g + 1)
                        window(g, step, 0)
                        window(g, step, 1)
                    if real(before):
                        transpose_probs(g - 1, (step - 1) % 4, 0)
                        transpose_probs(g - 1, (step - 1) % 4, 1)
                    if step == 0 and real(b - 2):
                        pe.wait_ge(s["send_done"], b - 1)
                        pe.wait_ge(s["zt_taken"], last(b) + 1)
                        need(pe, s["rk_taken"], last(b - 3) + 1)
                        for i in range(2):
                            done = nc.tensor.transpose(misc[:, i * 128:i * 128 + 128], send[:, i * SENT:i * SENT + D], ident)
                        done.then_inc(s["nt_ready"], 1)
                    if step == 1 and real(b - 2):
                        pe.wait_ge(s["hot_ready"], b - 1)
                        nc.tensor.matmul(misc[:, 0:E], before_b[:], hot_b[:, 0:E], start=True, stop=True)
                        nc.tensor.matmul(misc[:, E:2 * E], ones_b[:], hot_b[:, 0:E], start=True, stop=False)
                        nc.tensor.matmul(misc[:, E:2 * E], before_b[:], hot_b[:, E:2 * E], start=False, stop=True)
                        nc.tensor.matmul(misc[:, 2 * E:3 * E], ones_b[:], hot_b[:, 0:E], start=True, stop=False)
                        nc.tensor.matmul(misc[:, 2 * E:3 * E], ones_b[:], hot_b[:, E:2 * E], start=False, stop=True).then_inc(s["rk_ready"], 1)
                    if step == 2 and real(b + 1):
                        pe.wait_ge(s["z_a_done"], b + 2)
                        need(pe, s["yt_taken"], last(b - 1) + 1)
                        need(pe, s["zt_taken"], b + 1)
                        for i in range(2):
                            done = nc.tensor.transpose(misc[:, i * 128:i * 128 + 128], z_a[:, i * 128:i * 128 + 128], ident)
                        done.then_inc(s["zt_ready"], 1)
                    if real(after):
                        if step == 3:
                            pe.wait_ge(s["split_ready"], b + 2)
                        project_qk(g + 1, (step + 1) % 4, 0)
                        project_qk(g + 1, (step + 1) % 4, 1)
                    if step == 1 and real(b - 1):
                        pe.wait_ge(s["attn_taken"], 4 * b)
                        pe.wait_ge(s["zt_taken"], last(b) + 1)
                        need(pe, s["rk_taken"], b - 1)
                        for c in range(8):
                            done = nc.tensor.matmul(misc[:, 0:256], w_out[:, c * D:(c + 1) * D], attn[:, c * 256:c * 256 + 256], start=c == 0, stop=c == 7)
                        done.then_inc(s["y_ready"], 1)
                    if real(before):
                        apply_probs(g - 1, (step - 1) % 4, before)
                    if real(after):
                        project_v(g + 1, (step + 1) % 4)
                    if step == 0 and real(b - 2):
                        pe.wait_ge(s["nt_taken"], b - 1)
                        for i in range(2):
                            done = nc.tensor.matmul(misc[:, i * E:(i + 1) * E], nT[:, i * 128:i * 128 + 128], router[:], start=True, stop=True)
                        done.then_inc(s["lg_ready"], 1)
                    if step == 1 and real(b - 1):
                        pe.wait_ge(s["y_taken"], b)
                        for i in range(2):
                            done = nc.tensor.transpose(misc[:, i * 128:i * 128 + 128], yT[:, i * 128:i * 128 + 128], ident)
                        done.then_inc(s["yt_ready"], 1)

            turns(pe, body)

        @block.scalar
        def _(act):
            act.wait_ge(s["small_in"], 128)
            for n in range(2):
                nc.scalar.activation(c_col[n][:], c_col[n][:], ACT.Silu).then_inc(s["c_silu"], 1)
            act.wait_ge(s["consts_in"], 16)
            act.wait_ge(s["split_done"], 1)
            nc.scalar.preload_act_table_set("natural_log_exp_and_others")

            def exponentials(g, step, parity):
                act.wait_ge(s["negmax_ready"], 2 * g + parity + 1)
                need(act, s["pt_ready"], 2 * (g - 2) + parity + 1)
                need(act, s["inverse_ready"], 2 * (g - 2) + parity + 1)
                for n in range(4):
                    slot = step % 2 * 8 + parity * 4 + n
                    at = parity * 512 + n * 128
                    done = nc.scalar.activation(probs[step % 2][:, at:at + 128], scores_bank[parity][:, n * 128:n * 128 + 128], ACT.Exp,
                                                bias=neg_max[:, slot:slot + 1], accum_out=sums[:, slot:slot + 1])
                done.then_inc(s["exp_done"], 1)

            def layer_norm_scale(owner, n, kind):
                act.wait_ge(s["stats_" + kind], owner + 1)
                variance = moments[:, 4 * n:4 * n + 4].rearrange("p (i two) -> p i two", two=2)[:, :, 1]
                nc.scalar.activation(log_var[:, 2 * n:2 * n + 2], variance, ACT.Ln, bias=const[:, C_EPS:C_EPS + 1]).then_inc(s["log_" + kind], 1)
                act.wait_ge(s["log_" + kind], owner + 1)
                nc.scalar.activation(rstd[:, 2 * n:2 * n + 2], log_var[:, 2 * n:2 * n + 2], ACT.Exp, scale=-0.5).then_inc(s["rstd_" + kind], 1)

            def body(b, _, __):
                for step in range(4):
                    g = 4 * b + step
                    before = b if step else b - 1
                    after = b + 1 if step == 3 else b
                    if step == 1 and real(b + 1):
                        layer_norm_scale(b + 1, 0, "a")
                    if real(b):
                        exponentials(g, step, 0)
                        exponentials(g, step, 1)
                    if step == 3 and real(b - 1):
                        layer_norm_scale(b - 1, 2, "c")
                    if step == 2 and real(b - 1):
                        layer_norm_scale(b - 1, 1, "b")
                    if step == 2 and real(b + 1):
                        act.wait_ge(s["zt_ready"], b + 2)
                        need(act, s["split_ready"], b + 1)
                        nc.scalar.activation(hT[:], misc[:, 0:256], ACT.Identity, scale=mod_col[0][:, cols(CA * B + b + 1, 1)],
                                             bias=mod_col[0][:, cols(SA * B + b + 1, 1)]).then_inc(s["zt_taken"], 1)
                    if real(after):
                        act.wait_ge(s["qk0_ready"], g + 2)
                        need(act, s["scores_ready"], 2 * g)
                        nc.scalar.copy(qk[(step + 1) % 2][:, 0:512], proj_bank[3 * ((step + 1) % 4) % 2][:]).then_inc(s["qk0_taken"], 1)
                    if step == 1 and real(b - 2):
                        act.wait_ge(s["low_top_done"], b - 1)
                        need(act, s["score_done"], b - 2)
                        nc.scalar.activation(exp_top[:], low_top[:], ACT.Exp, scale=-1.0).then_inc(s["exp_top_done"], 1)
                    if step == 1 and real(b - 1):
                        act.wait_ge(s["y_ready"], b)
                        need(act, s["yt_ready"], b - 1)
                        nc.scalar.activation(yT[:], misc[:, 0:256], ACT.Copy, scale=mod_col[0][:, cols(GA * B + b - 1, 1)]).then_inc(s["y_taken"], 1)
                    if real(before):
                        act.wait_ge(s["attn_ready"], g)
                        need(act, s["y_ready"], before)
                        n = (step - 1) % 4
                        nc.scalar.copy(attn[:, n * 512:n * 512 + 512], attn_bank[:]).then_inc(s["attn_taken"], 1)

            turns(act, body)

        @block.vector
        def _(dve):
            steps = [0]

            def then(instruction):
                steps[0] += 1
                instruction.then_inc(s["setup_steps"], 1)
                dve.wait_ge(s["setup_steps"], steps[0])

            dve.wait_ge(s["consts_in"], 16)
            for to, at, size in ((ident_b, C_IDENT, 128), (window_b, C_WINDOW, 256), (before_b, C_BEFORE, 128), (ones_b, C_ONES, 128)):
                done = nc.vector.tensor_copy(to[:], const[:, at:at + size])
            done.then_inc(s["consts_cast"], 1)
            nc.vector.memset(send[:], 0.0)
            for n in range(2):
                nc.vector.tensor_copy(counts[n][:], const[:, C_REGION:C_REGION + E])
            dve.wait_ge(s["weights_in"], 96)
            raw = [half[:, 0:512] for pair in (probs, probsT, qk) for half in pair]
            for n, part in enumerate(raw):
                scale = DH ** -0.5 if n < 2 else 1.0
                at = slice(n * 512, n * 512 + 512)
                then(nc.vector.tensor_scalar(w_high[:, at], part, scale, None, ALU.mult))
                done = nc.vector.scalar_tensor_tensor(w_low[:, at], part, scale, w_high[:, at].bitcast(F32), ALU.mult, ALU.subtract)
            done.then_inc(s["split_done"], 1)

            def gate(out_, in_, rows, width):
                m = [mod_tmp[0:rows, k * width:(k + 1) * width] for k in range(2)]
                then(nc.vector.tensor_scalar(m[0], in_, -1.0, None, ALU.mult))
                then(nc.vector.tensor_tensor(m[1], in_, m[0], ALU.max))
                then(nc.vector.tensor_scalar(m[0], in_, 0.0, 2.0, ALU.is_ge, ALU.mult))
                then(nc.vector.tensor_scalar(m[0], m[0], -1.0, None, ALU.add))
                then(nc.vector.scalar_tensor_tensor(out_, m[1], GATE_MIN, m[0], ALU.max, ALU.mult))

            for n in range(2):
                dve.wait_ge(s["mod_made"], n + 1)
                columns, raw_rows = mod_col[n], mod_stage[n]
                then(nc.vector.tensor_copy(columns[:], banks[4 + n][:, 0:6 * B]))
                for kind in (CA, CB):
                    then(nc.vector.tensor_scalar(columns[:, kind * B:(kind + 1) * B], columns[:, kind * B:(kind + 1) * B], 1.0, None, ALU.add))
                for kind in (GA, GB):
                    gate(columns[:, kind * B:(kind + 1) * B], columns[:, kind * B:(kind + 1) * B], 128, B)
                for half in range(2):
                    then(nc.vector.tensor_copy(raw_rows[:, half * 384:half * 384 + 384], banks[2 * n + half][0:B, 0:384]))
                for kind in (CA, CB):
                    then(nc.vector.tensor_scalar(raw_rows[:, kind * D:(kind + 1) * D], raw_rows[:, kind * D:(kind + 1) * D], 1.0, None, ALU.add))
                for kind in (GA, GB):
                    gate(raw_rows[:, kind * D:(kind + 1) * D], raw_rows[:, kind * D:(kind + 1) * D], B, D)
                dve.sem_inc(s["mod_rows_made"], 1)
                dve.sem_inc(s["mod_taken"], 1)
            dve.wait_ge(s["x_in"], 64)

            def maxima(g, step, parity):
                dve.wait_ge(s["scores_ready"], 2 * g + parity + 1)
                need(dve, s["exp_done"], 2 * (g - 2) + parity + 1)
                slot = step % 2 * 8 + parity * 4
                nc.vector.tensor_reduce(neg_max[:, slot:slot + 4], scores_bank[parity][:].rearrange("p (n k) -> p n k", k=128), AX.X, ALU.max,
                                        negate=True).then_inc(s["negmax_ready"], 1)

            def inverses(g, step, parity):
                dve.wait_ge(s["exp_done"], 2 * g + parity + 1)
                need(dve, s["norm_done"], 2 * (g - 2) + parity + 1)
                slot = step % 2 * 8 + parity * 4
                nc.vector.reciprocal(inverse[:, slot:slot + 4], sums[:, slot:slot + 4]).then_inc(s["inverse_ready"], 1)

            def statistics(n, kind, owner, source):
                wait_apart(dve, s["rstd_" + kind], owner, s["passed_dve"])
                for i in range(2):
                    done = nc.vector.bn_stats(stats[:, 12 * n + 6 * i:12 * n + 6 * i + 6], source[i])
                done.then_inc(s["parts_" + kind], 1)
                wait_apart(dve, s["parts_" + kind], owner + 1, s["passed_dve"])
                for i in range(2):
                    done = nc.vector.bn_aggr(moments[:, 4 * n + 2 * i:4 * n + 2 * i + 2], stats[:, 12 * n + 6 * i:12 * n + 6 * i + 6])
                done.then_inc(s["stats_" + kind], 1)

            def normed(n, kind, owner, to, source):
                dve.wait_ge(s["rstd_" + kind], owner + 1)
                for i in range(2):
                    done = nc.vector.tensor_scalar(to[:, i * 128:i * 128 + 128], source[i], moments[:, 4 * n + 2 * i:4 * n + 2 * i + 1],
                                                   rstd[:, 2 * n + i:2 * n + i + 1], ALU.subtract, ALU.mult)
                done.then_inc(s[f"z_{kind}_done"], 1)

            def tiles_of_x(owner):
                return [x[:, cols(owner * 256 + i * 128, 128)] for i in range(2)]

            def choose(b):
                dve.wait_ge(s["lg_ready"], b + 1)
                nc.vector.tensor_copy(logits[:], misc[:, 0:16]).then_inc(s["lg_taken"], 1)
                wait_apart(dve, s["lg_taken"], b + 1, s["passed_dve"])
                for i in range(2):
                    done = nc.vector.max(top[:, i * 8:i * 8 + 8], logits[:, i * 8:i * 8 + 8])
                done.then_inc(s["top_done"], 1)
                wait_apart(dve, s["top_done"], b + 1, s["passed_dve"])
                for i in range(2):
                    done = nc.vector.max_index(top_at[:, i * 8:i * 8 + 8], top[:, i * 8:i * 8 + 8], logits[:, i * 8:i * 8 + 8])
                done.then_inc(s["top_at_done"], 1)
                need(dve, s["exp_top_done"], b)
                nc.vector.tensor_scalar(low_top[:], top[:].rearrange("p (i e) -> p i e", e=8)[:, :, 0], -87.0, None, ALU.max).then_inc(s["low_top_done"], 1)
                dve.wait_ge(s["top_at_done"], b + 1)
                nc.vector.tensor_copy(expert[:], top_at[:].rearrange("p (i e) -> p i e", e=8)[:, :, 0]).then_inc(s["expert_done"], 1)
                dve.wait_ge(s["expert_done"], b + 1)
                for i in range(2):
                    done = nc.vector.tensor_scalar(hot[:, i * 8:i * 8 + 8], const[:, C_INDEX:C_INDEX + E], expert[:, i:i + 1], None, ALU.is_equal)
                done.then_inc(s["hot_done"], 1)
                dve.wait_ge(s["hot_done"], b + 1)
                need(dve, s["rk_ready"], b)
                nc.vector.tensor_copy(hot_b[:], hot[:]).then_inc(s["hot_ready"], 1)

            def take_ranks(b):
                dve.wait_ge(s["rk_ready"], b + 1)
                nc.vector.tensor_tensor(place[:].rearrange("p (i e) -> p i e", e=8), misc[:, 0:16].rearrange("p (i e) -> p i e", e=8),
                                        counts[0][:].unsqueeze(1).broadcast_to([128, 2, 8]), ALU.add).then_inc(s["place_made"], 1)
                dve.wait_ge(s["place_made"], b + 1)
                nc.vector.tensor_tensor(counts[0][:], misc[:, 16:24], counts[0][:], ALU.add).then_inc(s["rk_taken"], 1)

            def choose_rows(b):
                nc.vector.tensor_tensor(picked[:], place[:], hot[:], ALU.mult).then_inc(s["picked_done"], 1)
                dve.wait_ge(s["picked_done"], b + 1)
                nc.vector.tensor_reduce(place_f[:], picked[:].rearrange("p (i e) -> p i e", e=8), AX.X, ALU.add).then_inc(s["place_summed"], 1)
                dve.wait_ge(s["place_summed"], b + 1)
                need(dve, sent_done, 32 * b)
                nc.vector.tensor_copy(rows_at[0][:, cols(2 * b, 2)], place_f[:])
                nc.vector.tensor_copy(rows_now[:], place_f[:]).then_inc(s["place_done"], 1)

            def score(b):
                dve.wait_ge(s["exp_top_done"], b + 1)
                nc.vector.tensor_scalar(low_top[:], exp_top[:], 1.0, None, ALU.add).then_inc(s["score_steps"], 1)
                dve.wait_ge(s["score_steps"], b + 1)
                nc.vector.reciprocal(send[:].rearrange("p (i w) -> p i w", w=SENT)[:, :, D], low_top[:]).then_inc(s["score_done"], 1)

            def body(b, _, __):
                for step in range(4):
                    g = 4 * b + step
                    before = b if step else b - 1
                    after = b + 1 if step == 3 else b

                    def take_transposed(parity):
                        if real(before):
                            dve.wait_ge(s["pt_ready"], 2 * (g - 1) + parity + 1)
                            need(dve, s["attn_ready"], g - 2)
                            nc.vector.tensor_copy(probsT[(step - 1) % 2][:, parity * 512:parity * 512 + 512], pt_bank[parity][:]).then_inc(s["pt_taken"], 1)

                    if step == 1 and real(b - 2):
                        choose(b - 2)
                    if step == 2 and real(b - 1):
                        dve.wait_ge(s["yt_ready"], b)
                        now = x[:, cols((b - 1) * 256, 256)]
                        nc.vector.tensor_tensor(now, misc[:, 0:256], now, ALU.add).then_inc(s["yt_taken"], 1)
                    if step == 3 and real(b + 1):
                        dve.wait_ge(s["zt_taken"], b + 2)
                        need(dve, s["v_ready"], 4 * b + 4)
                        nc.vector.tensor_copy(h_high[:], hT[:]).then_inc(s["high_done"], 1)
                        dve.wait_ge(s["high_done"], b + 2)
                        nc.vector.tensor_tensor(h_low[:], hT[:], h_high[:].bitcast(F32), ALU.subtract).then_inc(s["split_ready"], 1)
                    if real(b):
                        maxima(g, step, 0)
                        maxima(g, step, 1)
                    if step == 2 and real(b - 1):
                        dve.wait_ge(s["yt_taken"], b)
                        statistics(1, "b", b - 1, tiles_of_x(b - 1))
                    if step == 3 and real(b - 1):
                        dve.wait_ge(s["h_b_done"], b)
                        statistics(2, "c", b - 1, [h_b[:, i * 128:i * 128 + 128] for i in range(2)])
                    take_transposed(0)
                    if real(b):
                        inverses(g, step, 0)
                    take_transposed(1)
                    if step == 0 and real(b - 2):
                        dve.wait_ge(s["nt_ready"], b - 1)
                        need(dve, s["lg_ready"], b - 2)
                        nc.vector.tensor_copy(nT[:], misc[:, 0:256]).then_inc(s["nt_taken"], 1)
                    if step == 1 and real(b - 2):
                        take_ranks(b - 2)
                    if real(b):
                        inverses(g, step, 1)
                    if real(after):
                        dve.wait_ge(s["qk1_ready"], g + 2)
                        need(dve, s["scores_ready"], 2 * g)
                        nc.vector.tensor_copy(qk[(step + 1) % 2][:, 512:1024], proj_bank[(3 * ((step + 1) % 4) + 1) % 2][:]).then_inc(s["qk1_taken"], 1)
                    if step == 0 and real(b + 1):
                        statistics(0, "a", b + 1, tiles_of_x(b + 1))
                    if step == 1 and real(b + 1):
                        need(dve, s["zt_ready"], b + 1)
                        normed(0, "a", b + 1, z_a, tiles_of_x(b + 1))
                    if step == 1 and real(b - 2):
                        choose_rows(b - 2)
                    if step == 2 and real(b - 1):
                        need(dve, s["h_b_done"], b - 1)
                        normed(1, "b", b - 1, z_b, tiles_of_x(b - 1))
                    if step == 2 and real(b - 2):
                        score(b - 2)
                    if step == 3 and real(b - 1):
                        need(dve, s["send_done"], b - 1)
                        normed(2, "c", b - 1, z_c, [h_b[:, i * 128:i * 128 + 128] for i in range(2)])
                    if real(after):
                        dve.wait_ge(s["v_ready"], g + 2)
                        need(dve, s["attn_ready"], g - 2)
                        nc.vector.tensor_copy(v[(step + 1) % 4][:, 0:512], proj_bank[(3 * ((step + 1) % 4) + 2) % 2][:]).then_inc(s["v_taken"], 1)

            turns(dve, body)

        @block.gpsimd
        def _(pool):
            def normalise(g, step, parity):
                pool.wait_ge(s["inverse_ready"], 2 * g + parity + 1)
                slot = step % 2 * 8 + parity * 4
                p = probs[step % 2][:, parity * 512:parity * 512 + 512].rearrange("p (n k) -> p n k", k=128)
                nc.gpsimd.tensor_tensor(p, p, inverse[:, slot:slot + 4].unsqueeze(2).broadcast_to([128, 4, 128]), ALU.mult).then_inc(s["norm_done"], 1)

            def over_tiles(row):
                return row.unsqueeze(1).broadcast_to([128, 2, D])

            def tiles(buffer):
                return buffer.rearrange("p (i d) -> p i d", d=D)

            shift, scale, gate = (over_tiles(mod_b[:, n * D:(n + 1) * D]) for n in range(3))

            def body(b, _, __):
                for step in range(4):
                    g = 4 * b + step
                    if real(b):
                        normalise(g, step, 0)
                        normalise(g, step, 1)
                    if step == 2 and real(b - 1):
                        pool.wait_ge(s["z_b_done"], b)
                        pool.wait_ge(s["mod_b_in"], 16 * b)
                        need(pool, s["z_c_done"], b - 1)
                        nc.gpsimd.tensor_tensor(tiles(h_b[:]), tiles(z_b[:]), scale, ALU.mult).then_inc(s["scaled_b"], 1)
                        pool.wait_ge(s["scaled_b"], b)
                        nc.gpsimd.tensor_tensor(tiles(h_b[:]), tiles(h_b[:]), shift, ALU.add).then_inc(s["h_b_done"], 1)
                    if step == 2 and real(b - 2):
                        pool.wait_ge(s["place_done"], b - 1)
                        wait_apart(pool, s["score_done"], b - 1, s["passed_pool"])
                        for i in range(2):
                            nc.gpsimd.indirect_dma_start(sent[0], bass.IndirectOffsetOnAxis(ap=rows_now[:, i:i + 1], axis=0),
                                                         send[:, i * SENT:(i + 1) * SENT], None).then_inc(sent_done, 16)
                    if step == 3 and real(b - 1):
                        pool.wait_ge(s["h_b_done"], b)
                        nc.gpsimd.tensor_tensor(tiles(g_b[:]), tiles(h_b[:]), gate, ALU.mult).then_inc(s["gated_b"], 1)
                        pool.wait_ge(s["gated_b"], b)
                        now = x[:, cols((b - 1) * 256, 256)]
                        nc.gpsimd.tensor_tensor(now, now, g_b[:], ALU.add).then_inc(s["x_b_done"], 1)
                        pool.wait_ge(s["z_c_done"], b)
                        need(pool, sent_done, 32 * (b - 1))
                        need(pool, s["nt_ready"], b - 1)
                        rows = send[:].rearrange("p (i w) -> p i w", w=SENT)[:, :, 0:D]
                        nc.gpsimd.tensor_tensor(rows, tiles(z_c[:]), over_tiles(ln_row[:, 0:D]), ALU.mult).then_inc(s["scaled_c"], 1)
                        pool.wait_ge(s["scaled_c"], b)
                        nc.gpsimd.tensor_tensor(rows, rows, over_tiles(ln_row[:, D:2 * D]), ALU.add).then_inc(s["send_done"], 1)

            pool.wait_ge(s["small_in"], 128)
            turns(pool, body)
            pool.wait_ge(sent_done, 32 * B)

        ctx_block.close()
        clear(nc, used)


def experts(nc, t, layer, counts, rows_at, back_at, sent, back, banks, const, ident):
    ctx = ExitStack()
    with ctx:
        def sb(name, columns, kind=F32, rows=128):
            return ctx.enter_context(nc.sbuf_tensor(f"{name}_{layer}", [rows, columns], kind))

        used = []

        def sem(name):
            used.append(ctx.enter_context(nc.semaphore(f"e{layer}_{name}")))
            return used[-1]

        shared = layer == 0
        width = 2 * F if shared else F
        branches = 2 if shared else 1
        chunks = 2 * branches
        kinds = E + 1 if shared else E
        row = SENT if shared else D
        up_high, up_low = sb("up_high", kinds * width, F32R), sb("up_low", kinds * width, F32R)
        down = sb("down", kinds * F)
        raw = [sb(f"raw{n}", width) for n in range(2)]
        bias1 = bias2 = None
        if not shared:
            bias1, bias2 = sb("bias1", E * F), sb("bias2", E * D)
        tiles_of, ends, past, delta = sb("tiles_of", E), sb("ends", E), sb("past", SLOTS), sb("delta", E)
        tiles_u, counts_u = sb("tiles_u", E, U32), sb("counts_u", E, U32)
        slot_f, slot_row_f = sb("slot_f", SLOTS), sb("slot_row_f", SLOTS)
        slot_expert, slot_row = sb("slot_expert", SLOTS, U32), sb("slot_row", SLOTS, U32)
        back_f, moved = sb("back_f", TILES), sb("moved", TILES)
        zeros = sb("zeros", row)
        rows_in = [sb(f"rows_in{n}", row) for n in range(2)]
        n_high, n_low = ([sb(f"{k}{n}", 128, F32R) for n in range(2)] for k in ("n_high", "n_low"))
        act_out = [sb(f"act_out{n}", branches * F) for n in range(2)]
        hidden = [sb(f"hidden{n}", branches * F) for n in range(2)]
        hiddenT = [sb(f"hiddenT{n}", chunks * 128) for n in range(2)]
        result = [sb(f"result{n}", D) for n in range(2)]

        s = {n: sem(n) for n in """weights_in down_in part_taken parts setup_steps slots_ready zeroed
            nT_ready high_done split_ready first_ready activated hidden_ready biased hiddenT_ready hiddenT_taken y_ready y_taken""".split()}
        raw_in = [sem(f"raw_in{n}") for n in range(2)]
        rows_loaded = [sem(f"rows_loaded{n}") for n in range(2)]
        rows_stored = [sem(f"rows_stored{n}") for n in range(2)]
        first_bank = [banks[0:2], banks[2:4]]
        nT_bank, hidden_bank, y_bank = banks[4], banks[5], banks[6]
        names = ([("L0_ffn_gate_w", "L0_ffn_up_w", "L0_ffn_down_w"), ("L0_ffn_sh_gate", "L0_ffn_sh_up", "L0_ffn_sh_down")] if shared
                 else [("L1_ffn_W1", None, "L1_ffn_W2")])

        def slots(engine, body):
            turns(engine, body, SLOTS, 2, 1, 2)

        def slot(n):
            return real(n, SLOTS)

        ctx_block = ExitStack()
        block = ctx_block.enter_context(nc.Block())

        @block.sync
        def _(sp):
            for e in range(kinds):
                need(sp, s["part_taken"], e - 1)
                if not shared:
                    sp.dma_start(raw[e % 2][:], t["L1_ffn_W1"][e]).then_inc(raw_in[e % 2], 16)
                else:
                    for i in range(2):
                        source = t[names[0][i]][e] if e < E else t[names[1][i]]
                        sp.dma_start(raw[e % 2][:, i * F:(i + 1) * F], source).then_inc(raw_in[e % 2], 16)
            d = down[:].rearrange("p (e c n) -> p e c n", c=2, n=D)
            for e in range(kinds):
                source = t[names[0][2]][e] if e < E else t[names[1][2]]
                sp.dma_start(d[:, e], source.rearrange("(c p) n -> p c n", p=128)).then_inc(s["down_in"], 16)
            if not shared:
                sp.dma_start(bias1[:], t["L1_ffn_b1"].rearrange("e f -> (e f)").partition_broadcast(128)).then_inc(s["down_in"], 16)
                sp.dma_start(bias2[:], t["L1_ffn_b2"].rearrange("e d -> (e d)").partition_broadcast(128)).then_inc(s["down_in"], 16)
            sp.wait_ge(s["slots_ready"], 1)
            for e in range(E):
                at = sp.value_load(counts_u[0:1, e:e + 1], min_val=0, max_val=(E + 1) * CAP - 128)
                sp.dma_start(sent[bass.ds(at, 128), 0:row], zeros[:]).then_inc(s["zeroed"], 16)
            for n in range(E):
                sp.dma_start(sent[E * CAP + n * 128:E * CAP + n * 128 + 128, 0:row], zeros[:]).then_inc(s["zeroed"], 16)
            sp.wait_ge(s["zeroed"], 32 * E)

            def body(n, parity, half):
                if slot(n + 1):
                    p = 1 - parity
                    owner = n + 1
                    at = sp.value_load(slot_row[0:1, cols(owner, 1)], min_val=0, max_val=(E + 1) * CAP - 128)
                    need(sp, s["nT_ready"], owner - 1)
                    if shared:
                        need(sp, s["hidden_ready"], owner - 1)
                    sp.dma_start(rows_in[p][:], sent[bass.ds(at, 128), 0:row]).then_inc(rows_loaded[p], 16)
                if slot(n - 2):
                    sp.wait_ge(s["y_taken"], n - 1)
                    sp.dma_start(back[cols(128 * (n - 2), 128), :], result[parity][:]).then_inc(rows_stored[parity], 16)

            slots(sp, body)
            for p in range(2):
                sp.wait_ge(rows_stored[p], 16 * (SLOTS // 2))

        @block.tensor
        def _(pe):
            pe.wait_ge(s["parts"], 1)
            pe.wait_ge(s["slots_ready"], 1)
            pe.wait_ge(s["down_in"], 16 * (kinds if shared else kinds + 2))

            def body(n, parity, half):
                if slot(n):
                    own = pe.value_load(slot_expert[0:1, cols(n, 1)], min_val=0, max_val=kinds - 1)
                    pe.wait_ge(s["split_ready"], n + 1)
                    need(pe, s["hidden_ready"], n - 1)
                    for branch in range(branches):
                        weights = [w[:, cols(own * width, width)] if branch == 0 else w[:, E * width:(E + 1) * width] for w in (up_high, up_low)]
                        to = first_bank[parity][branch][:, 0:width]
                        nc.tensor.matmul(to, n_high[parity][:], weights[0], start=True, stop=False)
                        nc.tensor.matmul(to, n_high[parity][:], weights[1], start=False, stop=False)
                        done = nc.tensor.matmul(to, n_low[parity][:], weights[0], start=False, stop=True)
                    done.then_inc(s["first_ready"], 1)
                if slot(n + 1):
                    pe.wait_ge(rows_loaded[1 - parity], 16 * (half + 1 + parity))
                    need(pe, s["split_ready"], n + 1)
                    nc.tensor.transpose(nT_bank[:, 0:128], rows_in[1 - parity][:, 0:D], ident).then_inc(s["nT_ready"], 1)
                if slot(n - 1):
                    pe.wait_ge(s["hidden_ready"], n)
                    need(pe, s["hiddenT_taken"], n - 1)
                    for c in range(chunks):
                        done = nc.tensor.transpose(hidden_bank[:, c * 128:c * 128 + 128], hidden[1 - parity][:, c * 128:c * 128 + 128], ident)
                    done.then_inc(s["hiddenT_ready"], 1)
                if slot(n - 2):
                    own = pe.value_load(slot_expert[0:1, cols(n - 2, 1)], min_val=0, max_val=kinds - 1)
                    pe.wait_ge(s["hiddenT_taken"], n - 1)
                    need(pe, s["y_taken"], n - 2)
                    for c in range(chunks):
                        w = down[:, cols(own * F + c * D, D)] if c < 2 else down[:, E * F + (c - 2) * D:E * F + (c - 1) * D]
                        done = nc.tensor.matmul(y_bank[:, 0:D], hiddenT[parity][:, c * 128:c * 128 + 128], w, start=c == 0, stop=c == chunks - 1)
                    done.then_inc(s["y_ready"], 1)

            slots(pe, body)

        @block.scalar
        def _(act):
            def body(n, parity, half):
                if slot(n):
                    act.wait_ge(s["first_ready"], n + 1)
                    need(act, s["hidden_ready"], n - 1)
                    if shared:
                        score = rows_in[parity][:, D:D + 1]
                        nc.scalar.activation(act_out[parity][:, 0:F], first_bank[parity][0][:, 0:F], ACT.Silu, scale=score)
                        nc.scalar.activation(act_out[parity][:, F:2 * F], first_bank[parity][1][:, 0:F], ACT.Silu).then_inc(s["activated"], 1)
                    else:
                        act.wait_ge(s["biased"], n + 1)
                        need(act, s["hiddenT_ready"], n - 1)
                        nc.scalar.activation(hidden[parity][:], act_out[parity][:], ACT.Gelu).then_inc(s["hidden_ready"], 1)
                if slot(n - 1):
                    act.wait_ge(s["hiddenT_ready"], n)
                    need(act, s["y_ready"], n - 2)
                    nc.scalar.copy(hiddenT[1 - parity][:], hidden_bank[:, 0:chunks * 128]).then_inc(s["hiddenT_taken"], 1)

            slots(act, body)

        @block.vector
        def _(dve):
            steps = [0]

            def then(instruction):
                steps[0] += 1
                instruction.then_inc(s["setup_steps"], 1)
                dve.wait_ge(s["setup_steps"], steps[0])

            nc.vector.memset(zeros[:], 0.0)
            then(nc.vector.tensor_tensor(tiles_of[:], counts[:], const[:, C_REGION:C_REGION + E], ALU.subtract))
            then(nc.vector.tensor_scalar(tiles_of[:], tiles_of[:], 63.5, 1 / 128, ALU.add, ALU.mult))
            then(nc.vector.tensor_copy(tiles_u[:], tiles_of[:]))
            then(nc.vector.tensor_copy(tiles_of[:], tiles_u[:]))
            then(nc.vector.tensor_copy(counts_u[:], counts[:]))
            then(nc.vector.tensor_tensor_scan(ends[:], const[:, C_ONES:C_ONES + E], tiles_of[:], 0.0, ALU.mult, ALU.add))
            then(nc.vector.tensor_scalar(delta[:], tiles_of[:], -128.0, float(CAP), ALU.mult, ALU.add))
            then(nc.vector.memset(slot_f[:], 0.0))
            then(nc.vector.tensor_scalar(slot_row_f[:], const[:, C_SLOT:C_SLOT + SLOTS], 128.0, None, ALU.mult))
            for e in range(E):
                then(nc.vector.scalar_tensor_tensor(slot_f[:], const[:, C_SLOT:C_SLOT + SLOTS], ends[:, e:e + 1], slot_f[:], ALU.is_ge, ALU.add))
                then(nc.vector.tensor_scalar(past[:], const[:, C_SLOT:C_SLOT + SLOTS], ends[:, e:e + 1], delta[:, e:e + 1], ALU.is_ge, ALU.mult))
                then(nc.vector.tensor_tensor(slot_row_f[:], slot_row_f[:], past[:], ALU.add))
            then(nc.vector.tensor_scalar(slot_f[:], slot_f[:], float(kinds - 1), None, ALU.min))
            then(nc.vector.tensor_copy(slot_expert[:], slot_f[:]))
            then(nc.vector.tensor_copy(slot_row[:], slot_row_f[:]))
            dve.sem_inc(s["slots_ready"], 1)
            then(nc.vector.tensor_copy(back_f[:], rows_at[:]))
            for e in range(1, E):
                then(nc.vector.tensor_scalar(moved[:], rows_at[:], float(e * CAP), delta[:, e - 1:e], ALU.is_ge, ALU.mult))
                then(nc.vector.tensor_tensor(back_f[:], back_f[:], moved[:], ALU.subtract))
            then(nc.vector.tensor_copy(back_at[:], back_f[:]))
            for e in range(kinds):
                dve.wait_ge(raw_in[e % 2], 16 * branches * (e // 2 + 1))
                at = slice(e * width, (e + 1) * width)
                then(nc.vector.tensor_copy(up_high[:, at], raw[e % 2][:]))
                then(nc.vector.tensor_tensor(up_low[:, at], raw[e % 2][:], up_high[:, at].bitcast(F32), ALU.subtract))
                dve.sem_inc(s["part_taken"], 1)
            dve.sem_inc(s["parts"], 1)
            dve.wait_ge(s["down_in"], 16 * (kinds if shared else kinds + 2))

            def body(n, parity, half):
                if slot(n + 1):
                    dve.wait_ge(s["nT_ready"], n + 2)
                    need(dve, s["first_ready"], n)
                    p = 1 - parity
                    nc.vector.tensor_copy(n_high[p][:], nT_bank[:, 0:128]).then_inc(s["high_done"], 1)
                    dve.wait_ge(s["high_done"], n + 2)
                    nc.vector.tensor_tensor(n_low[p][:], nT_bank[:, 0:128], n_high[p][:].bitcast(F32), ALU.subtract).then_inc(s["split_ready"], 1)
                if slot(n):
                    dve.wait_ge(s["first_ready"], n + 1)
                    if shared:
                        dve.wait_ge(s["activated"], n + 1)
                        need(dve, s["hiddenT_ready"], n - 1)
                        nc.vector.scalar_tensor_tensor(hidden[parity][:, 0:F], first_bank[parity][0][:, F:2 * F], rows_in[parity][:, D:D + 1],
                                                       act_out[parity][:, 0:F], ALU.mult, ALU.mult)
                        nc.vector.tensor_tensor(hidden[parity][:, F:2 * F], first_bank[parity][1][:, F:2 * F], act_out[parity][:, F:2 * F],
                                                ALU.mult).then_inc(s["hidden_ready"], 1)
                    else:
                        own = dve.value_load(slot_expert[0:1, cols(n, 1)], min_val=0, max_val=E - 1)
                        need(dve, s["hidden_ready"], n - 1)
                        nc.vector.tensor_tensor(act_out[parity][:], first_bank[parity][0][:, 0:F], bias1[:, cols(own * F, F)], ALU.add).then_inc(s["biased"], 1)
                if slot(n - 2):
                    dve.wait_ge(s["y_ready"], n - 1)
                    need(dve, rows_stored[parity], 16 * (half - 1))
                    if shared:
                        nc.vector.tensor_copy(result[parity][:], y_bank[:, 0:D]).then_inc(s["y_taken"], 1)
                    else:
                        own = dve.value_load(slot_expert[0:1, cols(n - 2, 1)], min_val=0, max_val=E - 1)
                        nc.vector.tensor_tensor(result[parity][:], y_bank[:, 0:D], bias2[:, cols(own * D, D)], ALU.add).then_inc(s["y_taken"], 1)

            slots(dve, body)

        ctx_block.close()
        clear(nc, used)


def attention1(nc, t, x, const, ident, mod_col, mod_row, rows_at, back_at, counts, shifted, back, sent, got_in, sent_done, banks):
    ctx = ExitStack()
    with ctx:
        def sb(name, columns, kind=F32, rows=128):
            return ctx.enter_context(nc.sbuf_tensor("c_" + name, [rows, columns], kind))

        used = []

        def sem(name):
            used.append(ctx.enter_context(nc.semaphore("c_" + name)))
            return used[-1]

        HID = 256
        raw_hidden, raw_qk = sb("raw_hidden", 2 * HID), sb("raw_qk", D)
        hid_high, hid_low = sb("hid_high", 2 * HID, F32R), sb("hid_low", 2 * HID, F32R)
        wqk_high, wqk_low = sb("wqk_high", D, F32R), sb("wqk_low", D, F32R)
        w_out, router = sb("w_out", HID), sb("router", E)
        v_bias, router_bias, ln_row = sb("v_bias", HID), sb("router_bias", E), sb("ln_row", 2 * D)
        GATE_B, QK_B, GAMMA, BETA, OUT_B = 0, 2, 3, 5, 7
        col = sb("col", 8)
        got, at = sb("got", 256), sb("at", 2, U32)
        mod_d, mod_h, mod_f = sb("mod_d", D), sb("mod_h", 3 * D), sb("mod_f", 2 * D)
        stats, moments = sb("stats", 36), sb("moments", 12)
        var, guess, square, rstd = sb("var", 6), sb("guess", 6), sb("square", 6), sb("rstd", 6)
        half_bits, guess_bits = sb("half_bits", 6, mybir.dt.int32), sb("guess_bits", 6, mybir.dt.int32)
        z_d, z_e, z_f, h, gh, normed_rows = (sb(k, 256) for k in ("z_d", "z_e", "z_f", "h", "gh", "normed_rows"))
        nT, n_high, n_low = sb("nT", 256), sb("n_high", 256, F32R), sb("n_low", 256, F32R)
        qk, q, k_ = sb("qk", 256), sb("q", 256), sb("k", 256)
        v_sum, v, gate = sb("v_sum", 512), sb("v", 512), sb("gate", 512)
        weighed, attn = sb("weighed", 384), sb("attn", 384)
        gated, yT = sb("gated", 512), sb("yT", 256)
        send, rT = sb("send", 256), sb("rT", 256)
        logits, top, top_at, hot, hot_b, expert = sb("logits", 16), sb("top", 16), sb("top_at", 16, U32), sb("hot", 16), sb("hot_b", 16, BF16), sb("expert", 2)
        place, picked, place_f, rows_now = sb("place", 16), sb("picked", 16), sb("place_f", 2), sb("rows_now", 2, U32)
        before_b, ones_b = sb("before_b", 128, BF16), sb("ones_b", 128, BF16)

        s = {n: sem(n) for n in """weights_in split_done setup_steps at_done x2_gated x2_done mod_d_in mod_h_in mod_f_in
            seed_steps newton newton_steps z_d_done z_e_done z_f_done parts_d parts_e parts_f stats_d stats_e stats_f h_scaled h_done gh_done x_h_done
            n_scaled n_done nt_ready nT_high nT_split qk_ready qk_done q_k_done v_ready v_summed v_done gate_ready gate_done
            sim_ready weighed_done attn_done pv_ready gated_done y_ready yT_done yt_ready x3_done send_scaled send_done ht_ready rT_done
            lg_ready logits_done top_done top_at_done expert_done hot_done hot_ready rk_ready place_made rk_taken picked_done place_summed
            place_done passed_dve passed_pool""".split()}
        qk_bank, v_bank, gate_bank, sim_bank, pv_bank, y_bank, yt_bank, misc = banks
        BEHIND = 3

        def batches(engine, body):
            turns(engine, lambda n, _, __: body(n), B, 1, 4, BEHIND)

        ctx_block = ExitStack()
        block = ctx_block.enter_context(nc.Block())

        @block.sync
        def _(sp):
            loads = [(raw_hidden[:], t["L1_attn_W_hidden"]), (raw_qk[:], t["L1_attn_W_qk"]), (router[:], t["L1_ffn_Wr"]),
                     (w_out[:].rearrange("p (c n) -> p c n", n=D), t["L1_attn_W_out"].rearrange("(c p) n -> p c n", p=128)),
                     (v_bias[:], t["L1_attn_b_hidden"][0:HID].partition_broadcast(128)), (router_bias[:], t["L1_ffn_br"].partition_broadcast(128)),
                     (ln_row[:, 0:D], t["L1_attn_ln_g"].partition_broadcast(128)), (ln_row[:, D:2 * D], t["L1_attn_ln_b"].partition_broadcast(128)),
                     (col[:, QK_B:QK_B + 1], t["L1_attn_b_qk"].unsqueeze(1)), (col[:, OUT_B:OUT_B + 1], t["L1_attn_b_out"].unsqueeze(1))]
            for i in range(2):
                loads.append((col[:, GATE_B + i:GATE_B + i + 1], t["L1_attn_b_hidden"][HID + i * 128:HID + i * 128 + 128].unsqueeze(1)))
                loads.append((col[:, GAMMA + i:GAMMA + i + 1], t["L1_attn_os_gamma"][i].unsqueeze(1)))
                loads.append((col[:, BETA + i:BETA + i + 1], t["L1_attn_os_beta"][i].unsqueeze(1)))
            assert len(loads) == LOADS
            for to, source in loads:
                sp.dma_start(to, source, allow_slow_non_contiguous=True).then_inc(s["weights_in"], 16)

            def body(n):
                if real(n + 4):
                    need(sp, s["x2_done"], n + 4)
                    sp.dma_start(mod_d[:], mod_row[0][cols(n + 4, 1), GB * D:6 * D].broadcast_to([128, D])).then_inc(s["mod_d_in"], 16)
                if real(n + 3):
                    need(sp, s["x_h_done"], n + 3)
                    sp.dma_start(mod_h[:], mod_row[1][cols(n + 3, 1), 0:3 * D].broadcast_to([128, 3 * D])).then_inc(s["mod_h_in"], 16)
                if real(n - 1):
                    need(sp, s["send_done"], n - 1)
                    sp.dma_start(mod_f[:], mod_row[1][cols(n - 1, 1), SB * D:5 * D].broadcast_to([128, 2 * D])).then_inc(s["mod_f_in"], 16)

            batches(sp, body)

        @block.tensor
        def _(pe):
            pe.wait_ge(s["weights_in"], 16 * LOADS)
            pe.wait_ge(s["split_done"], 1)

            def product(to, left, right):
                nc.tensor.matmul(to, left[0], right[0], start=True, stop=False)
                nc.tensor.matmul(to, left[0], right[1], start=False, stop=False)
                return nc.tensor.matmul(to, left[1], right[0], start=False, stop=True)

            def part(pair, a, size):
                return [m[:, a:a + size] for m in pair]

            def body(n):
                normed_, hid = (n_high, n_low), (hid_high, hid_low)
                if real(n - 3):
                    pe.wait_ge(s["hot_ready"], n - 2)
                    nc.tensor.matmul(misc[:, 0:E], before_b[:], hot_b[:, 0:E], start=True, stop=True)
                    nc.tensor.matmul(misc[:, E:2 * E], ones_b[:], hot_b[:, 0:E], start=True, stop=False)
                    nc.tensor.matmul(misc[:, E:2 * E], before_b[:], hot_b[:, E:2 * E], start=False, stop=True)
                    nc.tensor.matmul(misc[:, 2 * E:3 * E], ones_b[:], hot_b[:, 0:E], start=True, stop=False)
                    nc.tensor.matmul(misc[:, 2 * E:3 * E], ones_b[:], hot_b[:, E:2 * E], start=False, stop=True).then_inc(s["rk_ready"], 1)
                if real(n):
                    pe.wait_ge(s["nT_split"], n + 1)
                    need(pe, s["qk_done"], n)
                    product(qk_bank[:, 0:256], part((wqk_high, wqk_low), 0, D), part(normed_, 0, 256)).then_inc(s["qk_ready"], 1)
                    need(pe, s["v_summed"], n)
                    for i in range(2):
                        done = product(v_bank[:, i * HID:(i + 1) * HID], part(normed_, i * 128, 128), part(hid, 0, HID))
                    done.then_inc(s["v_ready"], 1)
                if real(n - 1):
                    pe.wait_ge(s["attn_done"], n)
                    pe.wait_ge(s["v_done"], n)
                    need(pe, s["gated_done"], n - 1)
                    for c in range(2):
                        nc.tensor.matmul(pv_bank[:, c * 256:c * 256 + 256], v[:, c * 128:c * 128 + 128], attn[:, 0:256], start=True, stop=False, skip_group_check=True)
                        done = nc.tensor.matmul(pv_bank[:, c * 256 + 128:c * 256 + 256], v[:, HID + c * 128:HID + c * 128 + 128], attn[:, 256:384],
                                                start=False, stop=True, skip_group_check=True)
                    done.then_inc(s["pv_ready"], 1)
                if real(n):
                    need(pe, s["gate_done"], n)
                    for c in range(2):
                        done = product(gate_bank[:, c * 256:c * 256 + 256], part(hid, HID + c * 128, 128), part(normed_, 0, 256))
                    done.then_inc(s["gate_ready"], 1)
                    pe.wait_ge(s["q_k_done"], n + 1)
                    need(pe, s["weighed_done"], n)
                    nc.tensor.matmul(sim_bank[:, 0:256], k_[:, 0:128], q[:], start=True, stop=True)
                    nc.tensor.matmul(sim_bank[:, 256:384], k_[:, 128:256], q[:, 128:256], start=True, stop=True).then_inc(s["sim_ready"], 1)
                if real(n - 1):
                    pe.wait_ge(s["gated_done"], n)
                    need(pe, s["yT_done"], n - 1)
                    for c in range(2):
                        done = nc.tensor.matmul(y_bank[:, 0:256], w_out[:, c * D:(c + 1) * D], gated[:, c * 256:c * 256 + 256], start=c == 0, stop=c == 1)
                    done.then_inc(s["y_ready"], 1)
                if real(n + 1):
                    pe.wait_ge(s["n_done"], n + 2)
                    need(pe, s["rk_taken"], n - 2)
                    need(pe, s["nT_split"], n + 1)
                    for i in range(2):
                        done = nc.tensor.transpose(misc[:, i * 128:i * 128 + 128], normed_rows[:, i * 128:i * 128 + 128], ident)
                    done.then_inc(s["nt_ready"], 1)
                if real(n - 2):
                    pe.wait_ge(s["send_done"], n - 1)
                    pe.wait_ge(s["nT_split"], last(n + 1) + 1)
                    need(pe, s["rk_taken"], last(n - 3) + 1)
                    for i in range(2):
                        done = nc.tensor.transpose(misc[:, i * 128:i * 128 + 128], send[:, i * 128:i * 128 + 128], ident)
                    done.then_inc(s["ht_ready"], 1)
                if real(n - 1):
                    pe.wait_ge(s["yT_done"], n)
                    need(pe, s["x3_done"], n - 1)
                    for i in range(2):
                        done = nc.tensor.transpose(yt_bank[:, i * 128:i * 128 + 128], yT[:, i * 128:i * 128 + 128], ident)
                    done.then_inc(s["yt_ready"], 1)
                if real(n - 2):
                    pe.wait_ge(s["rT_done"], n - 1)
                    for i in range(2):
                        done = nc.tensor.matmul(misc[:, i * E:(i + 1) * E], rT[:, i * 128:i * 128 + 128], router[:], start=True, stop=True)
                    done.then_inc(s["lg_ready"], 1)

            batches(pe, body)

        @block.scalar
        def _(act):
            act.wait_ge(s["weights_in"], 16 * LOADS)

            def body(n):
                if real(n):
                    act.wait_ge(s["qk_ready"], n + 1)
                    need(act, s["q_k_done"], n)
                    nc.scalar.activation(qk[:], qk_bank[:, 0:256], ACT.Silu, bias=col[:, QK_B:QK_B + 1]).then_inc(s["qk_done"], 1)
                    act.wait_ge(s["v_summed"], n + 1)
                    need(act, s["pv_ready"], n)
                    nc.scalar.activation(v[:], v_sum[:], ACT.Silu).then_inc(s["v_done"], 1)
                    act.wait_ge(s["gate_ready"], n + 1)
                    need(act, s["gated_done"], n)
                    for c in range(2):
                        done = nc.scalar.activation(gate[:, c * 256:c * 256 + 256], gate_bank[:, c * 256:c * 256 + 256], ACT.Silu, bias=col[:, GATE_B + c:GATE_B + c + 1])
                    done.then_inc(s["gate_done"], 1)
                    act.wait_ge(s["weighed_done"], n + 1)
                    nc.scalar.activation(attn[:], weighed[:], ACT.Square).then_inc(s["attn_done"], 1)
                if real(n - 2):
                    act.wait_ge(s["ht_ready"], n - 1)
                    need(act, s["lg_ready"], n - 2)
                    nc.scalar.copy(rT[:], misc[:, 0:256]).then_inc(s["rT_done"], 1)

            batches(act, body)

        @block.vector
        def _(dve):
            steps = [0]

            def then(instruction):
                steps[0] += 1
                instruction.then_inc(s["setup_steps"], 1)
                dve.wait_ge(s["setup_steps"], steps[0])

            then(nc.vector.memset(moments[:], 1.0))
            nc.vector.tensor_copy(counts[:], const[:, C_REGION:C_REGION + E])
            nc.vector.tensor_copy(before_b[:], const[:, C_BEFORE:C_BEFORE + 128])
            nc.vector.tensor_copy(ones_b[:], const[:, C_ONES:C_ONES + 128])
            dve.wait_ge(s["weights_in"], 16 * LOADS)
            for raw, high, low in ((raw_hidden, hid_high, hid_low), (raw_qk, wqk_high, wqk_low)):
                then(nc.vector.tensor_copy(high[:], raw[:]))
                then(nc.vector.tensor_tensor(low[:], raw[:], high[:].bitcast(F32), ALU.subtract))
            dve.sem_inc(s["split_done"], 1)

            def rows_of(owner):
                return x[:, cols(owner * 256, 256)]

            def statistics(k, kind, owner, source):
                for i in range(2):
                    done = nc.vector.bn_stats(stats[:, 12 * k + 6 * i:12 * k + 6 * i + 6], source[i])
                done.then_inc(s["parts_" + kind], 1)
                wait_apart(dve, s["parts_" + kind], owner + 1, s["passed_dve"])
                for i in range(2):
                    done = nc.vector.bn_aggr(moments[:, 4 * k + 2 * i:4 * k + 2 * i + 2], stats[:, 12 * k + 6 * i:12 * k + 6 * i + 6])
                done.then_inc(s["stats_" + kind], 1)

            def normed(k, kind, to, source):
                for i in range(2):
                    done = nc.vector.tensor_scalar(to[:, i * 128:i * 128 + 128], source[i], moments[:, 4 * k + 2 * i:4 * k + 2 * i + 1],
                                                   rstd[:, 2 * k + i:2 * k + i + 1], ALU.subtract, ALU.mult)
                done.then_inc(s[f"z_{kind}_done"], 1)

            def tiles_of_x(owner):
                return [x[:, cols(owner * 256 + i * 128, 128)] for i in range(2)]

            def tiles_of(buffer):
                return [buffer[:, i * 128:i * 128 + 128] for i in range(2)]

            def body(n):
                turn = n + 4
                for kind, owner in (("d", n + 2), ("e", n + 1), ("f", n - 2)):
                    need(dve, s["stats_" + kind], min(owner + 1, B) if isinstance(owner, int) else owner + 1)
                need(dve, s["newton"], turn)
                nc.vector.tensor_scalar(var[:], moments[:].rearrange("p (k two) -> p k two", two=2)[:, :, 1], EPS, None, ALU.add).then_inc(s["seed_steps"], 1)
                dve.wait_ge(s["seed_steps"], 3 * turn + 1)
                nc.vector.tensor_scalar(half_bits[:], var[:].bitcast(mybir.dt.int32), 1, None, ALU.logical_shift_right).then_inc(s["seed_steps"], 1)
                dve.wait_ge(s["seed_steps"], 3 * turn + 2)
                nc.vector.tensor_scalar(guess_bits[:], half_bits[:], -1.0, float(0x5F3759DF), ALU.mult, ALU.add).then_inc(s["seed_steps"], 1)
                if real(n - 3):
                    dve.wait_ge(s["rk_ready"], n - 2)
                    nc.vector.tensor_tensor(place[:].rearrange("p (i e) -> p i e", e=8), misc[:, 0:16].rearrange("p (i e) -> p i e", e=8),
                                            counts[:].unsqueeze(1).broadcast_to([128, 2, 8]), ALU.add).then_inc(s["place_made"], 1)
                    dve.wait_ge(s["place_made"], n - 2)
                    nc.vector.tensor_tensor(counts[:], misc[:, 16:24], counts[:], ALU.add).then_inc(s["rk_taken"], 1)
                    nc.vector.tensor_tensor(picked[:], place[:], hot[:], ALU.mult).then_inc(s["picked_done"], 1)
                    dve.wait_ge(s["picked_done"], n - 2)
                    nc.vector.tensor_reduce(place_f[:], picked[:].rearrange("p (i e) -> p i e", e=8), AX.X, ALU.add).then_inc(s["place_summed"], 1)
                    dve.wait_ge(s["place_summed"], n - 2)
                    need(dve, sent_done, 32 * (n - 3))
                    nc.vector.tensor_copy(rows_at[:, cols(2 * (n - 3), 2)], place_f[:])
                    nc.vector.tensor_copy(rows_now[:], place_f[:]).then_inc(s["place_done"], 1)
                if real(n):
                    dve.wait_ge(s["qk_done"], n + 1)
                    need(dve, s["sim_ready"], n)
                    nc.vector.tensor_scalar(q[:], qk[:], col[:, GAMMA:GAMMA + 1], col[:, BETA:BETA + 1], ALU.mult, ALU.add)
                    nc.vector.tensor_scalar(k_[:], qk[:], col[:, GAMMA + 1:GAMMA + 2], col[:, BETA + 1:BETA + 2], ALU.mult, ALU.add).then_inc(s["q_k_done"], 1)
                    dve.wait_ge(s["v_ready"], n + 1)
                    need(dve, s["v_done"], n)
                    nc.vector.tensor_tensor(v_sum[:].rearrange("p (i f) -> p i f", i=2), v_bank[:].rearrange("p (i f) -> p i f", i=2),
                                            v_bias[:].unsqueeze(1).broadcast_to([128, 2, HID]), ALU.add).then_inc(s["v_summed"], 1)
                if real(n - 1):
                    dve.wait_ge(s["pv_ready"], n)
                    dve.wait_ge(s["gate_done"], n)
                    need(dve, s["y_ready"], n - 1)
                    nc.vector.tensor_tensor(gated[:], pv_bank[:], gate[:], ALU.mult).then_inc(s["gated_done"], 1)
                dve.wait_ge(s["newton"], turn + 1)
                if real(n + 2):
                    need(dve, s["h_scaled"], n + 2)
                    normed(0, "d", z_d, tiles_of_x(n + 2))
                if real(n + 1):
                    need(dve, s["n_scaled"], n + 1)
                    normed(1, "e", z_e, tiles_of(h))
                if real(n - 2):
                    need(dve, s["send_scaled"], n - 2)
                    normed(2, "f", z_f, tiles_of_x(n - 2))
                if real(n):
                    dve.wait_ge(s["sim_ready"], n + 1)
                    need(dve, s["attn_done"], n)
                    nc.vector.scalar_tensor_tensor(weighed[:], sim_bank[:, 0:384], 0.0, const[:, C_CAUSAL:C_CAUSAL + 384], ALU.max, ALU.mult).then_inc(s["weighed_done"], 1)
                if real(n - 1):
                    dve.wait_ge(s["y_ready"], n)
                    need(dve, s["yt_ready"], n - 1)
                    nc.vector.tensor_scalar(yT[:], y_bank[:, 0:256], col[:, OUT_B:OUT_B + 1], mod_col[1][:, cols(GA * B + n - 1, 1)], ALU.add, ALU.mult).then_inc(s["yT_done"], 1)
                if real(n + 1):
                    dve.wait_ge(s["nt_ready"], n + 2)
                    need(dve, s["gate_ready"], n + 1)
                    nc.vector.tensor_copy(n_high[:], misc[:, 0:256]).then_inc(s["nT_high"], 1)
                    dve.wait_ge(s["nT_high"], n + 2)
                    nc.vector.tensor_tensor(n_low[:], misc[:, 0:256], n_high[:].bitcast(F32), ALU.subtract).then_inc(s["nT_split"], 1)
                if real(n + 3):
                    dve.wait_ge(got_in, 32 * (n + 4))
                    dve.wait_ge(s["mod_d_in"], 16 * (n + 4))
                    two = got[:].rearrange("p (i d) -> p i d", d=D)
                    nc.vector.tensor_tensor(two, two, mod_d[:].unsqueeze(1).broadcast_to([128, 2, D]), ALU.mult).then_inc(s["x2_gated"], 1)
                    dve.wait_ge(s["x2_gated"], n + 4)
                    nc.vector.tensor_tensor(rows_of(n + 3), got[:], rows_of(n + 3), ALU.add).then_inc(s["x2_done"], 1)
                    wait_apart(dve, s["x2_done"], n + 4, s["passed_dve"])
                    statistics(0, "d", n + 3, tiles_of_x(n + 3))
                if real(n + 4):
                    nc.vector.tensor_copy(at[:], back_at[:, cols(2 * (n + 4), 2)]).then_inc(s["at_done"], 1)
                if real(n + 2):
                    dve.wait_ge(s["h_done"], n + 3)
                    statistics(1, "e", n + 2, tiles_of(h))
                if real(n - 1):
                    dve.wait_ge(s["yt_ready"], n)
                    dve.wait_ge(s["x_h_done"], n)
                    nc.vector.tensor_tensor(rows_of(n - 1), yt_bank[:, 0:256], rows_of(n - 1), ALU.add).then_inc(s["x3_done"], 1)
                    wait_apart(dve, s["x3_done"], n, s["passed_dve"])
                    statistics(2, "f", n - 1, tiles_of_x(n - 1))

                if real(n - 2):
                    dve.wait_ge(s["lg_ready"], n - 1)
                    nc.vector.tensor_tensor(logits[:].rearrange("p (i e) -> p i e", e=8), misc[:, 0:16].rearrange("p (i e) -> p i e", e=8),
                                            router_bias[:].unsqueeze(1).broadcast_to([128, 2, 8]), ALU.add).then_inc(s["logits_done"], 1)
                    wait_apart(dve, s["logits_done"], n - 1, s["passed_dve"])
                    for i in range(2):
                        done = nc.vector.max(top[:, i * 8:i * 8 + 8], logits[:, i * 8:i * 8 + 8])
                    done.then_inc(s["top_done"], 1)
                    wait_apart(dve, s["top_done"], n - 1, s["passed_dve"])
                    for i in range(2):
                        nc.vector.tensor_scalar(shifted[:, cols((n - 2) * 16 + i * 8, 8)], logits[:, i * 8:i * 8 + 8], top[:, i * 8:i * 8 + 1], None, ALU.subtract)
                        done = nc.vector.max_index(top_at[:, i * 8:i * 8 + 8], top[:, i * 8:i * 8 + 8], logits[:, i * 8:i * 8 + 8])
                    done.then_inc(s["top_at_done"], 1)
                    dve.wait_ge(s["top_at_done"], n - 1)
                    nc.vector.tensor_copy(expert[:], top_at[:].rearrange("p (i e) -> p i e", e=8)[:, :, 0]).then_inc(s["expert_done"], 1)
                    dve.wait_ge(s["expert_done"], n - 1)
                    for i in range(2):
                        done = nc.vector.tensor_scalar(hot[:, i * 8:i * 8 + 8], const[:, C_INDEX:C_INDEX + E], expert[:, i:i + 1], None, ALU.is_equal)
                    done.then_inc(s["hot_done"], 1)
                    dve.wait_ge(s["hot_done"], n - 1)
                    need(dve, s["rk_ready"], n - 2)
                    nc.vector.tensor_copy(hot_b[:], hot[:]).then_inc(s["hot_ready"], 1)

            batches(dve, body)

        @block.gpsimd
        def _(pool):
            def over_tiles(row):
                return row.unsqueeze(1).broadcast_to([128, 2, D])

            def tiles(buffer):
                return buffer.rearrange("p (i d) -> p i d", d=D)

            def affine(source, scale, shift, to, scaled, done, count):
                nc.gpsimd.tensor_tensor(tiles(to), tiles(source), over_tiles(scale), ALU.mult).then_inc(s[scaled], 1)
                pool.wait_ge(s[scaled], count)
                nc.gpsimd.tensor_tensor(tiles(to), tiles(to), over_tiles(shift), ALU.add).then_inc(s[done], 1)

            def body(n):
                turn = n + 4
                pool.wait_ge(s["seed_steps"], 3 * turn + 3)
                for k in range(NEWTON):
                    now = guess_bits[:].bitcast(F32) if k == 0 else guess[:]
                    if k == 0:
                        need(pool, s["z_f_done"], min(n - 2, B) if isinstance(n, int) else n - 2)
                        need(pool, s["z_e_done"], min(n + 1, B) if isinstance(n, int) else n + 1)
                        need(pool, s["z_d_done"], min(n + 2, B) if isinstance(n, int) else n + 2)
                    at_ = 4 * NEWTON * turn + 4 * k
                    nc.gpsimd.tensor_tensor(square[:], now, now, ALU.mult).then_inc(s["newton_steps"], 1)
                    pool.wait_ge(s["newton_steps"], at_ + 1)
                    nc.gpsimd.tensor_tensor(square[:], square[:], var[:], ALU.mult).then_inc(s["newton_steps"], 1)
                    wait_apart(pool, s["newton_steps"], at_ + 2, s["passed_pool"])
                    nc.gpsimd.tensor_scalar(square[:], square[:], -0.5, 1.5, ALU.mult, ALU.add).then_inc(s["newton_steps"], 1)
                    pool.wait_ge(s["newton_steps"], at_ + 3)
                    nc.gpsimd.tensor_tensor(rstd[:] if k == NEWTON - 1 else guess[:], now, square[:], ALU.mult).then_inc(s["newton_steps"], 1)
                    pool.wait_ge(s["newton_steps"], at_ + 4)
                pool.sem_inc(s["newton"], 1)
                if real(n - 3):
                    wait_apart(pool, s["place_done"], n - 2, s["passed_pool"])
                    for i in range(2):
                        nc.gpsimd.indirect_dma_start(sent, bass.IndirectOffsetOnAxis(ap=rows_now[:, i:i + 1], axis=0), send[:, i * D:(i + 1) * D], None).then_inc(sent_done, 16)
                if real(n + 2):
                    pool.wait_ge(s["z_d_done"], n + 3)
                    pool.wait_ge(s["mod_h_in"], 16 * (n + 3))
                    need(pool, s["z_e_done"], n + 2)
                    affine(z_d[:], mod_h[:, CA * D:(CA + 1) * D], mod_h[:, SA * D:(SA + 1) * D], h[:], "h_scaled", "h_done", n + 3)
                if real(n + 1):
                    pool.wait_ge(s["z_e_done"], n + 2)
                    need(pool, s["nt_ready"], n + 1)
                    affine(z_e[:], ln_row[:, 0:D], ln_row[:, D:2 * D], normed_rows[:], "n_scaled", "n_done", n + 2)
                if real(n + 2):
                    pool.wait_ge(s["h_done"], n + 3)
                    nc.gpsimd.tensor_tensor(tiles(gh[:]), tiles(h[:]), over_tiles(mod_h[:, GA * D:(GA + 1) * D]), ALU.mult).then_inc(s["gh_done"], 1)
                    pool.wait_ge(s["gh_done"], n + 3)
                    now = x[:, cols((n + 2) * 256, 256)]
                    nc.gpsimd.tensor_tensor(now, now, gh[:], ALU.add).then_inc(s["x_h_done"], 1)
                if real(n - 2):
                    pool.wait_ge(s["z_f_done"], n - 1)
                    pool.wait_ge(s["mod_f_in"], 16 * (n - 1))
                    need(pool, sent_done, 32 * (n - 2))
                    need(pool, s["ht_ready"], n - 2)
                    affine(z_f[:], mod_f[:, D:2 * D], mod_f[:, 0:D], send[:], "send_scaled", "send_done", n - 1)
                if real(n + 4):
                    pool.wait_ge(s["at_done"], n + 5)
                    wait_apart(pool, s["x2_done"], n + 4, s["passed_pool"])
                    for i in range(2):
                        nc.gpsimd.indirect_dma_start(got[:, i * D:(i + 1) * D], None, back, bass.IndirectOffsetOnAxis(ap=at[:, i:i + 1], axis=0)).then_inc(got_in, 16)

            batches(pool, body)
            pool.wait_ge(sent_done, 32 * B)

        ctx_block.close()
        clear(nc, used)


def combine(nc, out, x, mod_row, rows_at, back, shifted, got_in):
    ctx = ExitStack()
    with ctx:
        def sb(name, columns, kind=F32, rows=128):
            return ctx.enter_context(nc.sbuf_tensor("f_" + name, [rows, columns], kind))

        def sem(name):
            return ctx.enter_context(nc.semaphore("f_" + name))

        weight, exped, total = sb("weight", TILES), sb("exped", TILES * E), sb("total", TILES)
        got = [sb(f"got{n}", 2 * D) for n in range(2)]
        gate = [sb(f"gate{n}", D) for n in range(2)]
        result = [sb(f"result{n}", 2 * D) for n in range(2)]
        at = [sb(f"at{n}", 2, U32) for n in range(2)]
        s = {n: sem(n) for n in "passed at_done weighted result_done exp_done summed weight_done".split()}
        gate_in = [sem(f"gate_in{n}") for n in range(2)]
        stored = [sem(f"stored{n}") for n in range(2)]
        out_rows = out.rearrange("b (i p) d -> b p i d", p=128)
        block = ctx.enter_context(nc.Block())

        def batches(engine, body):
            turns(engine, body, B, 2, 2, 2)

        @block.sync
        def _(sp):
            def body(n, parity, half):
                if real(n + 1):
                    owner = half + parity
                    need(sp, s["result_done"], n)
                    sp.dma_start(gate[1 - parity][:], mod_row[cols(n + 1, 1), GB * D:6 * D].broadcast_to([128, D])).then_inc(gate_in[1 - parity], 16)

            batches(sp, body)

        @block.gpsimd
        def _(pool):
            def body(n, parity, half):
                if real(n + 1):
                    pool.wait_ge(s["at_done"], n + 2)
                    wait_apart(pool, s["result_done"], n, s["passed"])
                    for i in range(2):
                        nc.gpsimd.indirect_dma_start(got[1 - parity][:, i * D:(i + 1) * D], None, back,
                                                     bass.IndirectOffsetOnAxis(ap=at[1 - parity][:, i:i + 1], axis=0)).then_inc(got_in[1 - parity], 16)

            batches(pool, body)

        @block.vector
        def _(dve):
            def body(n, parity, half):
                if real(n):
                    dve.wait_ge(got_in[parity], 32 * (half + 1))
                    dve.wait_ge(gate_in[parity], 16 * (half + 1))
                    for i in range(2):
                        mine = got[parity][:, i * D:(i + 1) * D]
                        done = nc.vector.scalar_tensor_tensor(mine, mine, weight[:, cols(2 * n + i, 1)], gate[parity][:], ALU.mult, ALU.mult)
                    done.then_inc(s["weighted"], 1)
                    dve.wait_ge(s["weighted"], n + 1)
                    need(dve, stored[parity], 16 * half)
                    nc.vector.tensor_tensor(result[parity][:], got[parity][:], x[:, cols(n * 256, 256)], ALU.add).then_inc(s["result_done"], 1)
                if real(n + 2):
                    nc.vector.tensor_copy(at[parity][:], rows_at[:, cols(2 * (n + 2), 2)]).then_inc(s["at_done"], 1)

            dve.wait_ge(s["exp_done"], 1)
            nc.vector.tensor_reduce(total[:], exped[:].rearrange("p (t e) -> p t e", e=E), AX.X, ALU.add).then_inc(s["summed"], 1)
            dve.wait_ge(s["summed"], 1)
            nc.vector.reciprocal(weight[:], total[:]).then_inc(s["weight_done"], 1)
            dve.wait_ge(s["weight_done"], 1)
            batches(dve, body)

        @block.scalar
        def _(act):
            nc.scalar.activation(exped[:], shifted[:], ACT.Exp).then_inc(s["exp_done"], 1)

            def body(n, parity, half):
                if real(n):
                    act.wait_ge(s["result_done"], n + 1)
                    act.dma_start(out_rows[cols(n, 1)].squeeze(0), result[parity][:].rearrange("p (i d) -> p i d", d=D)).then_inc(stored[parity], 16)

            batches(act, body)
            for parity in range(2):
                act.wait_ge(stored[parity], 16 * (B // 2))


INPUTS = ["L0_attn_x", "L0_attn_Wqkv", "L0_attn_Wout", "L0_ffn_ln_w", "L0_ffn_ln_b", "L0_ffn_router_w", "L0_ffn_gate_w", "L0_ffn_up_w",
          "L0_ffn_down_w", "L0_ffn_sh_gate", "L0_ffn_sh_up", "L0_ffn_sh_down", "L0_wmod", "L1_attn_ln_g", "L1_attn_ln_b", "L1_attn_W_hidden",
          "L1_attn_b_hidden", "L1_attn_W_qk", "L1_attn_b_qk", "L1_attn_os_gamma", "L1_attn_os_beta", "L1_attn_W_out", "L1_attn_b_out",
          "L1_ffn_Wr", "L1_ffn_br", "L1_ffn_W1", "L1_ffn_b1", "L1_ffn_W2", "L1_ffn_b2", "L1_wmod"]


def kernel(**inputs):
    import numpy as np
    import concourse.bacc as bacc
    from concourse import mybir as m
    from concourse.bass_utils import run_bass_kernel_spmd as run

    nc = bacc.Bacc("TRN2", target_bir_lowering=False, num_devices=1)
    arrays = {name: np.ascontiguousarray(inputs[name]) for name in INPUTS}
    arrays["c0T"] = np.ascontiguousarray(np.asarray(inputs["L0_c"]).T)
    arrays["c1T"] = np.ascontiguousarray(np.asarray(inputs["L1_c"]).T)
    arrays["consts"] = constants()
    t = {name: nc.dram_tensor("in_" + name, a.shape, m.dt.from_np(a.dtype), kind="ExternalInput").ap() for name, a in arrays.items()}
    out = nc.dram_tensor("out", [B, S, D], F32, kind="ExternalOutput").ap()
    program(nc, t, out)
    r = run(nc, [{"in_" + name: a for name, a in arrays.items()}], core_ids=[0])
    return r.results[0]["out"]
```

```python
from contextlib import ExitStack

import concourse.bass as bass
import concourse.mybir as mybir
from concourse.alu_op_type import AluOpType as ALU

F32 = mybir.dt.float32
F32R = mybir.dt.float32r
BF16 = mybir.dt.bfloat16
U32 = mybir.dt.uint32
ACT = mybir.ActivationFunctionType
AX = mybir.AxisListType

B, S, D = 32, 256, 128
TILES = B * S // 128
HEADS, DH = 16, 64
UNITS = 4
E, F = 8, 256
EPS = 1e-5
GATE_MIN = 0.25
MASKED = -1e30
CAP = B * S + 128
SLOTS = TILES + E
SENT = 132
NEWTON = 3
LOADS = 16
SA, CA, GA, SB, CB, GB = range(6)

C_IDENT, C_WINDOW, C_BEFORE, C_ONES, C_REGION, C_INDEX, C_CAUSAL, C_SLOT, C_ROW, C_EPS, C_FIRST = 0, 128, 384, 512, 640, 648, 656, 1040, 1112, 1113, 1120
C_ALL = 1248


def constants():
    import numpy as np
    c = np.zeros((128, C_ALL), np.float32)
    p, j = np.arange(128)[:, None], np.arange(128)[None, :]
    c[:, C_IDENT:C_IDENT + 128] = p == j
    first = (j <= p) & (j >= p - 63)
    r = p % 64
    second = (j >= r + 1) & (j <= r + 64)
    c[:, C_WINDOW:C_WINDOW + 128] = np.where(first, 0, MASKED)
    c[:, C_WINDOW + 128:C_WINDOW + 256] = np.where(second, 0, MASKED)
    c[:, C_BEFORE:C_BEFORE + 128] = p < j
    c[:, C_ONES:C_ONES + 128] = 1
    c[:, C_REGION:C_REGION + E] = np.arange(E) * CAP
    c[:, C_INDEX:C_INDEX + E] = np.arange(E)
    i = np.arange(256)[None, :]
    c[:, C_CAUSAL:C_CAUSAL + 256] = (i >= p) / (i + 1.0)
    c[:, C_CAUSAL + 256:C_CAUSAL + 384] = (j >= p) / (j + 129.0)
    c[:, C_SLOT:C_SLOT + SLOTS] = np.arange(SLOTS)
    c[:, C_ROW] = np.arange(128)
    c[:, C_EPS] = EPS
    c[0, C_FIRST:C_FIRST + 128] = 1
    return c


def need(engine, semaphore, value):
    if not (isinstance(value, int) and value <= 0):
        engine.wait_ge(semaphore, value)


def wait_apart(engine, semaphore, value, passed):
    if not (isinstance(value, int) and value <= 0):
        engine.wait_ge(semaphore, value)
        engine.sem_inc(passed, 1)


def last(owner):
    return min(owner, B - 1) if isinstance(owner, int) else owner


def real(owner, count=B):
    return not isinstance(owner, int) or 0 <= owner < count


def turns(engine, body, count=B, unroll=1, ahead=1, behind=2):
    start = -(-(behind + 1) // unroll) * unroll
    end = (count - ahead) // unroll * unroll
    for n in range(-ahead, start):
        body(n, n % unroll, n // unroll)
    with engine.Fori(start // unroll, end // unroll) as i:
        for k in range(unroll):
            body(unroll * i + k, k, i)
    for n in range(end, count + behind):
        body(n, n % unroll, n // unroll)


def clear(nc, semaphores):
    with nc.Block() as block:
        @block.gpsimd
        def _(pool):
            for semaphore in semaphores[0::4]:
                pool.sem_clear(semaphore)

        @block.sync
        def _(sp):
            for semaphore in semaphores[1::4]:
                sp.sem_clear(semaphore)

        @block.scalar
        def _(act):
            for semaphore in semaphores[2::4]:
                act.sem_clear(semaphore)

        @block.vector
        def _(dve):
            for semaphore in semaphores[3::4]:
                dve.sem_clear(semaphore)


def cols(start, size):
    return bass.ds(start, size)


def program(nc, t, out):
    ctx = ExitStack()
    with ctx:
        def sb(name, columns, kind=F32, rows=128):
            return ctx.enter_context(nc.sbuf_tensor(name, [rows, columns], kind))

        def sem(name):
            return ctx.enter_context(nc.semaphore(name))

        sent_done = [sem(f"sent_done{n}") for n in range(2)]
        got_in = [sem(f"got_in{n}") for n in range(3)]

        x = sb("x", TILES * D)
        const = sb("const", C_ALL)
        ident = const[:, C_IDENT:C_IDENT + 128]
        mod_col = [sb(f"mod_col{n}", 6 * B) for n in range(2)]
        rows_at = [sb(f"rows_at{n}", TILES) for n in range(2)]
        back_at = [sb(f"back_at{n}", TILES, U32) for n in range(2)]
        shifted = sb("shifted", TILES * E)
        counts = [sb(f"counts{n}", E) for n in range(2)]
        mod_row = [nc.dram_tensor(f"mod_row{n}", [B, 6 * D], F32, kind="Internal").ap() for n in range(2)]
        sent = [nc.dram_tensor(f"sent{n}", [(E + 1) * CAP, (SENT, D)[n]], F32, kind="Internal").ap() for n in range(2)]
        back = [nc.dram_tensor(f"back{n}", [SLOTS * 128, D], F32, kind="Internal").ap() for n in range(2)]
        banks = [ctx.enter_context(nc.psum_tensor(f"bank{n}", [128, 512], F32)) for n in range(8)]

        UP = (E + 1) * 2 * F
        weights = sb("up_high", UP, F32R), sb("up_low", UP, F32R), sb("down", (E + 1) * F)

        setup_and_attention0(nc, t, x, const, ident, mod_col, rows_at, counts, mod_row, sent, sent_done[0], banks, weights)
        experts(nc, t, 0, counts[0], rows_at[0], back_at[0], sent[0], back[0], banks, const, ident, weights)
        attention1(nc, t, x, const, ident, mod_col, mod_row, rows_at[1], back_at[0], counts[1], shifted, back[0], sent[1], got_in[0], sent_done[1], banks, weights)
        experts(nc, t, 1, counts[1], rows_at[1], back_at[1], sent[1], back[1], banks, const, ident, weights)
        combine(nc, out, x, mod_row[1], back_at[1], back[1], shifted, got_in[1:3])


def setup_and_attention0(nc, t, x, const, ident, mod_col, rows_at, counts, mod_row, sent, sent_done, banks, weights):
    ctx = ExitStack()
    with ctx:
        def sb(name, columns, kind=F32, rows=128):
            return ctx.enter_context(nc.sbuf_tensor(name, [rows, columns], kind))

        used = []

        def sem(name):
            used.append(ctx.enter_context(nc.semaphore(name)))
            return used[-1]

        WQKV = 3 * HEADS * DH
        EXPERT_LOADS = 16 * 3 * (E + 1)
        w_high, w_low = sb("w_high", WQKV, F32R), sb("w_low", WQKV, F32R)
        w_out = sb("w_out", HEADS * DH)
        router = sb("router", E)
        c_col = [sb(f"c_col{n}", B) for n in range(2)]
        w_mod = [sb(f"w_mod{n}", 6 * D) for n in range(2)]
        mod_stage = [sb(f"mod_stage{n}", 6 * D, rows=B) for n in range(2)]
        mod_tmp = sb("mod_tmp", 4 * D)
        ident_b, window_b, before_b, ones_b = sb("ident_b", 128, BF16), sb("window_b", 256, BF16), sb("before_b", 128, BF16), sb("ones_b", 128, BF16)
        ln_row = sb("ln_row", 2 * D)
        hT = sb("hT", 256)
        h_high, h_low = sb("h_high", 256, F32R), sb("h_low", 256, F32R)
        qk = [sb(f"qk{n}", 1024) for n in range(2)]
        v = [sb(f"v{n}", 768) for n in range(4)]
        probs = [sb(f"probs{n}", 1024) for n in range(2)]
        probsT = [sb(f"probsT{n}", 1024) for n in range(2)]
        neg_max, sums, inverse = sb("neg_max", 16), sb("sums", 16), sb("inverse", 16)
        attn = sb("attn", 8 * 256)
        raw_experts = [v[n][:, 0:512] for n in range(4)] + [attn[:, n * 512:(n + 1) * 512] for n in range(4)] + [sb("raw_expert", 512)[:]]
        yT = sb("yT", 256)
        stats, moments = sb("stats", 3 * 12), sb("moments", 3 * 4)
        log_var, rstd = sb("log_var", 3 * 2), sb("rstd", 3 * 2)
        z_a, z_b, z_c, h_b, g_b = (sb(n, 256) for n in ("z_a", "z_b", "z_c", "h_b", "g_b"))
        mod_b = sb("mod_b", 3 * D)
        send = sb("send", 2 * SENT)
        nT = sb("nT", 256)
        logits, top, top_at, hot, hot_b = sb("logits", 16), sb("top", 16), sb("top_at", 16, U32), sb("hot", 16), sb("hot_b", 16, BF16)
        expert = sb("expert", 2)
        low_top, exp_top = sb("low_top", 2), sb("exp_top", 2)
        place, picked, place_f = sb("place", 16), sb("picked", 16), sb("place_f", 2)
        rows_now = sb("rows_now", 2, U32)

        names = """experts_in experts_high experts_low passed_dve passed_pool consts_in small_in weights_in x_in mod_sent  c_silu mod_made mod_taken mod_rows_made
              split_done consts_cast
            scores_ready negmax_ready exp_done inverse_ready norm_done pt_ready pt_taken
            qk0_ready qk1_ready v_ready qk0_taken qk1_taken v_taken attn_ready attn_taken
            y_ready y_taken yt_ready yt_taken zt_ready zt_taken split_ready nt_ready nt_taken
            lg_ready lg_taken log_a log_b log_c parts_a parts_b parts_c setup_steps high_done top_done top_at_done low_top_done expert_done hot_done place_made picked_done place_summed score_steps scaled_b scaled_c gated_b hot_ready rk_ready rk_taken
            stats_a stats_b stats_c rstd_a rstd_b rstd_c z_a_done z_b_done z_c_done h_b_done x_b_done send_done
            mod_b_in  exp_top_done score_done place_done
                     """.split()
        s = {n: sem("a_" + n) for n in names}
        v_shifted = [sem(f"a_v_shifted{n}") for n in range(4)]
        scores_bank, pt_bank, proj_bank = banks[0:2], banks[2:4], banks[4:6]
        attn_bank, misc = banks[6], banks[7]

        ctx_block = ExitStack()
        block = ctx_block.enter_context(nc.Block())

        @block.sync
        def _(sp):
            sp.dma_start(const[:], t["consts"]).then_inc(s["consts_in"], 16)
            for n in range(2):
                sp.dma_start(c_col[n][:], t[f"c{n}T"]).then_inc(s["small_in"], 16)
                sp.dma_start(w_mod[n][:], t[f"L{n}_wmod"]).then_inc(s["small_in"], 16)
            sp.dma_start(router[:], t["L0_ffn_router_w"]).then_inc(s["small_in"], 16)
            for n, name in enumerate(("L0_ffn_ln_w", "L0_ffn_ln_b")):
                sp.dma_start(ln_row[:, n * D:(n + 1) * D], t[name].partition_broadcast(128)).then_inc(s["small_in"], 16)
            for n in range(3):
                for half in range(2):
                    sp.dma_start((probs, probsT, qk)[n][half][:, 0:512], t["L0_attn_Wqkv"][:, n * 1024 + half * 512:n * 1024 + half * 512 + 512]).then_inc(s["weights_in"], 16)
            sp.dma_start(w_out[:].rearrange("p (c n) -> p c n", n=D), t["L0_attn_Wout"].rearrange("(c p) n -> p c n", p=128)).then_inc(s["small_in"], 16)
            x_dram = t["L0_attn_x"].rearrange("b (i p) d -> p (b i) d", p=128)
            x_view = x[:].rearrange("p (n d) -> p n d", d=D)
            for n in range(4):
                sp.dma_start(x_view[:, n * 16:(n + 1) * 16], x_dram[:, n * 16:(n + 1) * 16]).then_inc(s["x_in"], 16)
            loads = load_experts(sp, t, 0, raw_experts, weights[2], s["experts_in"])
            assert loads == EXPERT_LOADS
            for n in range(2):
                sp.wait_ge(s["mod_rows_made"], n + 1)
                sp.dma_start(mod_row[n], mod_stage[n][:]).then_inc(s["mod_sent"], 16)
            sp.wait_ge(s["mod_sent"], 32)

            def body(b, _, __):
                for step in range(4):
                    g = 4 * b + step
                    if step == 0 and real(b - 1):
                        need(sp, s["x_b_done"], b - 1)
                        sp.dma_start(mod_b[:], mod_row[0][cols(b - 1, 1), SB * D:6 * D].broadcast_to([128, 3 * D])).then_inc(s["mod_b_in"], 16)
                    if real(b + 1 if step == 3 else b):
                        n = (step + 1) % 4
                        sp.wait_ge(s["v_taken"], g + 2)
                        sp.dma_start(v[n][0:64, 512:768], v[n][64:128, 0:256]).then_inc(v_shifted[n], 16)
                        sp.dma_start(v[n][64:128, 512:768], v[n][0:64, 256:512]).then_inc(v_shifted[n], 16)

            turns(sp, body)

        @block.tensor
        def _(pe):
            pe.wait_ge(s["small_in"], 128)
            pe.wait_ge(s["c_silu"], 2)
            for n in range(2):
                for j in range(6):
                    nc.tensor.matmul(banks[4 + n][:, j * B:(j + 1) * B], w_mod[n][:, j * D:(j + 1) * D], c_col[n][:], start=True, stop=True)
                nc.tensor.matmul(banks[2 * n][0:B, 0:384], c_col[n][:], w_mod[n][:, 0:384], start=True, stop=True)
                nc.tensor.matmul(banks[2 * n + 1][0:B, 0:384], c_col[n][:], w_mod[n][:, 384:768], start=True, stop=True).then_inc(s["mod_made"], 1)
            pe.wait_ge(s["consts_cast"], 1)
            pe.wait_ge(s["mod_taken"], 2)
            pe.wait_ge(s["split_done"], 1)

            def window(g, step, parity):
                need(pe, s["exp_done"], 2 * (g - 1) + parity + 1)
                bank, rows = scores_bank[parity], slice(64 * parity, 64 * parity + 64)
                nc.tensor.matmul(bank[:].rearrange("p (j w) -> p j w", j=2), ident_b[:], window_b[:].unsqueeze(1).broadcast_to([128, 2, 256]), start=True, stop=False, skip_group_check=True)
                for j in range(2):
                    q, k = qk[step % 2][rows, j * 512:j * 512 + 256], qk[step % 2][rows, j * 512 + 256:j * 512 + 512]
                    at = bank[:, j * 256:j * 256 + 256]
                    nc.tensor.matmul(at[:, 0:128], q[:, 0:128], k[:, 0:128], start=False, stop=True, skip_group_check=True)
                    nc.tensor.matmul(at[0:64, 128:256], q[:, 128:192], k[:, 64:192], start=False, stop=True, skip_group_check=True)
                    done = nc.tensor.matmul(at[64:128, 128:256], q[:, 192:256], k[:, 128:256], start=False, stop=True, skip_group_check=True)
                done.then_inc(s["scores_ready"], 1)

            def transpose_probs(g, step, parity):
                need(pe, s["norm_done"], 2 * g + parity + 1)
                need(pe, s["pt_taken"], 2 * (g - 1) + parity + 1)
                for n in range(4):
                    at = parity * 512 + n * 128
                    done = nc.tensor.transpose(pt_bank[parity][:, n * 128:n * 128 + 128], probs[step % 2][:, at:at + 128], ident)
                done.then_inc(s["pt_ready"], 1)

            def project(bank, parts):
                for n, (left_high, left_low, right_high, right_low, at) in enumerate(parts):
                    nc.tensor.matmul(at, left_high, right_high, start=True, stop=False)
                    nc.tensor.matmul(at, left_high, right_low, start=False, stop=False)
                    done = nc.tensor.matmul(at, left_low, right_high, start=False, stop=True)
                return done

            def project_qk(g, step, pair):
                n = (3 * step + pair) % 2
                need(pe, s["v_taken" if pair else "qk1_taken"], g)
                parts = []
                for i in range(2):
                    c = i * HEADS * DH + (2 * step + pair) * 128
                    parts.append((w_high[:, c:c + 128], w_low[:, c:c + 128], h_high[:], h_low[:], proj_bank[n][:, i * 256:i * 256 + 256]))
                project(proj_bank[n], parts).then_inc(s["qk1_ready" if pair else "qk0_ready"], 1)

            def project_v(g, step):
                n = (3 * step + 2) % 2
                need(pe, s["qk0_taken"], g + 1)
                c = 2 * HEADS * DH + step * 256
                parts = [(h_high[:, i * 128:i * 128 + 128], h_low[:, i * 128:i * 128 + 128], w_high[:, c:c + 256], w_low[:, c:c + 256], proj_bank[n][:, i * 256:i * 256 + 256]) for i in range(2)]
                project(proj_bank[n], parts).then_inc(s["v_ready"], 1)

            def apply_probs(g, step, owner):
                pe.wait_ge(s["pt_taken"], 2 * g + 2)
                pe.wait_ge(v_shifted[step], 32 * (owner + 1))
                need(pe, s["attn_taken"], g)
                for j in range(2):
                    for parity in range(2):
                        rows = slice(64 * parity, 64 * parity + 64)
                        head = (2 * j + parity) * DH
                        p = probsT[step % 2][:, parity * 512 + j * 256:parity * 512 + j * 256 + 256]
                        for value, a, e in ((0, 0, 128), (2, 128, 192), (1, 192, 256)):
                            done = nc.tensor.matmul(attn_bank[rows, j * 256 + a:j * 256 + e], v[step % 4][:, value * 256 + head:value * 256 + head + DH], p[:, a:e], start=True, stop=True, skip_group_check=True)
                done.then_inc(s["attn_ready"], 1)

            def body(b, _, __):
                for step in range(4):
                    g = 4 * b + step
                    before = b if step else b - 1
                    after = b + 1 if step == 3 else b
                    if real(b):
                        pe.wait_ge(s["qk0_taken"], g + 1)
                        pe.wait_ge(s["qk1_taken"], g + 1)
                        window(g, step, 0)
                        window(g, step, 1)
                    if real(before):
                        transpose_probs(g - 1, (step - 1) % 4, 0)
                        transpose_probs(g - 1, (step - 1) % 4, 1)
                    if step == 0 and real(b - 2):
                        pe.wait_ge(s["send_done"], b - 1)
                        pe.wait_ge(s["zt_taken"], last(b) + 1)
                        need(pe, s["rk_taken"], last(b - 3) + 1)
                        for i in range(2):
                            done = nc.tensor.transpose(misc[:, i * 128:i * 128 + 128], send[:, i * SENT:i * SENT + D], ident)
                        done.then_inc(s["nt_ready"], 1)
                    if step == 1 and real(b - 2):
                        pe.wait_ge(s["hot_ready"], b - 1)
                        nc.tensor.matmul(misc[:, 0:E], before_b[:], hot_b[:, 0:E], start=True, stop=True)
                        nc.tensor.matmul(misc[:, E:2 * E], ones_b[:], hot_b[:, 0:E], start=True, stop=False)
                        nc.tensor.matmul(misc[:, E:2 * E], before_b[:], hot_b[:, E:2 * E], start=False, stop=True)
                        nc.tensor.matmul(misc[:, 2 * E:3 * E], ones_b[:], hot_b[:, 0:E], start=True, stop=False)
                        nc.tensor.matmul(misc[:, 2 * E:3 * E], ones_b[:], hot_b[:, E:2 * E], start=False, stop=True).then_inc(s["rk_ready"], 1)
                    if step == 2 and real(b + 1):
                        pe.wait_ge(s["z_a_done"], b + 2)
                        need(pe, s["yt_taken"], last(b - 1) + 1)
                        need(pe, s["zt_taken"], b + 1)
                        for i in range(2):
                            done = nc.tensor.transpose(misc[:, i * 128:i * 128 + 128], z_a[:, i * 128:i * 128 + 128], ident)
                        done.then_inc(s["zt_ready"], 1)
                    if real(after):
                        if step == 3:
                            pe.wait_ge(s["split_ready"], b + 2)
                        project_qk(g + 1, (step + 1) % 4, 0)
                        project_qk(g + 1, (step + 1) % 4, 1)
                    if step == 1 and real(b - 1):
                        pe.wait_ge(s["attn_taken"], 4 * b)
                        pe.wait_ge(s["zt_taken"], last(b) + 1)
                        need(pe, s["rk_taken"], b - 1)
                        for c in range(8):
                            done = nc.tensor.matmul(misc[:, 0:256], w_out[:, c * D:(c + 1) * D], attn[:, c * 256:c * 256 + 256], start=c == 0, stop=c == 7)
                        done.then_inc(s["y_ready"], 1)
                    if real(before):
                        apply_probs(g - 1, (step - 1) % 4, before)
                    if real(after):
                        project_v(g + 1, (step + 1) % 4)
                    if step == 0 and real(b - 2):
                        pe.wait_ge(s["nt_taken"], b - 1)
                        for i in range(2):
                            done = nc.tensor.matmul(misc[:, i * E:(i + 1) * E], nT[:, i * 128:i * 128 + 128], router[:], start=True, stop=True)
                        done.then_inc(s["lg_ready"], 1)
                    if step == 1 and real(b - 1):
                        pe.wait_ge(s["y_taken"], b)
                        for i in range(2):
                            done = nc.tensor.transpose(misc[:, i * 128:i * 128 + 128], yT[:, i * 128:i * 128 + 128], ident)
                        done.then_inc(s["yt_ready"], 1)

            turns(pe, body)

        @block.scalar
        def _(act):
            act.wait_ge(s["small_in"], 128)
            for n in range(2):
                nc.scalar.activation(c_col[n][:], c_col[n][:], ACT.Silu).then_inc(s["c_silu"], 1)
            split_experts_high(nc, act, raw_experts, weights[0], s["experts_in"], EXPERT_LOADS, s["experts_high"])
            act.wait_ge(s["experts_low"], E + 1)
            act.wait_ge(s["consts_in"], 16)
            act.wait_ge(s["split_done"], 1)
            nc.scalar.preload_act_table_set("natural_log_exp_and_others")

            def exponentials(g, step, parity):
                act.wait_ge(s["negmax_ready"], 2 * g + parity + 1)
                need(act, s["pt_ready"], 2 * (g - 2) + parity + 1)
                need(act, s["inverse_ready"], 2 * (g - 2) + parity + 1)
                for n in range(4):
                    slot = step % 2 * 8 + parity * 4 + n
                    at = parity * 512 + n * 128
                    done = nc.scalar.activation(probs[step % 2][:, at:at + 128], scores_bank[parity][:, n * 128:n * 128 + 128], ACT.Exp,
                                                bias=neg_max[:, slot:slot + 1], accum_out=sums[:, slot:slot + 1])
                done.then_inc(s["exp_done"], 1)

            def layer_norm_scale(owner, n, kind):
                act.wait_ge(s["stats_" + kind], owner + 1)
                variance = moments[:, 4 * n:4 * n + 4].rearrange("p (i two) -> p i two", two=2)[:, :, 1]
                nc.scalar.activation(log_var[:, 2 * n:2 * n + 2], variance, ACT.Ln, bias=const[:, C_EPS:C_EPS + 1]).then_inc(s["log_" + kind], 1)
                act.wait_ge(s["log_" + kind], owner + 1)
                nc.scalar.activation(rstd[:, 2 * n:2 * n + 2], log_var[:, 2 * n:2 * n + 2], ACT.Exp, scale=-0.5).then_inc(s["rstd_" + kind], 1)

            def body(b, _, __):
                for step in range(4):
                    g = 4 * b + step
                    before = b if step else b - 1
                    after = b + 1 if step == 3 else b
                    if step == 1 and real(b + 1):
                        layer_norm_scale(b + 1, 0, "a")
                    if real(b):
                        exponentials(g, step, 0)
                        exponentials(g, step, 1)
                    if step == 3 and real(b - 1):
                        layer_norm_scale(b - 1, 2, "c")
                    if step == 2 and real(b - 1):
                        layer_norm_scale(b - 1, 1, "b")
                    if step == 2 and real(b + 1):
                        act.wait_ge(s["zt_ready"], b + 2)
                        need(act, s["split_ready"], b + 1)
                        nc.scalar.activation(hT[:], misc[:, 0:256], ACT.Identity, scale=mod_col[0][:, cols(CA * B + b + 1, 1)],
                                             bias=mod_col[0][:, cols(SA * B + b + 1, 1)]).then_inc(s["zt_taken"], 1)
                    if real(after):
                        act.wait_ge(s["qk0_ready"], g + 2)
                        need(act, s["scores_ready"], 2 * g)
                        nc.scalar.copy(qk[(step + 1) % 2][:, 0:512], proj_bank[3 * ((step + 1) % 4) % 2][:]).then_inc(s["qk0_taken"], 1)
                    if step == 1 and real(b - 2):
                        act.wait_ge(s["low_top_done"], b - 1)
                        need(act, s["score_done"], b - 2)
                        nc.scalar.activation(exp_top[:], low_top[:], ACT.Exp, scale=-1.0).then_inc(s["exp_top_done"], 1)
                    if step == 1 and real(b - 1):
                        act.wait_ge(s["y_ready"], b)
                        need(act, s["yt_ready"], b - 1)
                        nc.scalar.activation(yT[:], misc[:, 0:256], ACT.Copy, scale=mod_col[0][:, cols(GA * B + b - 1, 1)]).then_inc(s["y_taken"], 1)
                    if real(before):
                        act.wait_ge(s["attn_ready"], g)
                        need(act, s["y_ready"], before)
                        n = (step - 1) % 4
                        nc.scalar.copy(attn[:, n * 512:n * 512 + 512], attn_bank[:]).then_inc(s["attn_taken"], 1)

            turns(act, body)

        @block.vector
        def _(dve):
            steps = [0]

            def then(instruction):
                steps[0] += 1
                instruction.then_inc(s["setup_steps"], 1)
                dve.wait_ge(s["setup_steps"], steps[0])

            dve.wait_ge(s["consts_in"], 16)
            for to, at, size in ((ident_b, C_IDENT, 128), (window_b, C_WINDOW, 256), (before_b, C_BEFORE, 128), (ones_b, C_ONES, 128)):
                done = nc.vector.tensor_copy(to[:], const[:, at:at + size])
            done.then_inc(s["consts_cast"], 1)
            nc.vector.memset(send[:], 0.0)
            for n in range(2):
                nc.vector.tensor_copy(counts[n][:], const[:, C_REGION:C_REGION + E])
            dve.wait_ge(s["weights_in"], 96)
            raw = [half[:, 0:512] for pair in (probs, probsT, qk) for half in pair]
            for n, part in enumerate(raw):
                scale = DH ** -0.5 if n < 2 else 1.0
                at = slice(n * 512, n * 512 + 512)
                then(nc.vector.tensor_scalar(w_high[:, at], part, scale, None, ALU.mult))
                done = nc.vector.scalar_tensor_tensor(w_low[:, at], part, scale, w_high[:, at].bitcast(F32), ALU.mult, ALU.subtract)
            done.then_inc(s["split_done"], 1)

            def gate(out_, in_, rows, width):
                m = [mod_tmp[0:rows, k * width:(k + 1) * width] for k in range(2)]
                then(nc.vector.tensor_scalar(m[0], in_, -1.0, None, ALU.mult))
                then(nc.vector.tensor_tensor(m[1], in_, m[0], ALU.max))
                then(nc.vector.tensor_scalar(m[0], in_, 0.0, 2.0, ALU.is_ge, ALU.mult))
                then(nc.vector.tensor_scalar(m[0], m[0], -1.0, None, ALU.add))
                then(nc.vector.scalar_tensor_tensor(out_, m[1], GATE_MIN, m[0], ALU.max, ALU.mult))

            for n in range(2):
                dve.wait_ge(s["mod_made"], n + 1)
                columns, raw_rows = mod_col[n], mod_stage[n]
                then(nc.vector.tensor_copy(columns[:], banks[4 + n][:, 0:6 * B]))
                for kind in (CA, CB):
                    then(nc.vector.tensor_scalar(columns[:, kind * B:(kind + 1) * B], columns[:, kind * B:(kind + 1) * B], 1.0, None, ALU.add))
                for kind in (GA, GB):
                    gate(columns[:, kind * B:(kind + 1) * B], columns[:, kind * B:(kind + 1) * B], 128, B)
                for half in range(2):
                    then(nc.vector.tensor_copy(raw_rows[:, half * 384:half * 384 + 384], banks[2 * n + half][0:B, 0:384]))
                for kind in (CA, CB):
                    then(nc.vector.tensor_scalar(raw_rows[:, kind * D:(kind + 1) * D], raw_rows[:, kind * D:(kind + 1) * D], 1.0, None, ALU.add))
                for kind in (GA, GB):
                    gate(raw_rows[:, kind * D:(kind + 1) * D], raw_rows[:, kind * D:(kind + 1) * D], B, D)
                dve.sem_inc(s["mod_rows_made"], 1)
                dve.sem_inc(s["mod_taken"], 1)
            dve.wait_ge(s["x_in"], 64)
            dve.wait_ge(s["experts_low"], E + 1)

            def maxima(g, step, parity):
                dve.wait_ge(s["scores_ready"], 2 * g + parity + 1)
                need(dve, s["exp_done"], 2 * (g - 2) + parity + 1)
                slot = step % 2 * 8 + parity * 4
                nc.vector.tensor_reduce(neg_max[:, slot:slot + 4], scores_bank[parity][:].rearrange("p (n k) -> p n k", k=128), AX.X, ALU.max,
                                        negate=True).then_inc(s["negmax_ready"], 1)

            def inverses(g, step, parity):
                dve.wait_ge(s["exp_done"], 2 * g + parity + 1)
                need(dve, s["norm_done"], 2 * (g - 2) + parity + 1)
                slot = step % 2 * 8 + parity * 4
                nc.vector.reciprocal(inverse[:, slot:slot + 4], sums[:, slot:slot + 4]).then_inc(s["inverse_ready"], 1)

            def statistics(n, kind, owner, source):
                wait_apart(dve, s["rstd_" + kind], owner, s["passed_dve"])
                for i in range(2):
                    done = nc.vector.bn_stats(stats[:, 12 * n + 6 * i:12 * n + 6 * i + 6], source[i])
                done.then_inc(s["parts_" + kind], 1)
                wait_apart(dve, s["parts_" + kind], owner + 1, s["passed_dve"])
                for i in range(2):
                    done = nc.vector.bn_aggr(moments[:, 4 * n + 2 * i:4 * n + 2 * i + 2], stats[:, 12 * n + 6 * i:12 * n + 6 * i + 6])
                done.then_inc(s["stats_" + kind], 1)

            def normed(n, kind, owner, to, source):
                dve.wait_ge(s["rstd_" + kind], owner + 1)
                for i in range(2):
                    done = nc.vector.tensor_scalar(to[:, i * 128:i * 128 + 128], source[i], moments[:, 4 * n + 2 * i:4 * n + 2 * i + 1],
                                                   rstd[:, 2 * n + i:2 * n + i + 1], ALU.subtract, ALU.mult)
                done.then_inc(s[f"z_{kind}_done"], 1)

            def tiles_of_x(owner):
                return [x[:, cols(owner * 256 + i * 128, 128)] for i in range(2)]

            def choose(b):
                dve.wait_ge(s["lg_ready"], b + 1)
                nc.vector.tensor_copy(logits[:], misc[:, 0:16]).then_inc(s["lg_taken"], 1)
                wait_apart(dve, s["lg_taken"], b + 1, s["passed_dve"])
                for i in range(2):
                    done = nc.vector.max(top[:, i * 8:i * 8 + 8], logits[:, i * 8:i * 8 + 8])
                done.then_inc(s["top_done"], 1)
                wait_apart(dve, s["top_done"], b + 1, s["passed_dve"])
                for i in range(2):
                    done = nc.vector.max_index(top_at[:, i * 8:i * 8 + 8], top[:, i * 8:i * 8 + 8], logits[:, i * 8:i * 8 + 8])
                done.then_inc(s["top_at_done"], 1)
                need(dve, s["exp_top_done"], b)
                nc.vector.tensor_scalar(low_top[:], top[:].rearrange("p (i e) -> p i e", e=8)[:, :, 0], -87.0, None, ALU.max).then_inc(s["low_top_done"], 1)
                dve.wait_ge(s["top_at_done"], b + 1)
                nc.vector.tensor_copy(expert[:], top_at[:].rearrange("p (i e) -> p i e", e=8)[:, :, 0]).then_inc(s["expert_done"], 1)
                dve.wait_ge(s["expert_done"], b + 1)
                for i in range(2):
                    done = nc.vector.tensor_scalar(hot[:, i * 8:i * 8 + 8], const[:, C_INDEX:C_INDEX + E], expert[:, i:i + 1], None, ALU.is_equal)
                done.then_inc(s["hot_done"], 1)
                dve.wait_ge(s["hot_done"], b + 1)
                need(dve, s["rk_ready"], b)
                nc.vector.tensor_copy(hot_b[:], hot[:]).then_inc(s["hot_ready"], 1)

            def take_ranks(b):
                dve.wait_ge(s["rk_ready"], b + 1)
                nc.vector.tensor_tensor(place[:].rearrange("p (i e) -> p i e", e=8), misc[:, 0:16].rearrange("p (i e) -> p i e", e=8),
                                        counts[0][:].unsqueeze(1).broadcast_to([128, 2, 8]), ALU.add).then_inc(s["place_made"], 1)
                dve.wait_ge(s["place_made"], b + 1)
                nc.vector.tensor_tensor(counts[0][:], misc[:, 16:24], counts[0][:], ALU.add).then_inc(s["rk_taken"], 1)

            def choose_rows(b):
                nc.vector.tensor_tensor(picked[:], place[:], hot[:], ALU.mult).then_inc(s["picked_done"], 1)
                dve.wait_ge(s["picked_done"], b + 1)
                nc.vector.tensor_reduce(place_f[:], picked[:].rearrange("p (i e) -> p i e", e=8), AX.X, ALU.add).then_inc(s["place_summed"], 1)
                dve.wait_ge(s["place_summed"], b + 1)
                need(dve, sent_done, 32 * b)
                nc.vector.tensor_copy(rows_at[0][:, cols(2 * b, 2)], place_f[:])
                nc.vector.tensor_copy(rows_now[:], place_f[:]).then_inc(s["place_done"], 1)

            def score(b):
                dve.wait_ge(s["exp_top_done"], b + 1)
                nc.vector.tensor_scalar(low_top[:], exp_top[:], 1.0, None, ALU.add).then_inc(s["score_steps"], 1)
                dve.wait_ge(s["score_steps"], b + 1)
                nc.vector.reciprocal(send[:].rearrange("p (i w) -> p i w", w=SENT)[:, :, D], low_top[:]).then_inc(s["score_done"], 1)

            def body(b, _, __):
                for step in range(4):
                    g = 4 * b + step
                    before = b if step else b - 1
                    after = b + 1 if step == 3 else b

                    def take_transposed(parity):
                        if real(before):
                            dve.wait_ge(s["pt_ready"], 2 * (g - 1) + parity + 1)
                            need(dve, s["attn_ready"], g - 2)
                            nc.vector.tensor_copy(probsT[(step - 1) % 2][:, parity * 512:parity * 512 + 512], pt_bank[parity][:]).then_inc(s["pt_taken"], 1)

                    if step == 1 and real(b - 2):
                        choose(b - 2)
                    if step == 2 and real(b - 1):
                        dve.wait_ge(s["yt_ready"], b)
                        now = x[:, cols((b - 1) * 256, 256)]
                        nc.vector.tensor_tensor(now, misc[:, 0:256], now, ALU.add).then_inc(s["yt_taken"], 1)
                    if step == 3 and real(b + 1):
                        dve.wait_ge(s["zt_taken"], b + 2)
                        need(dve, s["v_ready"], 4 * b + 4)
                        nc.vector.tensor_copy(h_high[:], hT[:]).then_inc(s["high_done"], 1)
                        dve.wait_ge(s["high_done"], b + 2)
                        nc.vector.tensor_tensor(h_low[:], hT[:], h_high[:].bitcast(F32), ALU.subtract).then_inc(s["split_ready"], 1)
                    if real(b):
                        maxima(g, step, 0)
                        maxima(g, step, 1)
                    if step == 2 and real(b - 1):
                        dve.wait_ge(s["yt_taken"], b)
                        statistics(1, "b", b - 1, tiles_of_x(b - 1))
                    if step == 3 and real(b - 1):
                        dve.wait_ge(s["h_b_done"], b)
                        statistics(2, "c", b - 1, [h_b[:, i * 128:i * 128 + 128] for i in range(2)])
                    take_transposed(0)
                    if real(b):
                        inverses(g, step, 0)
                    take_transposed(1)
                    if step == 0 and real(b - 2):
                        dve.wait_ge(s["nt_ready"], b - 1)
                        need(dve, s["lg_ready"], b - 2)
                        nc.vector.tensor_copy(nT[:], misc[:, 0:256]).then_inc(s["nt_taken"], 1)
                    if step == 1 and real(b - 2):
                        take_ranks(b - 2)
                    if real(b):
                        inverses(g, step, 1)
                    if real(after):
                        dve.wait_ge(s["qk1_ready"], g + 2)
                        need(dve, s["scores_ready"], 2 * g)
                        nc.vector.tensor_copy(qk[(step + 1) % 2][:, 512:1024], proj_bank[(3 * ((step + 1) % 4) + 1) % 2][:]).then_inc(s["qk1_taken"], 1)
                    if step == 0 and real(b + 1):
                        statistics(0, "a", b + 1, tiles_of_x(b + 1))
                    if step == 1 and real(b + 1):
                        need(dve, s["zt_ready"], b + 1)
                        normed(0, "a", b + 1, z_a, tiles_of_x(b + 1))
                    if step == 1 and real(b - 2):
                        choose_rows(b - 2)
                    if step == 2 and real(b - 1):
                        need(dve, s["h_b_done"], b - 1)
                        normed(1, "b", b - 1, z_b, tiles_of_x(b - 1))
                    if step == 2 and real(b - 2):
                        score(b - 2)
                    if step == 3 and real(b - 1):
                        need(dve, s["send_done"], b - 1)
                        normed(2, "c", b - 1, z_c, [h_b[:, i * 128:i * 128 + 128] for i in range(2)])
                    if real(after):
                        dve.wait_ge(s["v_ready"], g + 2)
                        need(dve, s["attn_ready"], g - 2)
                        nc.vector.tensor_copy(v[(step + 1) % 4][:, 0:512], proj_bank[(3 * ((step + 1) % 4) + 2) % 2][:]).then_inc(s["v_taken"], 1)

            turns(dve, body)

        @block.gpsimd
        def _(pool):
            def normalise(g, step, parity):
                pool.wait_ge(s["inverse_ready"], 2 * g + parity + 1)
                slot = step % 2 * 8 + parity * 4
                p = probs[step % 2][:, parity * 512:parity * 512 + 512].rearrange("p (n k) -> p n k", k=128)
                nc.gpsimd.tensor_tensor(p, p, inverse[:, slot:slot + 4].unsqueeze(2).broadcast_to([128, 4, 128]), ALU.mult).then_inc(s["norm_done"], 1)

            def over_tiles(row):
                return row.unsqueeze(1).broadcast_to([128, 2, D])

            def tiles(buffer):
                return buffer.rearrange("p (i d) -> p i d", d=D)

            shift, scale, gate = (over_tiles(mod_b[:, n * D:(n + 1) * D]) for n in range(3))

            def body(b, _, __):
                for step in range(4):
                    g = 4 * b + step
                    if real(b):
                        normalise(g, step, 0)
                        normalise(g, step, 1)
                    if step == 2 and real(b - 1):
                        pool.wait_ge(s["z_b_done"], b)
                        pool.wait_ge(s["mod_b_in"], 16 * b)
                        need(pool, s["z_c_done"], b - 1)
                        nc.gpsimd.tensor_tensor(tiles(h_b[:]), tiles(z_b[:]), scale, ALU.mult).then_inc(s["scaled_b"], 1)
                        pool.wait_ge(s["scaled_b"], b)
                        nc.gpsimd.tensor_tensor(tiles(h_b[:]), tiles(h_b[:]), shift, ALU.add).then_inc(s["h_b_done"], 1)
                    if step == 2 and real(b - 2):
                        pool.wait_ge(s["place_done"], b - 1)
                        wait_apart(pool, s["score_done"], b - 1, s["passed_pool"])
                        for i in range(2):
                            nc.gpsimd.indirect_dma_start(sent[0], bass.IndirectOffsetOnAxis(ap=rows_now[:, i:i + 1], axis=0),
                                                         send[:, i * SENT:(i + 1) * SENT], None).then_inc(sent_done, 16)
                    if step == 3 and real(b - 1):
                        pool.wait_ge(s["h_b_done"], b)
                        nc.gpsimd.tensor_tensor(tiles(g_b[:]), tiles(h_b[:]), gate, ALU.mult).then_inc(s["gated_b"], 1)
                        pool.wait_ge(s["gated_b"], b)
                        now = x[:, cols((b - 1) * 256, 256)]
                        nc.gpsimd.tensor_tensor(now, now, g_b[:], ALU.add).then_inc(s["x_b_done"], 1)
                        pool.wait_ge(s["z_c_done"], b)
                        need(pool, sent_done, 32 * (b - 1))
                        need(pool, s["nt_ready"], b - 1)
                        rows = send[:].rearrange("p (i w) -> p i w", w=SENT)[:, :, 0:D]
                        nc.gpsimd.tensor_tensor(rows, tiles(z_c[:]), over_tiles(ln_row[:, 0:D]), ALU.mult).then_inc(s["scaled_c"], 1)
                        pool.wait_ge(s["scaled_c"], b)
                        nc.gpsimd.tensor_tensor(rows, rows, over_tiles(ln_row[:, D:2 * D]), ALU.add).then_inc(s["send_done"], 1)

            split_experts_low(nc, pool, raw_experts, weights[0], weights[1], s["experts_high"], s["experts_low"])
            pool.wait_ge(s["small_in"], 128)
            turns(pool, body)
            pool.wait_ge(sent_done, 32 * B)

        ctx_block.close()
        clear(nc, used)


def load_experts(engine, t, layer, raw, second, loaded):
    def first(start, size):
        return raw[start // 512][:, start % 512:start % 512 + size]

    count = 0
    for e in range(E + 1 if layer == 0 else E):
        if layer:
            loads = [(first(e * F, F), t["L1_ffn_W1"][e])]
            down = t["L1_ffn_W2"][e]
        elif e < E:
            loads = [(first((2 * e + i) * F, F), t[f"L0_ffn_{k}_w"][e]) for i, k in enumerate(("gate", "up"))]
            down = t["L0_ffn_down_w"][e]
        else:
            loads = [(first((2 * e + i) * F, F), t[f"L0_ffn_sh_{k}"]) for i, k in enumerate(("gate", "up"))]
            down = t["L0_ffn_sh_down"]
        loads.append((second[:, e * F:(e + 1) * F].rearrange("p (c n) -> p c n", n=D), down.rearrange("(c p) n -> p c n", p=128)))
        for to, source in loads:
            engine.dma_start(to, source).then_inc(loaded, 16)
            count += 16
    return count


def split_experts_high(nc, act, raw, high, loaded, loads, high_done):
    act.wait_ge(loaded, loads)
    for n, piece in enumerate(raw):
        nc.scalar.copy(high[:, n * 512:(n + 1) * 512], piece).then_inc(high_done, 1)


def split_experts_low(nc, pool, raw, high, low, high_done, low_done):
    for n, piece in enumerate(raw):
        at = slice(n * 512, (n + 1) * 512)
        pool.wait_ge(high_done, n + 1)
        nc.gpsimd.tensor_tensor(low[:, at], piece, high[:, at].bitcast(F32), ALU.subtract).then_inc(low_done, 1)


def experts(nc, t, layer, counts, rows_at, back_at, sent, back, banks, const, ident, weights):
    ctx = ExitStack()
    with ctx:
        def sb(name, columns, kind=F32, rows=128):
            return ctx.enter_context(nc.sbuf_tensor(f"{name}_{layer}", [rows, columns], kind))

        used = []

        def sem(name):
            used.append(ctx.enter_context(nc.semaphore(f"e{layer}_{name}")))
            return used[-1]

        shared = layer == 0
        width = 2 * F if shared else F
        branches = 2 if shared else 1
        chunks = 2 * branches
        kinds = E + 1 if shared else E
        row = SENT if shared else D
        up_high, up_low, down = weights
        if not shared:
            bias1, bias2 = sb("bias1", E * F), sb("bias2", E * D)
        tiles_of, ends, delta = sb("tiles_of", E), sb("ends", E), sb("delta", E)
        tiles_u, counts_u = sb("tiles_u", E, U32), sb("counts_u", E, U32)
        past, moves = sb("past", SLOTS * E), sb("moves", SLOTS * E)
        slot_f, slot_move = sb("slot_f", SLOTS), sb("slot_move", SLOTS)
        slot_expert, slot_row = sb("slot_expert", SLOTS, U32), sb("slot_row", SLOTS, U32)
        zeros = sb("zeros", row)
        rows_in = [sb(f"rows_in{n}", row) for n in range(4)]
        n_high, n_low = ([sb(f"{k}{n}", 128, F32R) for n in range(2)] for k in ("n_high", "n_low"))
        act_out = [sb(f"act_out{n}", branches * F) for n in range(2)]
        hidden = [sb(f"hidden{n}", branches * F) for n in range(2)]
        hiddenT = [sb(f"hiddenT{n}", chunks * 128) for n in range(2)]
        result = [sb(f"result{n}", D) for n in range(2)]

        s = {n: sem(n) for n in """bias_in setup_steps zeros_ready counts_ready slots_ready zeroed
            nT_ready high_done split_ready first_ready activated hidden_ready biased hiddenT_ready hiddenT_taken y_ready y_taken""".split()}
        rows_loaded = [sem(f"rows_loaded{n}") for n in range(4)]
        rows_stored = [sem(f"rows_stored{n}") for n in range(2)]
        first_bank = [banks[0:2], banks[2:4]]
        nT_bank, hidden_bank, y_bank = banks[4], banks[5], banks[6]

        def slots(engine, body):
            turns(engine, lambda n, k, i: body(n, k % 2, k, i), SLOTS, 4, 3, 2)

        def slot(n):
            return real(n, SLOTS)

        def clear_tails(engine, of):
            for e in of:
                at = engine.value_load(counts_u[0:1, e:e + 1], min_val=0, max_val=(E + 1) * CAP - 128)
                engine.dma_start(sent[bass.ds(at, 128), 0:row], zeros[:]).then_inc(s["zeroed"], 16)

        ctx_block = ExitStack()
        block = ctx_block.enter_context(nc.Block())

        @block.sync
        def _(sp):
            if not shared:
                sp.dma_start(bias1[:], t["L1_ffn_b1"].rearrange("e f -> (e f)").partition_broadcast(128)).then_inc(s["bias_in"], 16)
                sp.dma_start(bias2[:], t["L1_ffn_b2"].rearrange("e d -> (e d)").partition_broadcast(128)).then_inc(s["bias_in"], 16)
            sp.wait_ge(s["counts_ready"], 1)
            clear_tails(sp, range(4))
            sp.wait_ge(s["slots_ready"], 1)
            sp.wait_ge(s["zeroed"], 16 * (E + 1))

            def body(n, parity, k, i):
                if slot(n + 3):
                    at = sp.value_load(slot_row[0:1, cols(n + 3, 1)], min_val=0, max_val=(E + 1) * CAP - 128)
                    need(sp, s["nT_ready"], n)
                    if shared:
                        need(sp, s["hidden_ready"], n)
                    sp.dma_start(rows_in[(k + 3) % 4][:], sent[bass.ds(at, 128), 0:row]).then_inc(rows_loaded[(k + 3) % 4], 16)
                if slot(n - 2):
                    sp.wait_ge(s["y_taken"], n - 1)
                    sp.dma_start(back[cols(128 * (n - 2), 128), :], result[parity][:]).then_inc(rows_stored[parity], 16)

            slots(sp, body)
            for p in range(2):
                sp.wait_ge(rows_stored[p], 16 * (SLOTS // 2))

        @block.tensor
        def _(pe):
            pe.wait_ge(s["slots_ready"], 1)

            def body(n, parity, k, i):
                if slot(n):
                    own = pe.value_load(slot_expert[0:1, cols(n, 1)], min_val=0, max_val=kinds - 1)
                    pe.wait_ge(s["split_ready"], n + 1)
                    need(pe, s["hidden_ready"], n - 1)
                    for branch in range(branches):
                        weights = [w[:, cols(own * width, width)] if branch == 0 else w[:, E * width:(E + 1) * width] for w in (up_high, up_low)]
                        to = first_bank[parity][branch][:, 0:width]
                        nc.tensor.matmul(to, n_high[parity][:], weights[0], start=True, stop=False)
                        nc.tensor.matmul(to, n_high[parity][:], weights[1], start=False, stop=False)
                        done = nc.tensor.matmul(to, n_low[parity][:], weights[0], start=False, stop=True)
                    done.then_inc(s["first_ready"], 1)
                if slot(n + 1):
                    buffer = (k + 1) % 4
                    pe.wait_ge(rows_loaded[buffer], 16 * (i + (k + 1) // 4 + 1))
                    need(pe, s["split_ready"], n + 1)
                    nc.tensor.transpose(nT_bank[:, 0:128], rows_in[buffer][:, 0:D], ident).then_inc(s["nT_ready"], 1)
                if slot(n - 1):
                    pe.wait_ge(s["hidden_ready"], n)
                    need(pe, s["hiddenT_taken"], n - 1)
                    for c in range(chunks):
                        done = nc.tensor.transpose(hidden_bank[:, c * 128:c * 128 + 128], hidden[1 - parity][:, c * 128:c * 128 + 128], ident)
                    done.then_inc(s["hiddenT_ready"], 1)
                if slot(n - 2):
                    own = pe.value_load(slot_expert[0:1, cols(n - 2, 1)], min_val=0, max_val=kinds - 1)
                    pe.wait_ge(s["hiddenT_taken"], n - 1)
                    need(pe, s["y_taken"], n - 2)
                    for c in range(chunks):
                        w = down[:, cols(own * F + c * D, D)] if c < 2 else down[:, E * F + (c - 2) * D:E * F + (c - 1) * D]
                        done = nc.tensor.matmul(y_bank[:, 0:D], hiddenT[parity][:, c * 128:c * 128 + 128], w, start=c == 0, stop=c == chunks - 1)
                    done.then_inc(s["y_ready"], 1)

            slots(pe, body)

        @block.scalar
        def _(act):
            act.wait_ge(s["zeros_ready"], 1)
            act.dma_start(sent[E * CAP:E * CAP + E * 128, 0:row].rearrange("(n p) w -> p n w", p=128), zeros[:].unsqueeze(1).broadcast_to([128, E, row])).then_inc(s["zeroed"], 16)
            act.wait_ge(s["counts_ready"], 1)
            clear_tails(act, range(4, E))

            def body(n, parity, k, i):
                if slot(n):
                    act.wait_ge(s["first_ready"], n + 1)
                    need(act, s["hidden_ready"], n - 1)
                    if shared:
                        score = rows_in[k][:, D:D + 1]
                        nc.scalar.activation(act_out[parity][:, 0:F], first_bank[parity][0][:, 0:F], ACT.Silu, scale=score)
                        nc.scalar.activation(act_out[parity][:, F:2 * F], first_bank[parity][1][:, 0:F], ACT.Silu).then_inc(s["activated"], 1)
                    else:
                        act.wait_ge(s["biased"], n + 1)
                        need(act, s["hiddenT_ready"], n - 1)
                        nc.scalar.activation(hidden[parity][:], act_out[parity][:], ACT.Gelu).then_inc(s["hidden_ready"], 1)
                if slot(n - 1):
                    act.wait_ge(s["hiddenT_ready"], n)
                    need(act, s["y_ready"], n - 2)
                    nc.scalar.copy(hiddenT[1 - parity][:], hidden_bank[:, 0:chunks * 128]).then_inc(s["hiddenT_taken"], 1)

            slots(act, body)

        @block.vector
        def _(dve):
            steps = [0]

            def then(instruction):
                steps[0] += 1
                instruction.then_inc(s["setup_steps"], 1)
                dve.wait_ge(s["setup_steps"], steps[0])

            nc.vector.memset(zeros[:], 0.0).then_inc(s["zeros_ready"], 1)
            nc.vector.tensor_copy(counts_u[:], counts[:]).then_inc(s["counts_ready"], 1)
            then(nc.vector.tensor_tensor(tiles_of[:], counts[:], const[:, C_REGION:C_REGION + E], ALU.subtract))
            then(nc.vector.tensor_scalar(tiles_of[:], tiles_of[:], 63.5, 1 / 128, ALU.add, ALU.mult))
            then(nc.vector.tensor_copy(tiles_u[:], tiles_of[:]))
            then(nc.vector.tensor_copy(tiles_of[:], tiles_u[:]))
            then(nc.vector.tensor_tensor_scan(ends[:], const[:, C_ONES:C_ONES + E], tiles_of[:], 0.0, ALU.mult, ALU.add))
            nc.vector.tensor_scalar(delta[:], tiles_of[:], -128.0, float(CAP), ALU.mult, ALU.add)

            def by_expert(buffer, count, experts_):
                return buffer[:, 0:count * experts_].rearrange("p (n e) -> p n e", e=experts_)

            def along(row, count):
                return row.unsqueeze(1).broadcast_to([128, count, row.shape[1]])

            slot_index = const[:, C_SLOT:C_SLOT + SLOTS]
            then(nc.vector.tensor_tensor(by_expert(past, SLOTS, E), slot_index.unsqueeze(2).broadcast_to([128, SLOTS, E]), along(ends[:], SLOTS), ALU.is_ge))
            nc.vector.tensor_reduce(slot_f[:], by_expert(past, SLOTS, E), AX.X, ALU.add)
            then(nc.vector.tensor_tensor(by_expert(moves, SLOTS, E), by_expert(past, SLOTS, E), along(delta[:], SLOTS), ALU.mult))
            then(nc.vector.tensor_reduce(slot_move[:], by_expert(moves, SLOTS, E), AX.X, ALU.add))
            nc.vector.tensor_scalar(slot_f[:], slot_f[:], float(kinds - 1), None, ALU.min)
            then(nc.vector.scalar_tensor_tensor(slot_move[:], slot_index, 128.0, slot_move[:], ALU.mult, ALU.add))
            nc.vector.tensor_copy(slot_row[:], slot_move[:])
            nc.vector.tensor_copy(slot_expert[:], slot_f[:]).then_inc(s["slots_ready"], 1)
            then(nc.vector.tensor_tensor(by_expert(past, TILES, E - 1), rows_at[:].unsqueeze(2).broadcast_to([128, TILES, E - 1]),
                                         along(const[:, C_REGION + 1:C_REGION + E], TILES), ALU.is_ge))
            then(nc.vector.tensor_tensor(by_expert(moves, TILES, E - 1), by_expert(past, TILES, E - 1), along(delta[:, 0:E - 1], TILES), ALU.mult))
            then(nc.vector.tensor_reduce(slot_f[:, 0:TILES], by_expert(moves, TILES, E - 1), AX.X, ALU.add))
            then(nc.vector.tensor_tensor(back_at[:], rows_at[:], slot_f[:, 0:TILES], ALU.subtract))
            dve.wait_ge(s["slots_ready"], 1)
            if not shared:
                dve.wait_ge(s["bias_in"], 32)

            def body(n, parity, k, i):
                if slot(n + 1):
                    dve.wait_ge(s["nT_ready"], n + 2)
                    need(dve, s["first_ready"], n)
                    p = 1 - parity
                    nc.vector.tensor_copy(n_high[p][:], nT_bank[:, 0:128]).then_inc(s["high_done"], 1)
                    dve.wait_ge(s["high_done"], n + 2)
                    nc.vector.tensor_tensor(n_low[p][:], nT_bank[:, 0:128], n_high[p][:].bitcast(F32), ALU.subtract).then_inc(s["split_ready"], 1)
                if slot(n):
                    if not shared:
                        own = dve.value_load(slot_expert[0:1, cols(n, 1)], min_val=0, max_val=E - 1)
                    dve.wait_ge(s["first_ready"], n + 1)
                    if shared:
                        dve.wait_ge(s["activated"], n + 1)
                        need(dve, s["hiddenT_ready"], n - 1)
                        nc.vector.scalar_tensor_tensor(hidden[parity][:, 0:F], first_bank[parity][0][:, F:2 * F], rows_in[k][:, D:D + 1],
                                                       act_out[parity][:, 0:F], ALU.mult, ALU.mult)
                        nc.vector.tensor_tensor(hidden[parity][:, F:2 * F], first_bank[parity][1][:, F:2 * F], act_out[parity][:, F:2 * F],
                                                ALU.mult).then_inc(s["hidden_ready"], 1)
                    else:
                        need(dve, s["hidden_ready"], n - 1)
                        nc.vector.tensor_tensor(act_out[parity][:], first_bank[parity][0][:, 0:F], bias1[:, cols(own * F, F)], ALU.add).then_inc(s["biased"], 1)
                if slot(n - 2):
                    if not shared:
                        own = dve.value_load(slot_expert[0:1, cols(n - 2, 1)], min_val=0, max_val=E - 1)
                    dve.wait_ge(s["y_ready"], n - 1)
                    need(dve, rows_stored[parity], 16 * (2 * i + k // 2 - 1))
                    if shared:
                        nc.vector.tensor_copy(result[parity][:], y_bank[:, 0:D]).then_inc(s["y_taken"], 1)
                    else:
                        nc.vector.tensor_tensor(result[parity][:], y_bank[:, 0:D], bias2[:, cols(own * D, D)], ALU.add).then_inc(s["y_taken"], 1)

            slots(dve, body)

        ctx_block.close()
        clear(nc, used)


def attention1(nc, t, x, const, ident, mod_col, mod_row, rows_at, back_at, counts, shifted, back, sent, got_in, sent_done, banks, weights):
    ctx = ExitStack()
    with ctx:
        def sb(name, columns, kind=F32, rows=128):
            return ctx.enter_context(nc.sbuf_tensor("c_" + name, [rows, columns], kind))

        used = []

        def sem(name):
            used.append(ctx.enter_context(nc.semaphore("c_" + name)))
            return used[-1]

        EXPERT_LOADS = 16 * 2 * E
        HID = 256
        raw_hidden, raw_qk = sb("raw_hidden", 2 * HID), sb("raw_qk", D)
        hid_high, hid_low = sb("hid_high", 2 * HID, F32R), sb("hid_low", 2 * HID, F32R)
        wqk_high, wqk_low = sb("wqk_high", D, F32R), sb("wqk_low", D, F32R)
        w_out, router = sb("w_out", HID), sb("router", E)
        first_row = sb("first_row", 128, F32R)
        bias_high, bias_low = sb("bias_high", HID, F32R), sb("bias_low", HID, F32R)
        v_bias, router_bias, ln_row = sb("v_bias", HID), sb("router_bias", E), sb("ln_row", 2 * D)
        raw_experts = [sb(f"raw_expert{n}", 512)[:] for n in range(E // 2)]
        GATE_B, QK_B, GAMMA, BETA, OUT_B = 0, 2, 3, 5, 7
        col = sb("col", 8)
        got, at = sb("got", 256), sb("at", 2, U32)
        mod_d, mod_h, mod_g, mod_f = sb("mod_d", D), sb("mod_h", 2 * D), sb("mod_g", D), sb("mod_f", 2 * D)
        stats, moments = sb("stats", 36), sb("moments", 12)
        var, neg_half, guess, square, rstd, offset = (sb(k, 6) for k in ("var", "neg_half", "guess", "square", "rstd", "offset"))
        out_bias = sb("out_bias", B)
        half_bits, guess_bits = sb("half_bits", 6, mybir.dt.int32), sb("guess_bits", 6, mybir.dt.int32)
        z_d, z_e, z_f, h, gh, normed_rows = (sb(k, 256) for k in ("z_d", "z_e", "z_f", "h", "gh", "normed_rows"))
        n_high, n_low = sb("n_high", 256, F32R), sb("n_low", 256, F32R)
        qk, q, k_ = sb("qk", 256), sb("q", 256), sb("k", 256)
        v, gate = sb("v", 512), sb("gate", 512)
        weighed, attn = sb("weighed", 384), sb("attn", 384)
        gated, yT = sb("gated", 512), sb("yT", 256)
        send, rT = sb("send", 256), sb("rT", 256)
        logits, top, top_at, hot, hot_b, expert = sb("logits", 16), sb("top", 16), sb("top_at", 16, U32), sb("hot", 16), sb("hot_b", 16, BF16), sb("expert", 2)
        place, picked, place_f, rows_now = sb("place", 16), sb("picked", 16), sb("place_f", 2), sb("rows_now", 2, U32)
        before_b, ones_b = sb("before_b", 128, BF16), sb("ones_b", 128, BF16)

        s = {n: sem(n) for n in """weights_in split_done setup_steps at_done x2_gated x2_done mod_d_in mod_h_in mod_g_in mod_f_in
            newton newton_steps z_d_done z_e_done z_f_done parts_d parts_e parts_f stats_d stats_e stats_f h_scaled h_done gh_done x_h_done
            n_scaled n_done nt_ready nT_high nT_split qk_ready qk_done q_k_done v_ready v_done gate_ready gate_done
            sim_ready weighed_done attn_done pv_ready gated_done y_ready yT_done yt_ready x3_done send_scaled send_done ht_ready rT_done
            lg_ready logits_done top_done top_at_done expert_done hot_done hot_ready rk_ready place_made rk_taken picked_done place_summed
            place_done experts_in experts_high experts_low passed_dve passed_pool""".split()}
        qk_bank, v_bank, gate_bank, sim_bank, pv_bank, y_bank, yt_bank, misc = banks
        BEHIND = 3

        def batches(engine, body):
            turns(engine, lambda n, _, __: body(n), B, 1, 4, BEHIND)

        ctx_block = ExitStack()
        block = ctx_block.enter_context(nc.Block())

        @block.sync
        def _(sp):
            loads = [(raw_hidden[:], t["L1_attn_W_hidden"]), (raw_qk[:], t["L1_attn_W_qk"]), (router[:], t["L1_ffn_Wr"]),
                     (w_out[:].rearrange("p (c n) -> p c n", n=D), t["L1_attn_W_out"].rearrange("(c p) n -> p c n", p=128)),
                     (v_bias[:], t["L1_attn_b_hidden"][0:HID].partition_broadcast(128)), (router_bias[:], t["L1_ffn_br"].partition_broadcast(128)),
                     (ln_row[:, 0:D], t["L1_attn_ln_g"].partition_broadcast(128)), (ln_row[:, D:2 * D], t["L1_attn_ln_b"].partition_broadcast(128)),
                     (col[:, QK_B:QK_B + 1], t["L1_attn_b_qk"].unsqueeze(1)), (col[:, OUT_B:OUT_B + 1], t["L1_attn_b_out"].unsqueeze(1))]
            for i in range(2):
                loads.append((col[:, GATE_B + i:GATE_B + i + 1], t["L1_attn_b_hidden"][HID + i * 128:HID + i * 128 + 128].unsqueeze(1)))
                loads.append((col[:, GAMMA + i:GAMMA + i + 1], t["L1_attn_os_gamma"][i].unsqueeze(1)))
                loads.append((col[:, BETA + i:BETA + i + 1], t["L1_attn_os_beta"][i].unsqueeze(1)))
            assert len(loads) == LOADS
            for to, source in loads:
                sp.dma_start(to, source, allow_slow_non_contiguous=True).then_inc(s["weights_in"], 16)

            assert load_experts(sp, t, 1, raw_experts, weights[2], s["experts_in"]) == EXPERT_LOADS

            def body(n):
                if real(n - 2):
                    need(sp, s["send_done"], n - 2)
                    sp.dma_start(mod_f[:], mod_row[1][cols(n - 2, 1), SB * D:5 * D].broadcast_to([128, 2 * D])).then_inc(s["mod_f_in"], 16)
                if real(n + 2):
                    need(sp, s["gh_done"], n + 2)
                    sp.dma_start(mod_g[:], mod_row[1][cols(n + 2, 1), GA * D:3 * D].broadcast_to([128, D])).then_inc(s["mod_g_in"], 16)
                if real(n + 3):
                    need(sp, s["h_done"], n + 3)
                    sp.dma_start(mod_h[:], mod_row[1][cols(n + 3, 1), 0:2 * D].broadcast_to([128, 2 * D])).then_inc(s["mod_h_in"], 16)
                if real(n + 4):
                    need(sp, s["x2_done"], n + 4)
                    sp.dma_start(mod_d[:], mod_row[0][cols(n + 4, 1), GB * D:6 * D].broadcast_to([128, D])).then_inc(s["mod_d_in"], 16)

            batches(sp, body)

        @block.tensor
        def _(pe):
            pe.wait_ge(s["weights_in"], 16 * LOADS)
            pe.wait_ge(s["split_done"], 1)

            def product(to, left, right, start=True):
                nc.tensor.matmul(to, left[0], right[0], start=start, stop=False)
                nc.tensor.matmul(to, left[0], right[1], start=False, stop=False)
                return nc.tensor.matmul(to, left[1], right[0], start=False, stop=True)

            def part(pair, a, size):
                return [m[:, a:a + size] for m in pair]

            def body(n):
                normed_, hid = (n_high, n_low), (hid_high, hid_low)
                if real(n):
                    pe.wait_ge(s["nT_split"], n + 1)
                    need(pe, s["qk_done"], n)
                    product(qk_bank[:, 0:256], part((wqk_high, wqk_low), 0, D), part(normed_, 0, 256)).then_inc(s["qk_ready"], 1)
                if real(n - 1):
                    pe.wait_ge(s["attn_done"], n)
                    pe.wait_ge(s["v_done"], n)
                    need(pe, s["gated_done"], n - 1)
                    for c in range(2):
                        nc.tensor.matmul(pv_bank[:, c * 256:c * 256 + 256], v[:, c * 128:c * 128 + 128], attn[:, 0:256], start=True, stop=False, skip_group_check=True)
                        done = nc.tensor.matmul(pv_bank[:, c * 256 + 128:c * 256 + 256], v[:, HID + c * 128:HID + c * 128 + 128], attn[:, 256:384],
                                                start=False, stop=True, skip_group_check=True)
                    done.then_inc(s["pv_ready"], 1)
                if real(n):
                    need(pe, s["v_done"], n)
                    for i in range(2):
                        to = v_bank[:, i * HID:(i + 1) * HID]
                        nc.tensor.matmul(to, first_row[:], bias_high[:], start=True, stop=False)
                        nc.tensor.matmul(to, first_row[:], bias_low[:], start=False, stop=False)
                        done = product(to, part(normed_, i * 128, 128), part(hid, 0, HID), start=False)
                    done.then_inc(s["v_ready"], 1)
                if real(n - 3):
                    pe.wait_ge(s["send_done"], n - 2)
                    pe.wait_ge(s["x3_done"], last(n - 2) + 1)
                    for i in range(2):
                        done = nc.tensor.transpose(yt_bank[:, i * 128:i * 128 + 128], send[:, i * 128:i * 128 + 128], ident)
                    done.then_inc(s["ht_ready"], 1)
                if real(n - 3):
                    pe.wait_ge(s["rT_done"], n - 2)
                    for i in range(2):
                        done = nc.tensor.matmul(yt_bank[:, i * E:(i + 1) * E], rT[:, i * 128:i * 128 + 128], router[:], start=True, stop=True)
                    done.then_inc(s["lg_ready"], 1)
                if real(n):
                    need(pe, s["gate_done"], n)
                    for c in range(2):
                        done = product(gate_bank[:, c * 256:c * 256 + 256], part(hid, HID + c * 128, 128), part(normed_, 0, 256))
                    done.then_inc(s["gate_ready"], 1)
                if real(n):
                    pe.wait_ge(s["q_k_done"], n + 1)
                    need(pe, s["weighed_done"], n)
                    nc.tensor.matmul(sim_bank[:, 0:256], k_[:, 0:128], q[:], start=True, stop=True)
                    nc.tensor.matmul(sim_bank[:, 256:384], k_[:, 128:256], q[:, 128:256], start=True, stop=True).then_inc(s["sim_ready"], 1)
                if real(n - 1):
                    pe.wait_ge(s["gated_done"], n)
                    need(pe, s["yT_done"], n - 1)
                    for c in range(2):
                        done = nc.tensor.matmul(y_bank[:, 0:256], w_out[:, c * D:(c + 1) * D], gated[:, c * 256:c * 256 + 256], start=c == 0, stop=c == 1)
                    done.then_inc(s["y_ready"], 1)
                if real(n - 3):
                    pe.wait_ge(s["hot_ready"], n - 2)
                    nc.tensor.matmul(yt_bank[:, 0:E], before_b[:], hot_b[:, 0:E], start=True, stop=True)
                    nc.tensor.matmul(yt_bank[:, E:2 * E], ones_b[:], hot_b[:, 0:E], start=True, stop=False)
                    nc.tensor.matmul(yt_bank[:, E:2 * E], before_b[:], hot_b[:, E:2 * E], start=False, stop=True)
                    nc.tensor.matmul(yt_bank[:, 2 * E:3 * E], ones_b[:], hot_b[:, 0:E], start=True, stop=False)
                    nc.tensor.matmul(yt_bank[:, 2 * E:3 * E], ones_b[:], hot_b[:, E:2 * E], start=False, stop=True).then_inc(s["rk_ready"], 1)
                if real(n + 1):
                    pe.wait_ge(s["n_done"], n + 2)
                    need(pe, s["nT_split"], n + 1)
                    for i in range(2):
                        done = nc.tensor.transpose(misc[:, i * 128:i * 128 + 128], normed_rows[:, i * 128:i * 128 + 128], ident)
                    done.then_inc(s["nt_ready"], 1)
                if real(n - 1):
                    pe.wait_ge(s["yT_done"], n)
                    need(pe, s["x3_done"], n - 1)
                    need(pe, s["rk_taken"], last(n - 3) + 1)
                    for i in range(2):
                        done = nc.tensor.transpose(yt_bank[:, i * 128:i * 128 + 128], yT[:, i * 128:i * 128 + 128], ident)
                    done.then_inc(s["yt_ready"], 1)

            batches(pe, body)

        @block.scalar
        def _(act):
            act.wait_ge(s["weights_in"], 16 * LOADS)
            split_experts_high(nc, act, raw_experts, weights[0], s["experts_in"], EXPERT_LOADS, s["experts_high"])

            def normed(k, kind, to, source):
                for i in range(2):
                    done = nc.scalar.activation(to[:, i * 128:i * 128 + 128], source[i], ACT.Identity, scale=rstd[:, 2 * k + i:2 * k + i + 1],
                                                bias=offset[:, 2 * k + i:2 * k + i + 1])
                done.then_inc(s[f"z_{kind}_done"], 1)

            def tiles_of_x(owner):
                return [x[:, cols(owner * 256 + i * 128, 128)] for i in range(2)]

            def body(n):
                turn = n + 4
                if real(n):
                    act.wait_ge(s["qk_ready"], n + 1)
                    need(act, s["q_k_done"], n)
                    nc.scalar.activation(qk[:], qk_bank[:, 0:256], ACT.Silu, bias=col[:, QK_B:QK_B + 1]).then_inc(s["qk_done"], 1)
                if real(n - 3):
                    act.wait_ge(s["ht_ready"], n - 2)
                    need(act, s["lg_ready"], n - 3)
                    nc.scalar.copy(rT[:], yt_bank[:, 0:256]).then_inc(s["rT_done"], 1)
                act.wait_ge(s["newton"], turn + 1)
                if real(n + 1):
                    need(act, s["n_scaled"], n + 1)
                    normed(1, "e", z_e, [h[:, i * 128:i * 128 + 128] for i in range(2)])
                if real(n + 2):
                    need(act, s["h_scaled"], n + 2)
                    normed(0, "d", z_d, tiles_of_x(n + 2))
                if real(n - 2):
                    need(act, s["send_scaled"], n - 2)
                    normed(2, "f", z_f, tiles_of_x(n - 2))
                if real(n):
                    act.wait_ge(s["v_ready"], n + 1)
                    need(act, s["pv_ready"], n)
                    nc.scalar.activation(v[:], v_bank[:], ACT.Silu).then_inc(s["v_done"], 1)
                    act.wait_ge(s["gate_ready"], n + 1)
                    need(act, s["gated_done"], n)
                    for c in range(2):
                        done = nc.scalar.activation(gate[:, c * 256:c * 256 + 256], gate_bank[:, c * 256:c * 256 + 256], ACT.Silu, bias=col[:, GATE_B + c:GATE_B + c + 1])
                    done.then_inc(s["gate_done"], 1)
                if real(n - 1):
                    act.wait_ge(s["y_ready"], n)
                    need(act, s["yt_ready"], n - 1)
                    nc.scalar.activation(yT[:], y_bank[:, 0:256], ACT.Identity, scale=mod_col[1][:, cols(GA * B + n - 1, 1)],
                                         bias=out_bias[:, cols(n - 1, 1)]).then_inc(s["yT_done"], 1)
                if real(n):
                    act.wait_ge(s["weighed_done"], n + 1)
                    need(act, s["pv_ready"], n)
                    nc.scalar.activation(attn[:], weighed[:], ACT.Square).then_inc(s["attn_done"], 1)
                if real(n + 1):
                    act.wait_ge(s["nt_ready"], n + 2)
                    need(act, s["gate_ready"], n + 1)
                    nc.scalar.copy(n_high[:], misc[:, 0:256]).then_inc(s["nT_high"], 1)

            batches(act, body)

        @block.vector
        def _(dve):
            steps = [0]

            def then(instruction):
                steps[0] += 1
                instruction.then_inc(s["setup_steps"], 1)
                dve.wait_ge(s["setup_steps"], steps[0])

            then(nc.vector.memset(moments[:], 1.0))
            nc.vector.tensor_copy(counts[:], const[:, C_REGION:C_REGION + E])
            nc.vector.tensor_copy(before_b[:], const[:, C_BEFORE:C_BEFORE + 128])
            nc.vector.tensor_copy(ones_b[:], const[:, C_ONES:C_ONES + 128])
            dve.wait_ge(s["weights_in"], 16 * LOADS)
            nc.vector.tensor_copy(first_row[:], const[:, C_FIRST:C_FIRST + 128])
            nc.vector.tensor_scalar(out_bias[:], mod_col[1][:, GA * B:(GA + 1) * B], col[:, OUT_B:OUT_B + 1], None, ALU.mult)
            for raw, high, low in ((raw_hidden, hid_high, hid_low), (raw_qk, wqk_high, wqk_low), (v_bias, bias_high, bias_low)):
                then(nc.vector.tensor_copy(high[:], raw[:]))
                then(nc.vector.tensor_tensor(low[:], raw[:], high[:].bitcast(F32), ALU.subtract))
            dve.sem_inc(s["split_done"], 1)

            def rows_of(owner):
                return x[:, cols(owner * 256, 256)]

            def statistics(k, kind, owner, source):
                for i in range(2):
                    done = nc.vector.bn_stats(stats[:, 12 * k + 6 * i:12 * k + 6 * i + 6], source[i])
                done.then_inc(s["parts_" + kind], 1)
                wait_apart(dve, s["parts_" + kind], owner + 1, s["passed_dve"])
                for i in range(2):
                    done = nc.vector.bn_aggr(moments[:, 4 * k + 2 * i:4 * k + 2 * i + 2], stats[:, 12 * k + 6 * i:12 * k + 6 * i + 6])
                done.then_inc(s["stats_" + kind], 1)

            def tiles_of_x(owner):
                return [x[:, cols(owner * 256 + i * 128, 128)] for i in range(2)]

            STEPS = 3 + 3 * NEWTON
            two = moments[:].rearrange("p (k two) -> p k two", two=2)

            def guess_step(turn, step):
                need(dve, s["newton_steps"], STEPS * turn + step)
                if step == 0:
                    done = nc.vector.tensor_scalar(var[:], two[:, :, 1], EPS, None, ALU.add)
                elif step == 1:
                    nc.vector.tensor_scalar(neg_half[:], var[:], -0.5, None, ALU.mult)
                    done = nc.vector.tensor_scalar(half_bits[:], var[:].bitcast(mybir.dt.int32), 1, None, ALU.logical_shift_right)
                else:
                    done = nc.vector.tensor_scalar(guess_bits[:], half_bits[:], -1.0, float(0x5F3759DF), ALU.mult, ALU.add)
                done.then_inc(s["newton_steps"], 1)

            def newton_step(turn, k, step):
                dve.wait_ge(s["newton_steps"], STEPS * turn + 3 * (k + 1) + step)
                now = guess[:] if k else guess_bits[:].bitcast(F32)
                if step == 0:
                    done = nc.vector.tensor_tensor(square[:], now, now, ALU.mult)
                elif step == 1:
                    done = nc.vector.tensor_tensor(square[:], square[:], neg_half[:], ALU.mult)
                else:
                    done = nc.vector.scalar_tensor_tensor(rstd[:] if k == NEWTON - 1 else guess[:], square[:], 1.5, now, ALU.add, ALU.mult)
                done.then_inc(s["newton_steps"], 1)

            def body(n):
                turn = n + 4
                need(dve, *((s["stats_f"], last(n - 2) + 1) if real(n - 2) else (s["stats_d"], last(n + 2) + 1)))
                for step in range(3):
                    guess_step(turn, step)
                newton_step(turn, 0, 0)
                newton_step(turn, 0, 1)
                newton_step(turn, 0, 2)
                newton_step(turn, 1, 0)
                if real(n):
                    dve.wait_ge(s["qk_done"], n + 1)
                    need(dve, s["sim_ready"], n)
                    nc.vector.tensor_scalar(q[:], qk[:], col[:, GAMMA:GAMMA + 1], col[:, BETA:BETA + 1], ALU.mult, ALU.add)
                newton_step(turn, 1, 1)
                if real(n):
                    nc.vector.tensor_scalar(k_[:], qk[:], col[:, GAMMA + 1:GAMMA + 2], col[:, BETA + 1:BETA + 2], ALU.mult, ALU.add).then_inc(s["q_k_done"], 1)
                newton_step(turn, 1, 2)
                newton_step(turn, 2, 0)
                newton_step(turn, 2, 1)
                need(dve, s["z_f_done"], min(n - 2, B) if isinstance(n, int) else n - 2)
                need(dve, s["z_e_done"], min(n + 1, B) if isinstance(n, int) else n + 1)
                need(dve, s["z_d_done"], min(n + 2, B) if isinstance(n, int) else n + 2)
                newton_step(turn, 2, 2)
                if real(n - 1):
                    dve.wait_ge(s["pv_ready"], n)
                    dve.wait_ge(s["gate_done"], n)
                    need(dve, s["y_ready"], n - 1)
                    nc.vector.tensor_tensor(gated[:, 0:256], pv_bank[:, 0:256], gate[:, 0:256], ALU.mult)
                dve.wait_ge(s["newton_steps"], STEPS * turn + STEPS)
                nc.vector.scalar_tensor_tensor(offset[:], two[:, :, 0], -1.0, rstd[:], ALU.mult, ALU.mult).then_inc(s["newton"], 1)
                if real(n - 1):
                    nc.vector.tensor_tensor(gated[:, 256:512], pv_bank[:, 256:512], gate[:, 256:512], ALU.mult).then_inc(s["gated_done"], 1)
                if real(n + 1):
                    dve.wait_ge(s["gh_done"], n + 2)
                    nc.vector.tensor_tensor(rows_of(n + 1), rows_of(n + 1), gh[:], ALU.add).then_inc(s["x_h_done"], 1)
                if real(n - 3):
                    dve.wait_ge(s["lg_ready"], n - 2)
                    nc.vector.tensor_tensor(logits[:].rearrange("p (i e) -> p i e", e=8), yt_bank[:, 0:16].rearrange("p (i e) -> p i e", e=8),
                                            router_bias[:].unsqueeze(1).broadcast_to([128, 2, 8]), ALU.add).then_inc(s["logits_done"], 1)
                    wait_apart(dve, s["logits_done"], n - 2, s["passed_dve"])
                    for i in range(2):
                        done = nc.vector.max(top[:, i * 8:i * 8 + 8], logits[:, i * 8:i * 8 + 8])
                    done.then_inc(s["top_done"], 1)
                if real(n):
                    dve.wait_ge(s["sim_ready"], n + 1)
                    need(dve, s["attn_done"], n)
                    nc.vector.scalar_tensor_tensor(weighed[:], sim_bank[:, 0:384], 0.0, const[:, C_CAUSAL:C_CAUSAL + 384], ALU.max, ALU.mult).then_inc(s["weighed_done"], 1)
                if real(n - 3):
                    wait_apart(dve, s["top_done"], n - 2, s["passed_dve"])
                    for i in range(2):
                        nc.vector.max_index(top_at[:, i * 8:i * 8 + 8], top[:, i * 8:i * 8 + 8], logits[:, i * 8:i * 8 + 8])
                    for i in range(2):
                        done = nc.vector.tensor_scalar(shifted[:, cols((2 * (n - 3) + i) * E, E)], logits[:, i * 8:i * 8 + 8], top[:, i * 8:i * 8 + 1], None, ALU.subtract)
                    done.then_inc(s["top_at_done"], 1)
                    dve.wait_ge(s["top_at_done"], n - 2)
                    nc.vector.tensor_copy(expert[:], top_at[:].rearrange("p (i e) -> p i e", e=8)[:, :, 0]).then_inc(s["expert_done"], 1)
                    dve.wait_ge(s["expert_done"], n - 2)
                    for i in range(2):
                        done = nc.vector.tensor_scalar(hot[:, i * 8:i * 8 + 8], const[:, C_INDEX:C_INDEX + E], expert[:, i:i + 1], None, ALU.is_equal)
                    done.then_inc(s["hot_done"], 1)
                    dve.wait_ge(s["hot_done"], n - 2)
                    need(dve, s["rk_ready"], n - 3)
                    nc.vector.tensor_copy(hot_b[:], hot[:]).then_inc(s["hot_ready"], 1)
                if real(n + 3):
                    dve.wait_ge(got_in, 32 * (n + 4))
                    dve.wait_ge(s["mod_d_in"], 16 * (n + 4))
                    rows = got[:].rearrange("p (i d) -> p i d", d=D)
                    nc.vector.tensor_tensor(rows, rows, mod_d[:].unsqueeze(1).broadcast_to([128, 2, D]), ALU.mult).then_inc(s["x2_gated"], 1)
                if real(n + 2):
                    dve.wait_ge(s["h_done"], n + 3)
                    statistics(1, "e", n + 2, [h[:, i * 128:i * 128 + 128] for i in range(2)])
                if real(n - 3):
                    dve.wait_ge(s["rk_ready"], n - 2)
                    nc.vector.tensor_tensor(place[:].rearrange("p (i e) -> p i e", e=8), yt_bank[:, 0:16].rearrange("p (i e) -> p i e", e=8),
                                            counts[:].unsqueeze(1).broadcast_to([128, 2, 8]), ALU.add).then_inc(s["place_made"], 1)
                    dve.wait_ge(s["place_made"], n - 2)
                    nc.vector.tensor_tensor(counts[:], yt_bank[:, 16:24], counts[:], ALU.add).then_inc(s["rk_taken"], 1)
                    nc.vector.tensor_tensor(picked[:], place[:], hot[:], ALU.mult).then_inc(s["picked_done"], 1)
                    dve.wait_ge(s["picked_done"], n - 2)
                    nc.vector.tensor_reduce(place_f[:], picked[:].rearrange("p (i e) -> p i e", e=8), AX.X, ALU.add).then_inc(s["place_summed"], 1)
                    dve.wait_ge(s["place_summed"], n - 2)
                    need(dve, sent_done, 32 * (n - 3))
                    nc.vector.tensor_copy(rows_at[:, cols(2 * (n - 3), 2)], place_f[:])
                    nc.vector.tensor_copy(rows_now[:], place_f[:]).then_inc(s["place_done"], 1)
                if real(n - 1):
                    dve.wait_ge(s["yt_ready"], n)
                    dve.wait_ge(s["x_h_done"], n)
                    nc.vector.tensor_tensor(rows_of(n - 1), yt_bank[:, 0:256], rows_of(n - 1), ALU.add).then_inc(s["x3_done"], 1)
                if real(n + 3):
                    dve.wait_ge(s["x2_gated"], n + 4)
                    nc.vector.tensor_tensor(rows_of(n + 3), got[:], rows_of(n + 3), ALU.add).then_inc(s["x2_done"], 1)
                if real(n + 1):
                    dve.wait_ge(s["nT_high"], n + 2)
                    nc.vector.tensor_tensor(n_low[:], misc[:, 0:256], n_high[:].bitcast(F32), ALU.subtract).then_inc(s["nT_split"], 1)
                if real(n + 3):
                    wait_apart(dve, s["x2_done"], n + 4, s["passed_dve"])
                    statistics(0, "d", n + 3, tiles_of_x(n + 3))
                if real(n + 4):
                    nc.vector.tensor_copy(at[:], back_at[:, cols(2 * (n + 4), 2)]).then_inc(s["at_done"], 1)
                if real(n - 1):
                    wait_apart(dve, s["x3_done"], n, s["passed_dve"])
                    statistics(2, "f", n - 1, tiles_of_x(n - 1))

            batches(dve, body)

        @block.gpsimd
        def _(pool):
            def over_tiles(row):
                return row.unsqueeze(1).broadcast_to([128, 2, D])

            def tiles(buffer):
                return buffer.rearrange("p (i d) -> p i d", d=D)

            def affine(source, scale, shift, to, scaled, done, count):
                nc.gpsimd.tensor_tensor(tiles(to), tiles(source), over_tiles(scale), ALU.mult).then_inc(s[scaled], 1)
                pool.wait_ge(s[scaled], count)
                nc.gpsimd.tensor_tensor(tiles(to), tiles(to), over_tiles(shift), ALU.add).then_inc(s[done], 1)

            def body(n):
                if real(n + 3):
                    pool.wait_ge(s["at_done"], n + 4)
                    wait_apart(pool, s["x2_done"], n + 3, s["passed_pool"])
                    for i in range(2):
                        nc.gpsimd.indirect_dma_start(got[:, i * D:(i + 1) * D], None, back, bass.IndirectOffsetOnAxis(ap=at[:, i:i + 1], axis=0)).then_inc(got_in, 16)
                if real(n - 3):
                    pool.wait_ge(s["z_f_done"], n - 2)
                    pool.wait_ge(s["mod_f_in"], 16 * (n - 2))
                    need(pool, sent_done, 32 * (n - 3))
                    need(pool, s["ht_ready"], n - 3)
                    affine(z_f[:], mod_f[:, D:2 * D], mod_f[:, 0:D], send[:], "send_scaled", "send_done", n - 2)
                if real(n + 1):
                    pool.wait_ge(s["h_done"], n + 2)
                    pool.wait_ge(s["mod_g_in"], 16 * (n + 2))
                    need(pool, s["x_h_done"], n + 1)
                    nc.gpsimd.tensor_tensor(tiles(gh[:]), tiles(h[:]), over_tiles(mod_g[:]), ALU.mult).then_inc(s["gh_done"], 1)
                if real(n + 2):
                    pool.wait_ge(s["z_d_done"], n + 3)
                    pool.wait_ge(s["mod_h_in"], 16 * (n + 3))
                    need(pool, s["z_e_done"], n + 2)
                    need(pool, s["gh_done"], last(n + 1) + 1)
                    affine(z_d[:], mod_h[:, CA * D:(CA + 1) * D], mod_h[:, SA * D:(SA + 1) * D], h[:], "h_scaled", "h_done", n + 3)
                if real(n + 1):
                    pool.wait_ge(s["z_e_done"], n + 2)
                    need(pool, s["nt_ready"], n + 1)
                    affine(z_e[:], ln_row[:, 0:D], ln_row[:, D:2 * D], normed_rows[:], "n_scaled", "n_done", n + 2)
                if real(n - 3):
                    wait_apart(pool, s["place_done"], n - 2, s["passed_pool"])
                    for i in range(2):
                        nc.gpsimd.indirect_dma_start(sent, bass.IndirectOffsetOnAxis(ap=rows_now[:, i:i + 1], axis=0), send[:, i * D:(i + 1) * D], None).then_inc(sent_done, 16)

            split_experts_low(nc, pool, raw_experts, weights[0], weights[1], s["experts_high"], s["experts_low"])
            batches(pool, body)
            pool.wait_ge(sent_done, 32 * B)

        ctx_block.close()
        clear(nc, used)


def combine(nc, out, x, mod_row, rows_at, back, shifted, got_in):
    ctx = ExitStack()
    with ctx:
        def sb(name, columns, kind=F32, rows=128):
            return ctx.enter_context(nc.sbuf_tensor("f_" + name, [rows, columns], kind))

        def sem(name):
            return ctx.enter_context(nc.semaphore("f_" + name))

        weight, exped, total = sb("weight", TILES), sb("exped", TILES * E), sb("total", TILES)
        got = [sb(f"got{n}", 2 * D) for n in range(2)]
        gate = [sb(f"gate{n}", D) for n in range(2)]
        result = [sb(f"result{n}", 2 * D) for n in range(2)]
        at = [sb(f"at{n}", 2, U32) for n in range(2)]
        s = {n: sem(n) for n in "passed at_done weighted result_done exp_done summed weight_done".split()}
        gate_in = [sem(f"gate_in{n}") for n in range(2)]
        stored = [sem(f"stored{n}") for n in range(2)]
        out_rows = out.rearrange("b (i p) d -> b p i d", p=128)
        block = ctx.enter_context(nc.Block())

        def batches(engine, body):
            turns(engine, body, B, 2, 2, 2)

        @block.sync
        def _(sp):
            def body(n, parity, half):
                if real(n + 1):
                    owner = half + parity
                    need(sp, s["result_done"], n)
                    sp.dma_start(gate[1 - parity][:], mod_row[cols(n + 1, 1), GB * D:6 * D].broadcast_to([128, D])).then_inc(gate_in[1 - parity], 16)

            batches(sp, body)

        @block.gpsimd
        def _(pool):
            def body(n, parity, half):
                if real(n + 1):
                    pool.wait_ge(s["at_done"], n + 2)
                    wait_apart(pool, s["result_done"], n, s["passed"])
                    for i in range(2):
                        nc.gpsimd.indirect_dma_start(got[1 - parity][:, i * D:(i + 1) * D], None, back,
                                                     bass.IndirectOffsetOnAxis(ap=at[1 - parity][:, i:i + 1], axis=0)).then_inc(got_in[1 - parity], 16)

            batches(pool, body)

        @block.vector
        def _(dve):
            def body(n, parity, half):
                if real(n):
                    dve.wait_ge(got_in[parity], 32 * (half + 1))
                    dve.wait_ge(gate_in[parity], 16 * (half + 1))
                    for i in range(2):
                        mine = got[parity][:, i * D:(i + 1) * D]
                        done = nc.vector.scalar_tensor_tensor(mine, mine, weight[:, cols(2 * n + i, 1)], gate[parity][:], ALU.mult, ALU.mult)
                    done.then_inc(s["weighted"], 1)
                    dve.wait_ge(s["weighted"], n + 1)
                    need(dve, stored[parity], 16 * half)
                    nc.vector.tensor_tensor(result[parity][:], got[parity][:], x[:, cols(n * 256, 256)], ALU.add).then_inc(s["result_done"], 1)
                if real(n + 2):
                    nc.vector.tensor_copy(at[parity][:], rows_at[:, cols(2 * (n + 2), 2)]).then_inc(s["at_done"], 1)

            dve.wait_ge(s["exp_done"], 1)
            nc.vector.tensor_reduce(total[:], exped[:].rearrange("p (t e) -> p t e", e=E), AX.X, ALU.add).then_inc(s["summed"], 1)
            dve.wait_ge(s["summed"], 1)
            nc.vector.reciprocal(weight[:], total[:]).then_inc(s["weight_done"], 1)
            dve.wait_ge(s["weight_done"], 1)
            batches(dve, body)

        @block.scalar
        def _(act):
            nc.scalar.activation(exped[:], shifted[:], ACT.Exp).then_inc(s["exp_done"], 1)

            def body(n, parity, half):
                if real(n):
                    act.wait_ge(s["result_done"], n + 1)
                    act.dma_start(out_rows[cols(n, 1)].squeeze(0), result[parity][:].rearrange("p (i d) -> p i d", d=D)).then_inc(stored[parity], 16)

            batches(act, body)
            for parity in range(2):
                act.wait_ge(stored[parity], 16 * (B // 2))


INPUTS = ["L0_attn_x", "L0_attn_Wqkv", "L0_attn_Wout", "L0_ffn_ln_w", "L0_ffn_ln_b", "L0_ffn_router_w", "L0_ffn_gate_w", "L0_ffn_up_w",
          "L0_ffn_down_w", "L0_ffn_sh_gate", "L0_ffn_sh_up", "L0_ffn_sh_down", "L0_wmod", "L1_attn_ln_g", "L1_attn_ln_b", "L1_attn_W_hidden",
          "L1_attn_b_hidden", "L1_attn_W_qk", "L1_attn_b_qk", "L1_attn_os_gamma", "L1_attn_os_beta", "L1_attn_W_out", "L1_attn_b_out",
          "L1_ffn_Wr", "L1_ffn_br", "L1_ffn_W1", "L1_ffn_b1", "L1_ffn_W2", "L1_ffn_b2", "L1_wmod"]


def kernel(**inputs):
    import numpy as np
    import concourse.bacc as bacc
    from concourse import mybir as m
    from concourse.bass_utils import run_bass_kernel_spmd as run

    nc = bacc.Bacc("TRN2", target_bir_lowering=False, num_devices=1)
    arrays = {name: np.ascontiguousarray(inputs[name]) for name in INPUTS}
    arrays["c0T"] = np.ascontiguousarray(np.asarray(inputs["L0_c"]).T)
    arrays["c1T"] = np.ascontiguousarray(np.asarray(inputs["L1_c"]).T)
    arrays["consts"] = constants()
    t = {name: nc.dram_tensor("in_" + name, a.shape, m.dt.from_np(a.dtype), kind="ExternalInput").ap() for name, a in arrays.items()}
    out = nc.dram_tensor("out", [B, S, D], F32, kind="ExternalOutput").ap()
    program(nc, t, out)
    r = run(nc, [{"in_" + name: a for name, a in arrays.items()}], core_ids=[0])
    return r.results[0]["out"]
```

```python
from contextlib import ExitStack

import concourse.bass as bass
import concourse.mybir as mybir
from concourse.alu_op_type import AluOpType as ALU

F32 = mybir.dt.float32
F32R = mybir.dt.float32r
BF16 = mybir.dt.bfloat16
U32 = mybir.dt.uint32
ACT = mybir.ActivationFunctionType
AX = mybir.AxisListType

B, S, D = 32, 256, 128
TILES = B * S // 128
HEADS, DH = 16, 64
E, F = 8, 256
EPS = 1e-5
GATE_MIN = 0.25
MASKED = -1e30
CAP = B * S + 128
SLOTS = TILES + E
SENT = 132
SCORE, TOKEN = 128, 129
NOWHERE = 2 * E
NEWTON = 3
LOADS = 16
SA, CA, GA, SB, CB, GB = range(6)

C_IDENT, C_WINDOW, C_BEFORE, C_ONES, C_REGION, C_INDEX, C_CAUSAL, C_SLOT, C_ROW, C_EPS, C_FIRST = 0, 128, 384, 512, 640, 648, 656, 1040, 1120, 1121, 1128
C_ALL = 1256


def constants():
    import numpy as np
    c = np.zeros((128, C_ALL), np.float32)
    p, j = np.arange(128)[:, None], np.arange(128)[None, :]
    c[:, C_IDENT:C_IDENT + 128] = p == j
    first = (j <= p) & (j >= p - 63)
    r = p % 64
    second = (j >= r + 1) & (j <= r + 64)
    c[:, C_WINDOW:C_WINDOW + 128] = np.where(first, 0, MASKED)
    c[:, C_WINDOW + 128:C_WINDOW + 256] = np.where(second, 0, MASKED)
    c[:, C_BEFORE:C_BEFORE + 128] = p < j
    c[:, C_ONES:C_ONES + 128] = 1
    c[:, C_REGION:C_REGION + E] = np.arange(E) * CAP
    c[:, C_INDEX:C_INDEX + E] = np.arange(E)
    i = np.arange(256)[None, :]
    c[:, C_CAUSAL:C_CAUSAL + 256] = (i >= p) / (i + 1.0)
    c[:, C_CAUSAL + 256:C_CAUSAL + 384] = (j >= p) / (j + 129.0)
    c[:, C_SLOT:C_SLOT + TILES + NOWHERE] = np.arange(TILES + NOWHERE)
    c[:, C_ROW] = np.arange(128)
    c[:, C_EPS] = EPS
    c[0, C_FIRST:C_FIRST + 128] = 1
    return c


def need(engine, semaphore, value):
    if not (isinstance(value, int) and value <= 0):
        engine.wait_ge(semaphore, value)


def wait_apart(engine, semaphore, value, passed):
    if not (isinstance(value, int) and value <= 0):
        engine.wait_ge(semaphore, value)
        engine.sem_inc(passed, 1)


def last(owner):
    return min(owner, B - 1) if isinstance(owner, int) else owner


def real(owner, count=B):
    return not isinstance(owner, int) or 0 <= owner < count


def turns(engine, body, count=B, unroll=1, ahead=1, behind=2):
    start = -(-(behind + 1) // unroll) * unroll
    end = (count - ahead) // unroll * unroll
    for n in range(-ahead, start):
        body(n, n % unroll, n // unroll)
    with engine.Fori(start // unroll, end // unroll) as i:
        for k in range(unroll):
            body(unroll * i + k, k, i)
    for n in range(end, count + behind):
        body(n, n % unroll, n // unroll)


def clear(nc, semaphores):
    with nc.Block() as block:
        @block.gpsimd
        def _(pool):
            for semaphore in semaphores[0::4]:
                pool.sem_clear(semaphore)

        @block.sync
        def _(sp):
            for semaphore in semaphores[1::4]:
                sp.sem_clear(semaphore)

        @block.scalar
        def _(act):
            for semaphore in semaphores[2::4]:
                act.sem_clear(semaphore)

        @block.vector
        def _(dve):
            for semaphore in semaphores[3::4]:
                dve.sem_clear(semaphore)


def cols(start, size):
    return bass.ds(start, size)


def program(nc, t, out):
    ctx = ExitStack()
    with ctx:
        def sb(name, columns, kind=F32, rows=128):
            return ctx.enter_context(nc.sbuf_tensor(name, [rows, columns], kind))

        def sem(name):
            return ctx.enter_context(nc.semaphore(name))

        sent_done = [sem(f"sent_done{n}") for n in range(2)]
        returned = [[sem(f"returned{n}_{k}") for k in range(4)] for n in range(2)]

        x = sb("x", TILES * D)
        const = sb("const", C_ALL)
        ident = const[:, C_IDENT:C_IDENT + 128]
        mod_col = [sb(f"mod_col{n}", 6 * B) for n in range(2)]
        token = sb("token", TILES + NOWHERE, U32)
        blank = sb("blank", E * SENT)
        shifted = sb("shifted", TILES * E)
        counts = [sb(f"counts{n}", E) for n in range(2)]
        mod_row = [nc.dram_tensor(f"mod_row{n}", [B, 6 * D], F32, kind="Internal").ap() for n in range(2)]
        sent = [nc.dram_tensor(f"sent{n}", [(E + 1) * CAP, SENT], F32, kind="Internal").ap() for n in range(2)]
        back = [nc.dram_tensor(f"back{n}", [(TILES + NOWHERE) * 128, D], F32, kind="Internal").ap() for n in range(2)]
        banks = [ctx.enter_context(nc.psum_tensor(f"bank{n}", [128, 512], F32)) for n in range(8)]

        UP = (E + 1) * 2 * F
        weights = sb("up_high", UP, F32R), sb("up_low", UP, F32R), sb("down", (E + 1) * F)

        setup_and_attention0(nc, t, x, const, ident, mod_col, token, blank, counts, mod_row, sent, sent_done[0], banks, weights)
        experts(nc, t, 0, counts[0], blank, sent[0], back[0], returned[0], banks, const, ident, weights)
        attention1(nc, t, x, const, ident, mod_col, mod_row, token, counts[1], shifted, back[0], sent[1], sent_done[1], banks, weights)
        experts(nc, t, 1, counts[1], blank, sent[1], back[1], returned[1], banks, const, ident, weights)
        combine(nc, out, x, mod_row[1], back[1], shifted)


def setup_and_attention0(nc, t, x, const, ident, mod_col, token, blank, counts, mod_row, sent, sent_done, banks, weights):
    ctx = ExitStack()
    with ctx:
        def sb(name, columns, kind=F32, rows=128):
            return ctx.enter_context(nc.sbuf_tensor(name, [rows, columns], kind))

        used = []

        def sem(name):
            used.append(ctx.enter_context(nc.semaphore(name)))
            return used[-1]

        WQKV = 3 * HEADS * DH
        EXPERT_LOADS = 16 * 3 * (E + 1)
        w_high, w_low = sb("w_high", WQKV, F32R), sb("w_low", WQKV, F32R)
        w_out = sb("w_out", HEADS * DH)
        router = sb("router", E)
        c_col = [sb(f"c_col{n}", B) for n in range(2)]
        w_mod = [sb(f"w_mod{n}", 6 * D) for n in range(2)]
        mod_stage = [sb(f"mod_stage{n}", 6 * D, rows=B) for n in range(2)]
        mod_tmp, mod_tmp_pool = sb("mod_tmp", 4 * B), sb("mod_tmp_pool", 4 * D)
        ident_b, window_b, before_b, ones_b = sb("ident_b", 128, BF16), sb("window_b", 256, BF16), sb("before_b", 128, BF16), sb("ones_b", 128, BF16)
        ln_row = sb("ln_row", 2 * D)
        hT = sb("hT", 256)
        h_high, h_low = sb("h_high", 256, F32R), sb("h_low", 256, F32R)
        qk = [sb(f"qk{n}", 1024) for n in range(2)]
        v = [sb(f"v{n}", 768) for n in range(4)]
        probs = [sb(f"probs{n}", 1024) for n in range(2)]
        probsT = [sb(f"probsT{n}", 1024) for n in range(2)]
        neg_max, sums, inverse = sb("neg_max", 16), sb("sums", 16), sb("inverse", 16)
        attn = sb("attn", 8 * 256)
        raw_experts = [w_mod[n][:, 0:512] for n in range(2)] + [sb(f"raw_expert{n}", 512)[:] for n in range(E - 1)]
        yT = sb("yT", 256)
        stats, moments = sb("stats", 3 * 12), sb("moments", 3 * 4)
        log_var, rstd = sb("log_var", 3 * 2), sb("rstd", 3 * 2)
        z_a, z_b, z_c, h_b, g_b = (sb(n, 256) for n in ("z_a", "z_b", "z_c", "h_b", "g_b"))
        mod_b = sb("mod_b", 3 * D)
        send = sb("send", 2 * SENT)
        nT = sb("nT", 256)
        logits, top, top_at, hot, hot_b = sb("logits", 16), sb("top", 16), sb("top_at", 16, U32), sb("hot", 16), sb("hot_b", 16, BF16)
        expert = sb("expert", 2)
        low_top, exp_top = sb("low_top", 2), sb("exp_top", 2)
        place, picked, place_f = sb("place", 16), sb("picked", 16), sb("place_f", 2)
        rows_now = sb("rows_now", 2, U32)

        names = """token_made blank_made blank_sent experts_in experts_high passed_dve passed_pool consts_in small_in
            weights_in x_first_in x_in mod_sent c_silu qkv_high mod_in mod_made mod_copied pool_steps mod_rows_made
            split_done consts_cast scores_ready negmax_ready exp_done inverse_ready norm_done pt_ready pt_taken
            qk0_ready qk1_ready v_ready qk0_taken qk1_taken v_taken attn_ready attn_taken y_ready y_taken yt_ready
            yt_taken zt_ready zt_taken split_ready nt_ready nt_taken lg_ready lg_taken log_a log_b log_c parts_a
            parts_b parts_c setup_steps high_done top_done top_at_done low_top_done expert_done hot_done place_made
            picked_done place_summed score_steps scaled_b scaled_c gated_b hot_ready rk_ready rk_taken stats_a
            stats_b stats_c rstd_a rstd_b rstd_c z_a_done z_b_done z_c_done h_b_done x_b_done send_done mod_b_in
            exp_top_done score_done place_done""".split()
        s = {n: sem("a_" + n) for n in names}
        v_shifted = [sem(f"a_v_shifted{n}") for n in range(4)]
        scores_bank, pt_bank, proj_bank = banks[0:2], banks[2:4], banks[4:6]
        attn_bank, misc = banks[6], banks[7]

        ctx_block = ExitStack()
        block = ctx_block.enter_context(nc.Block())

        @block.sync
        def _(sp):
            sp.dma_start(const[:], t["consts"]).then_inc(s["consts_in"], 16)
            for n in range(2):
                sp.dma_start(c_col[n][:], t[f"c{n}T"]).then_inc(s["mod_in"], 16)
                sp.dma_start(w_mod[n][:], t[f"L{n}_wmod"]).then_inc(s["mod_in"], 16)
            sp.dma_start(router[:], t["L0_ffn_router_w"]).then_inc(s["small_in"], 16)
            for n, name in enumerate(("L0_ffn_ln_w", "L0_ffn_ln_b")):
                sp.dma_start(ln_row[:, n * D:(n + 1) * D], t[name].partition_broadcast(128)).then_inc(s["small_in"], 16)
            for n in range(3):
                for half in range(2):
                    sp.dma_start((probs, probsT, qk)[n][half][:, 0:512], t["L0_attn_Wqkv"][:, n * 1024 + half * 512:n * 1024 + half * 512 + 512]).then_inc(s["weights_in"], 16)
            x_dram = t["L0_attn_x"].rearrange("b (i p) d -> p (b i) d", p=128)
            x_view = x[:].rearrange("p (n d) -> p n d", d=D)
            sp.dma_start(x_view[:, 0:16], x_dram[:, 0:16]).then_inc(s["x_first_in"], 16)
            sp.dma_start(w_out[:].rearrange("p (c n) -> p c n", n=D), t["L0_attn_Wout"].rearrange("(c p) n -> p c n", p=128)).then_inc(s["small_in"], 16)
            for n in range(1, 4):
                sp.dma_start(x_view[:, n * 16:(n + 1) * 16], x_dram[:, n * 16:(n + 1) * 16]).then_inc(s["x_in"], 16)
            sp.wait_ge(s["blank_made"], 1)
            for n in range(2):
                sp.dma_start(sent[n][E * CAP:E * CAP + E * 128, :].rearrange("(n p) w -> p n w", p=128),
                             blank[:].rearrange("p (n w) -> p n w", w=SENT)).then_inc(s["blank_sent"], 16)
            sp.wait_ge(s["mod_made"], 2)
            loads = load_experts(sp, t, 0, raw_experts, weights[2], s["experts_in"])
            assert loads == EXPERT_LOADS
            for n in range(2):
                sp.wait_ge(s["mod_rows_made"], n + 1)
                sp.dma_start(mod_row[n], mod_stage[n][:]).then_inc(s["mod_sent"], 16)
            sp.wait_ge(s["mod_sent"], 32)

            def body(b, _, __):
                for step in range(4):
                    g = 4 * b + step
                    if step == 0 and real(b - 1):
                        need(sp, s["x_b_done"], b - 1)
                        sp.dma_start(mod_b[:], mod_row[0][cols(b - 1, 1), SB * D:6 * D].broadcast_to([128, 3 * D])).then_inc(s["mod_b_in"], 16)
                    if real(b + 1 if step == 3 else b):
                        n = (step + 1) % 4
                        sp.wait_ge(s["v_taken"], g + 2)
                        sp.dma_start(v[n][0:64, 512:768], v[n][64:128, 0:256]).then_inc(v_shifted[n], 16)
                        sp.dma_start(v[n][64:128, 512:768], v[n][0:64, 256:512]).then_inc(v_shifted[n], 16)

            turns(sp, body)

        @block.tensor
        def _(pe):
            pe.wait_ge(s["mod_in"], 64)
            pe.wait_ge(s["c_silu"], 2)
            for n in range(2):
                for j in range(6):
                    nc.tensor.matmul(banks[4 + n][:, j * B:(j + 1) * B], w_mod[n][:, j * D:(j + 1) * D], c_col[n][:], start=True, stop=True)
                nc.tensor.matmul(banks[2 * n][0:B, 0:384], c_col[n][:], w_mod[n][:, 0:384], start=True, stop=True)
                nc.tensor.matmul(banks[2 * n + 1][0:B, 0:384], c_col[n][:], w_mod[n][:, 384:768], start=True, stop=True).then_inc(s["mod_made"], 1)
            pe.wait_ge(s["consts_cast"], 1)
            pe.wait_ge(s["mod_copied"], 6)
            pe.wait_ge(s["small_in"], 64)
            pe.wait_ge(s["split_done"], 1)

            def window(g, step, parity):
                need(pe, s["exp_done"], 2 * (g - 1) + parity + 1)
                bank, rows = scores_bank[parity], slice(64 * parity, 64 * parity + 64)
                nc.tensor.matmul(bank[:].rearrange("p (j w) -> p j w", j=2), ident_b[:], window_b[:].unsqueeze(1).broadcast_to([128, 2, 256]), start=True, stop=False, skip_group_check=True)
                for j in range(2):
                    q, k = qk[step % 2][rows, j * 512:j * 512 + 256], qk[step % 2][rows, j * 512 + 256:j * 512 + 512]
                    at = bank[:, j * 256:j * 256 + 256]
                    nc.tensor.matmul(at[:, 0:128], q[:, 0:128], k[:, 0:128], start=False, stop=True, skip_group_check=True)
                    nc.tensor.matmul(at[0:64, 128:256], q[:, 128:192], k[:, 64:192], start=False, stop=True, skip_group_check=True)
                    done = nc.tensor.matmul(at[64:128, 128:256], q[:, 192:256], k[:, 128:256], start=False, stop=True, skip_group_check=True)
                done.then_inc(s["scores_ready"], 1)

            def transpose_probs(g, step, parity):
                need(pe, s["norm_done"], 2 * g + parity + 1)
                need(pe, s["pt_taken"], 2 * (g - 1) + parity + 1)
                for n in range(4):
                    at = parity * 512 + n * 128
                    done = nc.tensor.transpose(pt_bank[parity][:, n * 128:n * 128 + 128], probs[step % 2][:, at:at + 128], ident)
                done.then_inc(s["pt_ready"], 1)

            def project(bank, parts):
                for n, (left_high, left_low, right_high, right_low, at) in enumerate(parts):
                    nc.tensor.matmul(at, left_high, right_high, start=True, stop=False)
                    nc.tensor.matmul(at, left_high, right_low, start=False, stop=False)
                    done = nc.tensor.matmul(at, left_low, right_high, start=False, stop=True)
                return done

            def project_qk(g, step, pair):
                n = (3 * step + pair) % 2
                need(pe, s["v_taken" if pair else "qk1_taken"], g)
                parts = []
                for i in range(2):
                    c = i * HEADS * DH + (2 * step + pair) * 128
                    parts.append((w_high[:, c:c + 128], w_low[:, c:c + 128], h_high[:], h_low[:], proj_bank[n][:, i * 256:i * 256 + 256]))
                project(proj_bank[n], parts).then_inc(s["qk1_ready" if pair else "qk0_ready"], 1)

            def project_v(g, step):
                n = (3 * step + 2) % 2
                need(pe, s["qk0_taken"], g + 1)
                c = 2 * HEADS * DH + step * 256
                parts = [(h_high[:, i * 128:i * 128 + 128], h_low[:, i * 128:i * 128 + 128], w_high[:, c:c + 256], w_low[:, c:c + 256], proj_bank[n][:, i * 256:i * 256 + 256]) for i in range(2)]
                project(proj_bank[n], parts).then_inc(s["v_ready"], 1)

            def apply_probs(g, step, owner):
                pe.wait_ge(s["pt_taken"], 2 * g + 2)
                pe.wait_ge(v_shifted[step], 32 * (owner + 1))
                need(pe, s["attn_taken"], g)
                for j in range(2):
                    for parity in range(2):
                        rows = slice(64 * parity, 64 * parity + 64)
                        head = (2 * j + parity) * DH
                        p = probsT[step % 2][:, parity * 512 + j * 256:parity * 512 + j * 256 + 256]
                        for value, a, e in ((0, 0, 128), (2, 128, 192), (1, 192, 256)):
                            done = nc.tensor.matmul(attn_bank[rows, j * 256 + a:j * 256 + e], v[step % 4][:, value * 256 + head:value * 256 + head + DH], p[:, a:e], start=True, stop=True, skip_group_check=True)
                done.then_inc(s["attn_ready"], 1)

            def body(b, _, __):
                for step in range(4):
                    g = 4 * b + step
                    before = b if step else b - 1
                    after = b + 1 if step == 3 else b
                    if real(b):
                        pe.wait_ge(s["qk0_taken"], g + 1)
                        pe.wait_ge(s["qk1_taken"], g + 1)
                        window(g, step, 0)
                        window(g, step, 1)
                    if real(before):
                        transpose_probs(g - 1, (step - 1) % 4, 0)
                        transpose_probs(g - 1, (step - 1) % 4, 1)
                    if step == 0 and real(b - 2):
                        pe.wait_ge(s["send_done"], b - 1)
                        pe.wait_ge(s["zt_taken"], last(b) + 1)
                        need(pe, s["rk_taken"], last(b - 3) + 1)
                        for i in range(2):
                            done = nc.tensor.transpose(misc[:, i * 128:i * 128 + 128], send[:, i * SENT:i * SENT + D], ident)
                        done.then_inc(s["nt_ready"], 1)
                    if step == 1 and real(b - 2):
                        pe.wait_ge(s["hot_ready"], b - 1)
                        nc.tensor.matmul(misc[:, 0:E], before_b[:], hot_b[:, 0:E], start=True, stop=True)
                        nc.tensor.matmul(misc[:, E:2 * E], ones_b[:], hot_b[:, 0:E], start=True, stop=False)
                        nc.tensor.matmul(misc[:, E:2 * E], before_b[:], hot_b[:, E:2 * E], start=False, stop=True)
                        nc.tensor.matmul(misc[:, 2 * E:3 * E], ones_b[:], hot_b[:, 0:E], start=True, stop=False)
                        nc.tensor.matmul(misc[:, 2 * E:3 * E], ones_b[:], hot_b[:, E:2 * E], start=False, stop=True).then_inc(s["rk_ready"], 1)
                    if step == 2 and real(b + 1):
                        pe.wait_ge(s["z_a_done"], b + 2)
                        need(pe, s["yt_taken"], last(b - 1) + 1)
                        need(pe, s["zt_taken"], b + 1)
                        for i in range(2):
                            done = nc.tensor.transpose(misc[:, i * 128:i * 128 + 128], z_a[:, i * 128:i * 128 + 128], ident)
                        done.then_inc(s["zt_ready"], 1)
                    if real(after):
                        if step == 3:
                            pe.wait_ge(s["split_ready"], b + 2)
                        project_qk(g + 1, (step + 1) % 4, 0)
                        project_qk(g + 1, (step + 1) % 4, 1)
                    if step == 1 and real(b - 1):
                        pe.wait_ge(s["attn_taken"], 4 * b)
                        pe.wait_ge(s["zt_taken"], last(b) + 1)
                        need(pe, s["rk_taken"], b - 1)
                        for c in range(8):
                            done = nc.tensor.matmul(misc[:, 0:256], w_out[:, c * D:(c + 1) * D], attn[:, c * 256:c * 256 + 256], start=c == 0, stop=c == 7)
                        done.then_inc(s["y_ready"], 1)
                    if real(before):
                        apply_probs(g - 1, (step - 1) % 4, before)
                    if real(after):
                        project_v(g + 1, (step + 1) % 4)
                    if step == 0 and real(b - 2):
                        pe.wait_ge(s["nt_taken"], b - 1)
                        for i in range(2):
                            done = nc.tensor.matmul(misc[:, i * E:(i + 1) * E], nT[:, i * 128:i * 128 + 128], router[:], start=True, stop=True)
                        done.then_inc(s["lg_ready"], 1)
                    if step == 1 and real(b - 1):
                        pe.wait_ge(s["y_taken"], b)
                        for i in range(2):
                            done = nc.tensor.transpose(misc[:, i * 128:i * 128 + 128], yT[:, i * 128:i * 128 + 128], ident)
                        done.then_inc(s["yt_ready"], 1)

            turns(pe, body)

        def finish_modulation(engine, then, m, tmp, rows, width):
            scale, gate = (m.rearrange("p (half kind w) -> p half kind w", half=2, w=width)[:, :, kind] for kind in (CA, GA))
            size, sign = (tmp[0:rows, k * 2 * width:(k + 1) * 2 * width].rearrange("p (half w) -> p half w", half=2) for k in range(2))
            then(engine.tensor_scalar(scale, scale, 1.0, None, ALU.add))
            then(engine.tensor_scalar(sign, gate, 0.0, 2.0, ALU.is_ge, ALU.mult))
            then(engine.tensor_scalar(sign, sign, -1.0, None, ALU.add))
            then(engine.tensor_tensor(size, gate, sign, ALU.mult))
            then(engine.tensor_scalar(size, size, GATE_MIN, None, ALU.max))
            then(engine.tensor_tensor(gate, size, sign, ALU.mult))

        raw = [half[:, 0:512] for pair in (probs, probsT, qk) for half in pair]

        @block.scalar
        def _(act):
            act.wait_ge(s["mod_in"], 64)
            for n in range(2):
                nc.scalar.activation(c_col[n][:], c_col[n][:], ACT.Silu).then_inc(s["c_silu"], 1)
            act.wait_ge(s["weights_in"], 96)
            for n, part in enumerate(raw):
                nc.scalar.activation(w_high[:, n * 512:n * 512 + 512], part, ACT.Copy, scale=DH ** -0.5 if n < 2 else 1.0).then_inc(s["qkv_high"], 1)
            for n in range(2):
                act.wait_ge(s["mod_made"], n + 1)
                nc.scalar.copy(mod_col[n][:], banks[4 + n][:, 0:6 * B]).then_inc(s["mod_copied"], 1)
                for half in range(2):
                    nc.scalar.copy(mod_stage[n][:, half * 384:half * 384 + 384], banks[2 * n + half][0:B, 0:384]).then_inc(s["mod_copied"], 1)
            act.wait_ge(s["consts_in"], 16)
            act.wait_ge(s["split_done"], 1)
            nc.scalar.preload_act_table_set("natural_log_exp_and_others")

            def exponentials(g, step, parity):
                act.wait_ge(s["negmax_ready"], 2 * g + parity + 1)
                need(act, s["pt_ready"], 2 * (g - 2) + parity + 1)
                need(act, s["inverse_ready"], 2 * (g - 2) + parity + 1)
                for n in range(4):
                    slot = step % 2 * 8 + parity * 4 + n
                    at = parity * 512 + n * 128
                    done = nc.scalar.activation(probs[step % 2][:, at:at + 128], scores_bank[parity][:, n * 128:n * 128 + 128], ACT.Exp,
                                                bias=neg_max[:, slot:slot + 1], accum_out=sums[:, slot:slot + 1])
                done.then_inc(s["exp_done"], 1)

            def layer_norm_scale(owner, n, kind):
                act.wait_ge(s["stats_" + kind], owner + 1)
                variance = moments[:, 4 * n:4 * n + 4].rearrange("p (i two) -> p i two", two=2)[:, :, 1]
                nc.scalar.activation(log_var[:, 2 * n:2 * n + 2], variance, ACT.Ln, bias=const[:, C_EPS:C_EPS + 1]).then_inc(s["log_" + kind], 1)
                act.wait_ge(s["log_" + kind], owner + 1)
                nc.scalar.activation(rstd[:, 2 * n:2 * n + 2], log_var[:, 2 * n:2 * n + 2], ACT.Exp, scale=-0.5).then_inc(s["rstd_" + kind], 1)

            def body(b, _, __):
                for step in range(4):
                    g = 4 * b + step
                    before = b if step else b - 1
                    after = b + 1 if step == 3 else b
                    if step == 1 and real(b + 1):
                        layer_norm_scale(b + 1, 0, "a")
                    if real(b):
                        exponentials(g, step, 0)
                        exponentials(g, step, 1)
                    if step == 2 and real(b + 1):
                        act.wait_ge(s["zt_ready"], b + 2)
                        need(act, s["split_ready"], b + 1)
                        nc.scalar.activation(hT[:], misc[:, 0:256], ACT.Identity, scale=mod_col[0][:, cols(CA * B + b + 1, 1)],
                                             bias=mod_col[0][:, cols(SA * B + b + 1, 1)]).then_inc(s["zt_taken"], 1)
                    if real(after):
                        act.wait_ge(s["qk0_ready"], g + 2)
                        need(act, s["scores_ready"], 2 * g)
                        nc.scalar.copy(qk[(step + 1) % 2][:, 0:512], proj_bank[3 * ((step + 1) % 4) % 2][:]).then_inc(s["qk0_taken"], 1)
                    if step == 2 and real(b - 1):
                        layer_norm_scale(b - 1, 1, "b")
                    if step == 3 and real(b - 1):
                        layer_norm_scale(b - 1, 2, "c")
                    if step == 1 and real(b - 2):
                        act.wait_ge(s["low_top_done"], b - 1)
                        need(act, s["score_done"], b - 2)
                        nc.scalar.activation(exp_top[:], low_top[:], ACT.Exp, scale=-1.0).then_inc(s["exp_top_done"], 1)
                    if step == 1 and real(b - 1):
                        act.wait_ge(s["y_ready"], b)
                        need(act, s["yt_ready"], b - 1)
                        nc.scalar.activation(yT[:], misc[:, 0:256], ACT.Copy, scale=mod_col[0][:, cols(GA * B + b - 1, 1)]).then_inc(s["y_taken"], 1)
                    if real(before):
                        act.wait_ge(s["attn_ready"], g)
                        need(act, s["y_ready"], before)
                        n = (step - 1) % 4
                        nc.scalar.copy(attn[:, n * 512:n * 512 + 512], attn_bank[:]).then_inc(s["attn_taken"], 1)

                if isinstance(b, int) and 0 <= b < 3:
                    split_experts_high(nc, act, raw_experts, range(3 * b, 3 * b + 3), weights[0], s["experts_in"], EXPERT_LOADS, s["experts_high"])

            turns(act, body)

        @block.vector
        def _(dve):
            steps = [0]

            def then(instruction):
                steps[0] += 1
                instruction.then_inc(s["setup_steps"], 1)
                dve.wait_ge(s["setup_steps"], steps[0])

            dve.wait_ge(s["consts_in"], 16)
            for to, at, size in ((ident_b, C_IDENT, 128), (window_b, C_WINDOW, 256), (before_b, C_BEFORE, 128), (ones_b, C_ONES, 128)):
                done = nc.vector.tensor_copy(to[:], const[:, at:at + size])
            done.then_inc(s["consts_cast"], 1)
            nc.vector.memset(send[:], 0.0)
            for n in range(2):
                nc.vector.tensor_copy(counts[n][:], const[:, C_REGION:C_REGION + E])
            for n, part in enumerate(raw):
                dve.wait_ge(s["qkv_high"], n + 1)
                at = slice(n * 512, n * 512 + 512)
                done = nc.vector.scalar_tensor_tensor(w_low[:, at], part, DH ** -0.5 if n < 2 else 1.0, w_high[:, at].bitcast(F32), ALU.mult, ALU.subtract)
            done.then_inc(s["split_done"], 1)
            dve.wait_ge(s["mod_copied"], 1)
            finish_modulation(nc.vector, then, mod_col[0][:], mod_tmp, 128, B)
            dve.wait_ge(s["x_first_in"], 16)

            def maxima(g, step, parity):
                dve.wait_ge(s["scores_ready"], 2 * g + parity + 1)
                need(dve, s["exp_done"], 2 * (g - 2) + parity + 1)
                slot = step % 2 * 8 + parity * 4
                nc.vector.tensor_reduce(neg_max[:, slot:slot + 4], scores_bank[parity][:].rearrange("p (n k) -> p n k", k=128), AX.X, ALU.max,
                                        negate=True).then_inc(s["negmax_ready"], 1)

            def inverses(g, step, parity):
                dve.wait_ge(s["exp_done"], 2 * g + parity + 1)
                need(dve, s["norm_done"], 2 * (g - 2) + parity + 1)
                slot = step % 2 * 8 + parity * 4
                nc.vector.reciprocal(inverse[:, slot:slot + 4], sums[:, slot:slot + 4]).then_inc(s["inverse_ready"], 1)

            def statistics(n, kind, owner, source):
                wait_apart(dve, s["rstd_" + kind], owner, s["passed_dve"])
                for i in range(2):
                    done = nc.vector.bn_stats(stats[:, 12 * n + 6 * i:12 * n + 6 * i + 6], source[i])
                done.then_inc(s["parts_" + kind], 1)
                wait_apart(dve, s["parts_" + kind], owner + 1, s["passed_dve"])
                for i in range(2):
                    done = nc.vector.bn_aggr(moments[:, 4 * n + 2 * i:4 * n + 2 * i + 2], stats[:, 12 * n + 6 * i:12 * n + 6 * i + 6])
                done.then_inc(s["stats_" + kind], 1)

            def normed(n, kind, owner, to, source):
                dve.wait_ge(s["rstd_" + kind], owner + 1)
                for i in range(2):
                    done = nc.vector.tensor_scalar(to[:, i * 128:i * 128 + 128], source[i], moments[:, 4 * n + 2 * i:4 * n + 2 * i + 1],
                                                   rstd[:, 2 * n + i:2 * n + i + 1], ALU.subtract, ALU.mult)
                done.then_inc(s[f"z_{kind}_done"], 1)

            def tiles_of_x(owner):
                return [x[:, cols(owner * 256 + i * 128, 128)] for i in range(2)]

            def choose(b):
                dve.wait_ge(s["lg_ready"], b + 1)
                nc.vector.tensor_copy(logits[:], misc[:, 0:16]).then_inc(s["lg_taken"], 1)
                wait_apart(dve, s["lg_taken"], b + 1, s["passed_dve"])
                for i in range(2):
                    done = nc.vector.max(top[:, i * 8:i * 8 + 8], logits[:, i * 8:i * 8 + 8])
                done.then_inc(s["top_done"], 1)
                wait_apart(dve, s["top_done"], b + 1, s["passed_dve"])
                for i in range(2):
                    done = nc.vector.max_index(top_at[:, i * 8:i * 8 + 8], top[:, i * 8:i * 8 + 8], logits[:, i * 8:i * 8 + 8])
                done.then_inc(s["top_at_done"], 1)
                need(dve, s["exp_top_done"], b)
                nc.vector.tensor_scalar(low_top[:], top[:].rearrange("p (i e) -> p i e", e=8)[:, :, 0], -87.0, None, ALU.max).then_inc(s["low_top_done"], 1)
                dve.wait_ge(s["top_at_done"], b + 1)
                nc.vector.tensor_copy(expert[:], top_at[:].rearrange("p (i e) -> p i e", e=8)[:, :, 0]).then_inc(s["expert_done"], 1)
                dve.wait_ge(s["expert_done"], b + 1)
                for i in range(2):
                    done = nc.vector.tensor_scalar(hot[:, i * 8:i * 8 + 8], const[:, C_INDEX:C_INDEX + E], expert[:, i:i + 1], None, ALU.is_equal)
                done.then_inc(s["hot_done"], 1)
                dve.wait_ge(s["hot_done"], b + 1)
                need(dve, s["rk_ready"], b)
                nc.vector.tensor_copy(hot_b[:], hot[:]).then_inc(s["hot_ready"], 1)

            def take_ranks(b):
                dve.wait_ge(s["rk_ready"], b + 1)
                nc.vector.tensor_tensor(place[:].rearrange("p (i e) -> p i e", e=8), misc[:, 0:16].rearrange("p (i e) -> p i e", e=8),
                                        counts[0][:].unsqueeze(1).broadcast_to([128, 2, 8]), ALU.add).then_inc(s["place_made"], 1)
                dve.wait_ge(s["place_made"], b + 1)
                nc.vector.tensor_tensor(counts[0][:], misc[:, 16:24], counts[0][:], ALU.add).then_inc(s["rk_taken"], 1)

            def choose_rows(b):
                nc.vector.tensor_tensor(picked[:], place[:], hot[:], ALU.mult).then_inc(s["picked_done"], 1)
                dve.wait_ge(s["picked_done"], b + 1)
                nc.vector.tensor_reduce(place_f[:], picked[:].rearrange("p (i e) -> p i e", e=8), AX.X, ALU.add).then_inc(s["place_summed"], 1)
                dve.wait_ge(s["place_summed"], b + 1)
                need(dve, sent_done, 32 * b)
                nc.vector.tensor_copy(rows_now[:], place_f[:]).then_inc(s["place_done"], 1)

            def score(b):
                dve.wait_ge(s["exp_top_done"], b + 1)
                nc.vector.tensor_scalar(low_top[:], exp_top[:], 1.0, None, ALU.add).then_inc(s["score_steps"], 1)
                dve.wait_ge(s["score_steps"], b + 1)
                nc.vector.tensor_copy(send[:].bitcast(U32).rearrange("p (i w) -> p i w", w=SENT)[:, :, TOKEN], token[:, cols(2 * b, 2)])
                nc.vector.reciprocal(send[:].rearrange("p (i w) -> p i w", w=SENT)[:, :, SCORE], low_top[:]).then_inc(s["score_done"], 1)

            def body(b, _, __):
                for step in range(4):
                    g = 4 * b + step
                    before = b if step else b - 1
                    after = b + 1 if step == 3 else b

                    def take_transposed(parity):
                        if real(before):
                            dve.wait_ge(s["pt_ready"], 2 * (g - 1) + parity + 1)
                            need(dve, s["attn_ready"], g - 2)
                            nc.vector.tensor_copy(probsT[(step - 1) % 2][:, parity * 512:parity * 512 + 512], pt_bank[parity][:]).then_inc(s["pt_taken"], 1)

                    if step == 1 and real(b - 2):
                        choose(b - 2)
                    if step == 2 and real(b - 1):
                        dve.wait_ge(s["yt_ready"], b)
                        now = x[:, cols((b - 1) * 256, 256)]
                        nc.vector.tensor_tensor(now, misc[:, 0:256], now, ALU.add).then_inc(s["yt_taken"], 1)
                    if step == 3 and real(b + 1):
                        dve.wait_ge(s["zt_taken"], b + 2)
                        need(dve, s["v_ready"], 4 * b + 4)
                        nc.vector.tensor_copy(h_high[:], hT[:]).then_inc(s["high_done"], 1)
                        dve.wait_ge(s["high_done"], b + 2)
                        nc.vector.tensor_tensor(h_low[:], hT[:], h_high[:].bitcast(F32), ALU.subtract).then_inc(s["split_ready"], 1)
                    if real(b):
                        maxima(g, step, 0)
                        maxima(g, step, 1)
                    take_transposed(0)
                    if real(b):
                        inverses(g, step, 0)
                    take_transposed(1)
                    if step == 0 and real(b - 2):
                        dve.wait_ge(s["nt_ready"], b - 1)
                        need(dve, s["lg_ready"], b - 2)
                        nc.vector.tensor_copy(nT[:], misc[:, 0:256]).then_inc(s["nt_taken"], 1)
                    if step == 1 and real(b - 2):
                        take_ranks(b - 2)
                    if real(b):
                        inverses(g, step, 1)
                    if step == 2 and real(b - 1):
                        dve.wait_ge(s["yt_taken"], b)
                        statistics(1, "b", b - 1, tiles_of_x(b - 1))
                    if step == 3 and real(b - 1):
                        dve.wait_ge(s["h_b_done"], b)
                        statistics(2, "c", b - 1, [h_b[:, i * 128:i * 128 + 128] for i in range(2)])
                    if real(after):
                        dve.wait_ge(s["qk1_ready"], g + 2)
                        need(dve, s["scores_ready"], 2 * g)
                        nc.vector.tensor_copy(qk[(step + 1) % 2][:, 512:1024], proj_bank[(3 * ((step + 1) % 4) + 1) % 2][:]).then_inc(s["qk1_taken"], 1)
                    if step == 0 and isinstance(b, int) and b == 0:
                        dve.wait_ge(s["x_in"], 48)
                    if step == 0 and real(b + 1):
                        statistics(0, "a", b + 1, tiles_of_x(b + 1))
                    if step == 1 and real(b + 1):
                        need(dve, s["zt_ready"], b + 1)
                        normed(0, "a", b + 1, z_a, tiles_of_x(b + 1))
                    if step == 1 and real(b - 2):
                        choose_rows(b - 2)
                    if step == 2 and real(b - 1):
                        need(dve, s["h_b_done"], b - 1)
                        normed(1, "b", b - 1, z_b, tiles_of_x(b - 1))
                    if step == 2 and real(b - 2):
                        score(b - 2)
                    if step == 3 and real(b - 1):
                        need(dve, s["send_done"], b - 1)
                        normed(2, "c", b - 1, z_c, [h_b[:, i * 128:i * 128 + 128] for i in range(2)])
                    if real(after):
                        dve.wait_ge(s["v_ready"], g + 2)
                        need(dve, s["attn_ready"], g - 2)
                        nc.vector.tensor_copy(v[(step + 1) % 4][:, 0:512], proj_bank[(3 * ((step + 1) % 4) + 2) % 2][:]).then_inc(s["v_taken"], 1)

            turns(dve, body)

        @block.gpsimd
        def _(pool):
            def normalise(g, step, parity):
                pool.wait_ge(s["inverse_ready"], 2 * g + parity + 1)
                slot = step % 2 * 8 + parity * 4
                p = probs[step % 2][:, parity * 512:parity * 512 + 512].rearrange("p (n k) -> p n k", k=128)
                nc.gpsimd.tensor_tensor(p, p, inverse[:, slot:slot + 4].unsqueeze(2).broadcast_to([128, 4, 128]), ALU.mult).then_inc(s["norm_done"], 1)

            def over_tiles(row):
                return row.unsqueeze(1).broadcast_to([128, 2, D])

            def tiles(buffer):
                return buffer.rearrange("p (i d) -> p i d", d=D)

            shift, scale, gate = (over_tiles(mod_b[:, n * D:(n + 1) * D]) for n in range(3))

            def body(b, _, __):
                for step in range(4):
                    g = 4 * b + step
                    if real(b):
                        normalise(g, step, 0)
                        normalise(g, step, 1)
                    if step == 2 and real(b - 1):
                        pool.wait_ge(s["z_b_done"], b)
                        pool.wait_ge(s["mod_b_in"], 16 * b)
                        need(pool, s["z_c_done"], b - 1)
                        nc.gpsimd.tensor_tensor(tiles(h_b[:]), tiles(z_b[:]), scale, ALU.mult).then_inc(s["scaled_b"], 1)
                        pool.wait_ge(s["scaled_b"], b)
                        nc.gpsimd.tensor_tensor(tiles(h_b[:]), tiles(h_b[:]), shift, ALU.add).then_inc(s["h_b_done"], 1)
                    if step == 2 and real(b - 2):
                        pool.wait_ge(s["place_done"], b - 1)
                        wait_apart(pool, s["score_done"], b - 1, s["passed_pool"])
                        for i in range(2):
                            nc.gpsimd.indirect_dma_start(sent[0], bass.IndirectOffsetOnAxis(ap=rows_now[:, i:i + 1], axis=0),
                                                         send[:, i * SENT:(i + 1) * SENT], None).then_inc(sent_done, 16)
                    if step == 3 and real(b - 1):
                        pool.wait_ge(s["h_b_done"], b)
                        nc.gpsimd.tensor_tensor(tiles(g_b[:]), tiles(h_b[:]), gate, ALU.mult).then_inc(s["gated_b"], 1)
                        pool.wait_ge(s["gated_b"], b)
                        now = x[:, cols((b - 1) * 256, 256)]
                        nc.gpsimd.tensor_tensor(now, now, g_b[:], ALU.add).then_inc(s["x_b_done"], 1)
                        pool.wait_ge(s["z_c_done"], b)
                        need(pool, sent_done, 32 * (b - 1))
                        need(pool, s["nt_ready"], b - 1)
                        rows = send[:].rearrange("p (i w) -> p i w", w=SENT)[:, :, 0:D]
                        nc.gpsimd.tensor_tensor(rows, tiles(z_c[:]), over_tiles(ln_row[:, 0:D]), ALU.mult).then_inc(s["scaled_c"], 1)
                        pool.wait_ge(s["scaled_c"], b)
                        nc.gpsimd.tensor_tensor(rows, rows, over_tiles(ln_row[:, D:2 * D]), ALU.add).then_inc(s["send_done"], 1)

                if isinstance(b, int) and 0 <= b < 3:
                    split_experts_low(nc, pool, raw_experts, range(3 * b, 3 * b + 3), weights[0], weights[1], s["experts_high"])

            pool.wait_ge(s["consts_in"], 16)
            nc.gpsimd.tensor_scalar(token[:], const[:, C_SLOT:C_SLOT + TILES + NOWHERE], 128.0, const[:, C_ROW:C_ROW + 1], ALU.mult, ALU.add).then_inc(s["token_made"], 1)
            nc.gpsimd.memset(blank[:], 0.0).then_inc(s["token_made"], 1)
            pool.wait_ge(s["token_made"], 2)
            nc.gpsimd.tensor_copy(blank[:].bitcast(U32).rearrange("p (n w) -> p n w", w=SENT)[:, :, TOKEN], token[:, TILES + E:TILES + NOWHERE]).then_inc(s["blank_made"], 1)
            pool.wait_ge(s["blank_sent"], 32)
            nc.gpsimd.tensor_copy(blank[:].bitcast(U32).rearrange("p (n w) -> p n w", w=SENT)[:, :, TOKEN], token[:, TILES:TILES + E])
            steps = [0]

            def then(instruction):
                steps[0] += 1
                instruction.then_inc(s["pool_steps"], 1)
                pool.wait_ge(s["pool_steps"], steps[0])

            for n in range(2):
                pool.wait_ge(s["mod_copied"], 3 * n + 3)
                finish_modulation(nc.gpsimd, then, mod_stage[n][:], mod_tmp_pool, B, D)
                pool.sem_inc(s["mod_rows_made"], 1)
            finish_modulation(nc.gpsimd, then, mod_col[1][:], mod_tmp_pool, 128, B)
            pool.wait_ge(s["small_in"], 64)
            turns(pool, body)
            pool.wait_ge(sent_done, 32 * B)

        ctx_block.close()
        clear(nc, used)


def load_experts(engine, t, layer, raw, second, loaded):
    def first(start, size):
        return raw[start // 512][:, start % 512:start % 512 + size]

    count = 0
    for e in range(E + 1 if layer == 0 else E):
        if layer:
            loads = [(first(e * F, F), t["L1_ffn_W1"][e])]
            down = t["L1_ffn_W2"][e]
        elif e < E:
            loads = [(first((2 * e + i) * F, F), t[f"L0_ffn_{k}_w"][e]) for i, k in enumerate(("gate", "up"))]
            down = t["L0_ffn_down_w"][e]
        else:
            loads = [(first((2 * e + i) * F, F), t[f"L0_ffn_sh_{k}"]) for i, k in enumerate(("gate", "up"))]
            down = t["L0_ffn_sh_down"]
        loads.append((second[:, e * F:(e + 1) * F].rearrange("p (c n) -> p c n", n=D), down.rearrange("(c p) n -> p c n", p=128)))
        for to, source in loads:
            engine.dma_start(to, source).then_inc(loaded, 16)
            count += 16
    return count


def split_experts_high(nc, act, raw, pieces, high, loaded, loads, high_done):
    act.wait_ge(loaded, loads)
    for n in pieces:
        nc.scalar.copy(high[:, n * 512:(n + 1) * 512], raw[n]).then_inc(high_done, 1)


def split_experts_low(nc, pool, raw, pieces, high, low, high_done):
    for n in pieces:
        at = slice(n * 512, (n + 1) * 512)
        pool.wait_ge(high_done, n + 1)
        nc.gpsimd.tensor_tensor(low[:, at], raw[n], high[:, at].bitcast(F32), ALU.subtract)


def experts(nc, t, layer, counts, blank, sent, back, returned, banks, const, ident, weights):
    ctx = ExitStack()
    with ctx:
        def sb(name, columns, kind=F32, rows=128):
            return ctx.enter_context(nc.sbuf_tensor(f"{name}_{layer}", [rows, columns], kind))

        used = []

        def sem(name):
            used.append(ctx.enter_context(nc.semaphore(f"e{layer}_{name}")))
            return used[-1]

        shared = layer == 0
        width = 2 * F if shared else F
        branches = 2 if shared else 1
        chunks = 2 * branches
        kinds = E + 1 if shared else E
        up_high, up_low, down = weights
        if not shared:
            bias1, bias2 = sb("bias1", E * F), sb("bias2", E * D)
        tiles_of, ends, delta = sb("tiles_of", E), sb("ends", E), sb("delta", E)
        tiles_u, counts_u = sb("tiles_u", E, U32), sb("counts_u", E, U32)
        past, moves = sb("past", SLOTS * E), sb("moves", SLOTS * E)
        slot_f, slot_move = sb("slot_f", SLOTS), sb("slot_move", SLOTS)
        slot_expert, slot_row = sb("slot_expert", SLOTS, U32), sb("slot_row", SLOTS, U32)
        rows_in = [sb(f"rows_in{n}", SENT) for n in range(4)]
        n_high, n_low = ([sb(f"{k}{n}", 128, F32R) for n in range(2)] for k in ("n_high", "n_low"))
        act_out = [sb(f"act_out{n}", branches * F) for n in range(2)]
        hidden = [sb(f"hidden{n}", branches * F) for n in range(2)]
        hiddenT = [sb(f"hiddenT{n}", chunks * 128) for n in range(2)]
        result = [sb(f"result{n}", D) for n in range(4)]
        index = [sb(f"index{n}", 1, U32) for n in range(4)]

        s = {n: sem(n) for n in """bias_in setup_steps passed counts_ready slots_ready blanks_sent
            nT_ready high_done split_ready first_ready activated hidden_ready biased hiddenT_ready hiddenT_taken y_ready y_taken""".split()}
        rows_loaded = [sem(f"rows_loaded{n}") for n in range(4)]
        first_bank = [banks[0:2], banks[2:4]]
        nT_bank, hidden_bank, y_bank = banks[4], banks[5], banks[6]

        def slots(engine, body):
            turns(engine, lambda n, k, i: body(n, k % 2, k, i), SLOTS, 4, 3, 4)

        def slot(n):
            return real(n, SLOTS)

        def clear_tails(engine, of):
            for e in of:
                at = engine.value_load(counts_u[0:1, e:e + 1], min_val=0, max_val=(E + 1) * CAP - 128)
                engine.dma_start(sent[bass.ds(at, 128), :], blank[:, e * SENT:(e + 1) * SENT]).then_inc(s["blanks_sent"], 16)

        ctx_block = ExitStack()
        block = ctx_block.enter_context(nc.Block())

        @block.sync
        def _(sp):
            if not shared:
                sp.dma_start(bias1[:], t["L1_ffn_b1"].rearrange("e f -> (e f)").partition_broadcast(128)).then_inc(s["bias_in"], 16)
                sp.dma_start(bias2[:], t["L1_ffn_b2"].rearrange("e d -> (e d)").partition_broadcast(128)).then_inc(s["bias_in"], 16)
            sp.wait_ge(s["counts_ready"], 1)
            clear_tails(sp, range(4))
            sp.wait_ge(s["slots_ready"], 1)
            sp.wait_ge(s["blanks_sent"], 16 * E)

            def body(n, parity, k, i):
                if slot(n + 3):
                    at = sp.value_load(slot_row[0:1, cols(n + 3, 1)], min_val=0, max_val=(E + 1) * CAP - 128)
                    need(sp, s["nT_ready"], n)
                    need(sp, s["hidden_ready"], n)
                    sp.dma_start(rows_in[(k + 3) % 4][:], sent[bass.ds(at, 128), :]).then_inc(rows_loaded[(k + 3) % 4], 16)

            slots(sp, body)

        @block.gpsimd
        def _(pool):
            def body(n, parity, k, i):
                if slot(n - 2):
                    wait_apart(pool, s["y_taken"], n - 1, s["passed"])
                    m = (k - 2) % 4
                    nc.gpsimd.indirect_dma_start(back, bass.IndirectOffsetOnAxis(ap=index[m][:], axis=0), result[m][:], None).then_inc(returned[m], 16)

            slots(pool, body)
            for m in range(4):
                pool.wait_ge(returned[m], 16 * (SLOTS // 4))

        @block.tensor
        def _(pe):
            pe.wait_ge(s["slots_ready"], 1)

            def body(n, parity, k, i):
                if slot(n):
                    own = pe.value_load(slot_expert[0:1, cols(n, 1)], min_val=0, max_val=kinds - 1)
                    pe.wait_ge(s["split_ready"], n + 1)
                    need(pe, s["hidden_ready"], n - 1)
                    for branch in range(branches):
                        weights = [w[:, cols(own * width, width)] if branch == 0 else w[:, E * width:(E + 1) * width] for w in (up_high, up_low)]
                        to = first_bank[parity][branch][:, 0:width]
                        nc.tensor.matmul(to, n_high[parity][:], weights[0], start=True, stop=False)
                        nc.tensor.matmul(to, n_high[parity][:], weights[1], start=False, stop=False)
                        done = nc.tensor.matmul(to, n_low[parity][:], weights[0], start=False, stop=True)
                    done.then_inc(s["first_ready"], 1)
                if slot(n + 1):
                    buffer = (k + 1) % 4
                    pe.wait_ge(rows_loaded[buffer], 16 * (i + (k + 1) // 4 + 1))
                    need(pe, s["split_ready"], n + 1)
                    nc.tensor.transpose(nT_bank[:, 0:128], rows_in[buffer][:, 0:D], ident).then_inc(s["nT_ready"], 1)
                if slot(n - 1):
                    pe.wait_ge(s["hidden_ready"], n)
                    need(pe, s["hiddenT_taken"], n - 1)
                    for c in range(chunks):
                        done = nc.tensor.transpose(hidden_bank[:, c * 128:c * 128 + 128], hidden[1 - parity][:, c * 128:c * 128 + 128], ident)
                    done.then_inc(s["hiddenT_ready"], 1)
                if slot(n - 2):
                    own = pe.value_load(slot_expert[0:1, cols(n - 2, 1)], min_val=0, max_val=kinds - 1)
                    pe.wait_ge(s["hiddenT_taken"], n - 1)
                    need(pe, s["y_taken"], n - 2)
                    for c in range(chunks):
                        w = down[:, cols(own * F + c * D, D)] if c < 2 else down[:, E * F + (c - 2) * D:E * F + (c - 1) * D]
                        done = nc.tensor.matmul(y_bank[:, 0:D], hiddenT[parity][:, c * 128:c * 128 + 128], w, start=c == 0, stop=c == chunks - 1)
                    done.then_inc(s["y_ready"], 1)

            slots(pe, body)

        @block.scalar
        def _(act):
            act.wait_ge(s["counts_ready"], 1)
            clear_tails(act, range(4, E))

            def body(n, parity, k, i):
                if slot(n):
                    act.wait_ge(s["first_ready"], n + 1)
                    need(act, s["hidden_ready"], n - 1)
                    if shared:
                        score = rows_in[k][:, SCORE:SCORE + 1]
                        nc.scalar.activation(act_out[parity][:, 0:F], first_bank[parity][0][:, 0:F], ACT.Silu, scale=score)
                        nc.scalar.activation(act_out[parity][:, F:2 * F], first_bank[parity][1][:, 0:F], ACT.Silu).then_inc(s["activated"], 1)
                    else:
                        act.wait_ge(s["biased"], n + 1)
                        need(act, s["hiddenT_ready"], n - 1)
                        nc.scalar.activation(hidden[parity][:], act_out[parity][:], ACT.Gelu).then_inc(s["hidden_ready"], 1)
                if slot(n - 1):
                    act.wait_ge(s["hiddenT_ready"], n)
                    need(act, s["y_ready"], n - 2)
                    nc.scalar.copy(hiddenT[1 - parity][:], hidden_bank[:, 0:chunks * 128]).then_inc(s["hiddenT_taken"], 1)

            slots(act, body)

        @block.vector
        def _(dve):
            steps = [0]

            def then(instruction):
                steps[0] += 1
                instruction.then_inc(s["setup_steps"], 1)
                dve.wait_ge(s["setup_steps"], steps[0])

            nc.vector.tensor_copy(counts_u[:], counts[:]).then_inc(s["counts_ready"], 1)
            then(nc.vector.tensor_tensor(tiles_of[:], counts[:], const[:, C_REGION:C_REGION + E], ALU.subtract))
            then(nc.vector.tensor_scalar(tiles_of[:], tiles_of[:], 63.5, 1 / 128, ALU.add, ALU.mult))
            then(nc.vector.tensor_copy(tiles_u[:], tiles_of[:]))
            then(nc.vector.tensor_copy(tiles_of[:], tiles_u[:]))
            then(nc.vector.tensor_tensor_scan(ends[:], const[:, C_ONES:C_ONES + E], tiles_of[:], 0.0, ALU.mult, ALU.add))
            nc.vector.tensor_scalar(delta[:], tiles_of[:], -128.0, float(CAP), ALU.mult, ALU.add)

            def by_expert(buffer, count, experts_):
                return buffer[:, 0:count * experts_].rearrange("p (n e) -> p n e", e=experts_)

            def along(row, count):
                return row.unsqueeze(1).broadcast_to([128, count, row.shape[1]])

            slot_index = const[:, C_SLOT:C_SLOT + SLOTS]
            then(nc.vector.tensor_tensor(by_expert(past, SLOTS, E), slot_index.unsqueeze(2).broadcast_to([128, SLOTS, E]), along(ends[:], SLOTS), ALU.is_ge))
            nc.vector.tensor_reduce(slot_f[:], by_expert(past, SLOTS, E), AX.X, ALU.add)
            then(nc.vector.tensor_tensor(by_expert(moves, SLOTS, E), by_expert(past, SLOTS, E), along(delta[:], SLOTS), ALU.mult))
            then(nc.vector.tensor_reduce(slot_move[:], by_expert(moves, SLOTS, E), AX.X, ALU.add))
            nc.vector.tensor_scalar(slot_f[:], slot_f[:], float(kinds - 1), None, ALU.min)
            then(nc.vector.scalar_tensor_tensor(slot_move[:], slot_index, 128.0, slot_move[:], ALU.mult, ALU.add))
            nc.vector.tensor_copy(slot_row[:], slot_move[:])
            nc.vector.tensor_copy(slot_expert[:], slot_f[:]).then_inc(s["slots_ready"], 1)
            dve.wait_ge(s["slots_ready"], 1)
            if not shared:
                dve.wait_ge(s["bias_in"], 32)

            def body(n, parity, k, i):
                if slot(n + 1):
                    dve.wait_ge(s["nT_ready"], n + 2)
                    need(dve, s["first_ready"], n)
                    p = 1 - parity
                    nc.vector.tensor_copy(n_high[p][:], nT_bank[:, 0:128]).then_inc(s["high_done"], 1)
                    dve.wait_ge(s["high_done"], n + 2)
                    nc.vector.tensor_tensor(n_low[p][:], nT_bank[:, 0:128], n_high[p][:].bitcast(F32), ALU.subtract).then_inc(s["split_ready"], 1)
                if slot(n):
                    dve.wait_ge(rows_loaded[k], 16 * (i + 1))
                    need(dve, returned[k], 16 * i)
                    nc.vector.tensor_copy(index[k][:], rows_in[k][:, TOKEN:TOKEN + 1].bitcast(U32))
                    if not shared:
                        own = dve.value_load(slot_expert[0:1, cols(n, 1)], min_val=0, max_val=E - 1)
                    dve.wait_ge(s["first_ready"], n + 1)
                    if shared:
                        dve.wait_ge(s["activated"], n + 1)
                        need(dve, s["hiddenT_ready"], n - 1)
                        nc.vector.scalar_tensor_tensor(hidden[parity][:, 0:F], first_bank[parity][0][:, F:2 * F], rows_in[k][:, SCORE:SCORE + 1],
                                                       act_out[parity][:, 0:F], ALU.mult, ALU.mult)
                        nc.vector.tensor_tensor(hidden[parity][:, F:2 * F], first_bank[parity][1][:, F:2 * F], act_out[parity][:, F:2 * F],
                                                ALU.mult).then_inc(s["hidden_ready"], 1)
                    else:
                        need(dve, s["hidden_ready"], n - 1)
                        nc.vector.tensor_tensor(act_out[parity][:], first_bank[parity][0][:, 0:F], bias1[:, cols(own * F, F)], ALU.add).then_inc(s["biased"], 1)
                if slot(n - 2):
                    if not shared:
                        own = dve.value_load(slot_expert[0:1, cols(n - 2, 1)], min_val=0, max_val=E - 1)
                    dve.wait_ge(s["y_ready"], n - 1)
                    m = (k - 2) % 4
                    need(dve, returned[m], 16 * (i - (k < 2)))
                    if shared:
                        nc.vector.tensor_copy(result[m][:], y_bank[:, 0:D]).then_inc(s["y_taken"], 1)
                    else:
                        nc.vector.tensor_tensor(result[m][:], y_bank[:, 0:D], bias2[:, cols(own * D, D)], ALU.add).then_inc(s["y_taken"], 1)

            slots(dve, body)

        ctx_block.close()
        clear(nc, used)


def attention1(nc, t, x, const, ident, mod_col, mod_row, token, counts, shifted, back, sent, sent_done, banks, weights):
    ctx = ExitStack()
    with ctx:
        def sb(name, columns, kind=F32, rows=128):
            return ctx.enter_context(nc.sbuf_tensor("c_" + name, [rows, columns], kind))

        used = []

        def sem(name):
            used.append(ctx.enter_context(nc.semaphore("c_" + name)))
            return used[-1]

        EXPERT_LOADS = 16 * 2 * E
        HID = 256
        raw_hidden, raw_qk = sb("raw_hidden", 2 * HID), sb("raw_qk", D)
        hid_high, hid_low = sb("hid_high", 2 * HID, F32R), sb("hid_low", 2 * HID, F32R)
        wqk_high, wqk_low = sb("wqk_high", D, F32R), sb("wqk_low", D, F32R)
        w_out, router = sb("w_out", HID), sb("router", E)
        first_row = sb("first_row", 128, F32R)
        bias_high, bias_low = sb("bias_high", HID, F32R), sb("bias_low", HID, F32R)
        v_bias, router_bias, ln_row = sb("v_bias", HID), sb("router_bias", E), sb("ln_row", 2 * D)
        raw_experts = [sb(f"raw_expert{n}", 512)[:] for n in range(E // 2)]
        GATE_B, QK_B, GAMMA, BETA, OUT_B = 0, 2, 3, 5, 7
        col = sb("col", 8)
        got = sb("got", 256)
        mod_d, mod_h, mod_g, mod_f = sb("mod_d", D), sb("mod_h", 2 * D), sb("mod_g", D), sb("mod_f", 2 * D)
        stats, moments = sb("stats", 36), sb("moments", 12)
        var, neg_half, guess, square, rstd, offset = (sb(k, 6) for k in ("var", "neg_half", "guess", "square", "rstd", "offset"))
        out_bias = sb("out_bias", B)
        half_bits, guess_bits = sb("half_bits", 6, mybir.dt.int32), sb("guess_bits", 6, mybir.dt.int32)
        z_d, z_e, z_f, h, gh, normed_rows = (sb(k, 256) for k in ("z_d", "z_e", "z_f", "h", "gh", "normed_rows"))
        n_high, n_low = sb("n_high", 256, F32R), sb("n_low", 256, F32R)
        qk, q, k_ = sb("qk", 256), sb("q", 256), sb("k", 256)
        v, gate = sb("v", 512), sb("gate", 512)
        weighed, attn = sb("weighed", 384), sb("attn", 384)
        gated, yT = sb("gated", 512), sb("yT", 256)
        send, rT = sb("send", 2 * SENT), sb("rT", 256)
        logits, top, top_at, hot, hot_b, expert = sb("logits", 16), sb("top", 16), sb("top_at", 16, U32), sb("hot", 16), sb("hot_b", 16, BF16), sb("expert", 2)
        place, picked, place_f, rows_now = sb("place", 16), sb("picked", 16), sb("place_f", 2), sb("rows_now", 2, U32)
        before_b, ones_b = sb("before_b", 128, BF16), sb("ones_b", 128, BF16)

        s = {n: sem(n) for n in """weights_in split_done setup_steps got_in x2_gated x2_done mod_d_in mod_h_in mod_g_in mod_f_in
            newton newton_steps z_d_done z_e_done z_f_done parts_d parts_e parts_f stats_d stats_e stats_f h_scaled h_done gh_done x_h_done
            n_scaled n_done nt_ready nT_high nT_split qk_ready qk_done q_k_done v_ready v_done gate_ready gate_done
            sim_ready weighed_done attn_done pv_ready gated_done y_ready yT_done yt_ready x3_done send_scaled send_done ht_ready rT_done
            lg_ready logits_done top_done top_at_done expert_done hot_done hot_ready rk_ready place_made rk_taken picked_done place_summed
            place_done experts_in experts_high passed_dve passed_pool""".split()}
        qk_bank, v_bank, gate_bank, sim_bank, pv_bank, y_bank, yt_bank, misc = banks
        BEHIND = 3

        def batches(engine, body):
            turns(engine, lambda n, _, __: body(n), B, 1, 4, BEHIND)

        ctx_block = ExitStack()
        block = ctx_block.enter_context(nc.Block())

        @block.sync
        def _(sp):
            loads = [(raw_hidden[:], t["L1_attn_W_hidden"]), (raw_qk[:], t["L1_attn_W_qk"]), (router[:], t["L1_ffn_Wr"]),
                     (w_out[:].rearrange("p (c n) -> p c n", n=D), t["L1_attn_W_out"].rearrange("(c p) n -> p c n", p=128)),
                     (v_bias[:], t["L1_attn_b_hidden"][0:HID].partition_broadcast(128)), (router_bias[:], t["L1_ffn_br"].partition_broadcast(128)),
                     (ln_row[:, 0:D], t["L1_attn_ln_g"].partition_broadcast(128)), (ln_row[:, D:2 * D], t["L1_attn_ln_b"].partition_broadcast(128)),
                     (col[:, QK_B:QK_B + 1], t["L1_attn_b_qk"].unsqueeze(1)), (col[:, OUT_B:OUT_B + 1], t["L1_attn_b_out"].unsqueeze(1))]
            for i in range(2):
                loads.append((col[:, GATE_B + i:GATE_B + i + 1], t["L1_attn_b_hidden"][HID + i * 128:HID + i * 128 + 128].unsqueeze(1)))
                loads.append((col[:, GAMMA + i:GAMMA + i + 1], t["L1_attn_os_gamma"][i].unsqueeze(1)))
                loads.append((col[:, BETA + i:BETA + i + 1], t["L1_attn_os_beta"][i].unsqueeze(1)))
            assert len(loads) == LOADS
            for to, source in loads:
                sp.dma_start(to, source, allow_slow_non_contiguous=True).then_inc(s["weights_in"], 16)

            assert load_experts(sp, t, 1, raw_experts, weights[2], s["experts_in"]) == EXPERT_LOADS

            def body(n):
                if real(n - 2):
                    need(sp, s["send_done"], n - 2)
                    sp.dma_start(mod_f[:], mod_row[1][cols(n - 2, 1), SB * D:5 * D].broadcast_to([128, 2 * D])).then_inc(s["mod_f_in"], 16)
                if real(n + 2):
                    need(sp, s["gh_done"], n + 2)
                    sp.dma_start(mod_g[:], mod_row[1][cols(n + 2, 1), GA * D:3 * D].broadcast_to([128, D])).then_inc(s["mod_g_in"], 16)
                if real(n + 3):
                    need(sp, s["h_done"], n + 3)
                    sp.dma_start(mod_h[:], mod_row[1][cols(n + 3, 1), 0:2 * D].broadcast_to([128, 2 * D])).then_inc(s["mod_h_in"], 16)
                if real(n + 4):
                    need(sp, s["x2_done"], n + 4)
                    sp.dma_start(mod_d[:], mod_row[0][cols(n + 4, 1), GB * D:6 * D].broadcast_to([128, D])).then_inc(s["mod_d_in"], 16)
                    sp.dma_start(got[:].rearrange("p (i d) -> p i d", d=D), back[cols((n + 4) * 256, 256), :].rearrange("(i p) d -> p i d", p=128)).then_inc(s["got_in"], 16)

            batches(sp, body)

        @block.tensor
        def _(pe):
            pe.wait_ge(s["weights_in"], 16 * LOADS)
            pe.wait_ge(s["split_done"], 1)

            def product(to, left, right, start=True):
                nc.tensor.matmul(to, left[0], right[0], start=start, stop=False)
                nc.tensor.matmul(to, left[0], right[1], start=False, stop=False)
                return nc.tensor.matmul(to, left[1], right[0], start=False, stop=True)

            def part(pair, a, size):
                return [m[:, a:a + size] for m in pair]

            def body(n):
                normed_, hid = (n_high, n_low), (hid_high, hid_low)
                if real(n):
                    pe.wait_ge(s["nT_split"], n + 1)
                    need(pe, s["qk_done"], n)
                    product(qk_bank[:, 0:256], part((wqk_high, wqk_low), 0, D), part(normed_, 0, 256)).then_inc(s["qk_ready"], 1)
                if real(n - 1):
                    pe.wait_ge(s["attn_done"], n)
                    pe.wait_ge(s["v_done"], n)
                    need(pe, s["gated_done"], n - 1)
                    for c in range(2):
                        nc.tensor.matmul(pv_bank[:, c * 256:c * 256 + 256], v[:, c * 128:c * 128 + 128], attn[:, 0:256], start=True, stop=False, skip_group_check=True)
                        done = nc.tensor.matmul(pv_bank[:, c * 256 + 128:c * 256 + 256], v[:, HID + c * 128:HID + c * 128 + 128], attn[:, 256:384],
                                                start=False, stop=True, skip_group_check=True)
                    done.then_inc(s["pv_ready"], 1)
                if real(n - 3):
                    pe.wait_ge(s["send_done"], n - 2)
                    pe.wait_ge(s["x3_done"], last(n - 2) + 1)
                    for i in range(2):
                        done = nc.tensor.transpose(yt_bank[:, i * 128:i * 128 + 128], send[:, i * SENT:i * SENT + D], ident)
                    done.then_inc(s["ht_ready"], 1)
                if real(n):
                    need(pe, s["v_done"], n)
                    for i in range(2):
                        to = v_bank[:, i * HID:(i + 1) * HID]
                        nc.tensor.matmul(to, first_row[:], bias_high[:], start=True, stop=False)
                        nc.tensor.matmul(to, first_row[:], bias_low[:], start=False, stop=False)
                        done = product(to, part(normed_, i * 128, 128), part(hid, 0, HID), start=False)
                    done.then_inc(s["v_ready"], 1)
                if real(n - 3):
                    pe.wait_ge(s["rT_done"], n - 2)
                    for i in range(2):
                        done = nc.tensor.matmul(yt_bank[:, i * E:(i + 1) * E], rT[:, i * 128:i * 128 + 128], router[:], start=True, stop=True)
                    done.then_inc(s["lg_ready"], 1)
                if real(n):
                    need(pe, s["gate_done"], n)
                    for c in range(2):
                        done = product(gate_bank[:, c * 256:c * 256 + 256], part(hid, HID + c * 128, 128), part(normed_, 0, 256))
                    done.then_inc(s["gate_ready"], 1)
                if real(n):
                    pe.wait_ge(s["q_k_done"], n + 1)
                    need(pe, s["weighed_done"], n)
                    nc.tensor.matmul(sim_bank[:, 0:256], k_[:, 0:128], q[:], start=True, stop=True)
                    nc.tensor.matmul(sim_bank[:, 256:384], k_[:, 128:256], q[:, 128:256], start=True, stop=True).then_inc(s["sim_ready"], 1)
                if real(n - 1):
                    pe.wait_ge(s["gated_done"], n)
                    need(pe, s["yT_done"], n - 1)
                    for c in range(2):
                        done = nc.tensor.matmul(y_bank[:, 0:256], w_out[:, c * D:(c + 1) * D], gated[:, c * 256:c * 256 + 256], start=c == 0, stop=c == 1)
                    done.then_inc(s["y_ready"], 1)
                if real(n - 3):
                    pe.wait_ge(s["hot_ready"], n - 2)
                    nc.tensor.matmul(yt_bank[:, 0:E], before_b[:], hot_b[:, 0:E], start=True, stop=True)
                    nc.tensor.matmul(yt_bank[:, E:2 * E], ones_b[:], hot_b[:, 0:E], start=True, stop=False)
                    nc.tensor.matmul(yt_bank[:, E:2 * E], before_b[:], hot_b[:, E:2 * E], start=False, stop=True)
                    nc.tensor.matmul(yt_bank[:, 2 * E:3 * E], ones_b[:], hot_b[:, 0:E], start=True, stop=False)
                    nc.tensor.matmul(yt_bank[:, 2 * E:3 * E], ones_b[:], hot_b[:, E:2 * E], start=False, stop=True).then_inc(s["rk_ready"], 1)
                if real(n + 1):
                    pe.wait_ge(s["n_done"], n + 2)
                    need(pe, s["nT_split"], n + 1)
                    for i in range(2):
                        done = nc.tensor.transpose(misc[:, i * 128:i * 128 + 128], normed_rows[:, i * 128:i * 128 + 128], ident)
                    done.then_inc(s["nt_ready"], 1)
                if real(n - 1):
                    pe.wait_ge(s["yT_done"], n)
                    need(pe, s["x3_done"], n - 1)
                    need(pe, s["rk_taken"], last(n - 3) + 1)
                    for i in range(2):
                        done = nc.tensor.transpose(yt_bank[:, i * 128:i * 128 + 128], yT[:, i * 128:i * 128 + 128], ident)
                    done.then_inc(s["yt_ready"], 1)

            batches(pe, body)

        @block.scalar
        def _(act):
            act.wait_ge(s["weights_in"], 16 * LOADS)

            def normed(k, kind, to, source):
                for i in range(2):
                    done = nc.scalar.activation(to[:, i * 128:i * 128 + 128], source[i], ACT.Identity, scale=rstd[:, 2 * k + i:2 * k + i + 1],
                                                bias=offset[:, 2 * k + i:2 * k + i + 1])
                done.then_inc(s[f"z_{kind}_done"], 1)

            def tiles_of_x(owner):
                return [x[:, cols(owner * 256 + i * 128, 128)] for i in range(2)]

            def body(n):
                turn = n + 4
                if real(n):
                    act.wait_ge(s["qk_ready"], n + 1)
                    need(act, s["q_k_done"], n)
                    nc.scalar.activation(qk[:], qk_bank[:, 0:256], ACT.Silu, bias=col[:, QK_B:QK_B + 1]).then_inc(s["qk_done"], 1)
                if real(n - 3):
                    act.wait_ge(s["ht_ready"], n - 2)
                    need(act, s["lg_ready"], n - 3)
                    nc.scalar.copy(rT[:], yt_bank[:, 0:256]).then_inc(s["rT_done"], 1)
                act.wait_ge(s["newton"], turn + 1)
                if real(n + 1):
                    need(act, s["n_scaled"], n + 1)
                    normed(1, "e", z_e, [h[:, i * 128:i * 128 + 128] for i in range(2)])
                if real(n + 2):
                    need(act, s["h_scaled"], n + 2)
                    normed(0, "d", z_d, tiles_of_x(n + 2))
                if real(n - 2):
                    need(act, s["send_scaled"], n - 2)
                    normed(2, "f", z_f, tiles_of_x(n - 2))
                if real(n):
                    act.wait_ge(s["v_ready"], n + 1)
                    need(act, s["pv_ready"], n)
                    nc.scalar.activation(v[:], v_bank[:], ACT.Silu).then_inc(s["v_done"], 1)
                    act.wait_ge(s["gate_ready"], n + 1)
                    need(act, s["gated_done"], n)
                    for c in range(2):
                        done = nc.scalar.activation(gate[:, c * 256:c * 256 + 256], gate_bank[:, c * 256:c * 256 + 256], ACT.Silu, bias=col[:, GATE_B + c:GATE_B + c + 1])
                    done.then_inc(s["gate_done"], 1)
                if real(n - 1):
                    act.wait_ge(s["y_ready"], n)
                    need(act, s["yt_ready"], n - 1)
                    nc.scalar.activation(yT[:], y_bank[:, 0:256], ACT.Identity, scale=mod_col[1][:, cols(GA * B + n - 1, 1)],
                                         bias=out_bias[:, cols(n - 1, 1)]).then_inc(s["yT_done"], 1)
                if real(n):
                    act.wait_ge(s["weighed_done"], n + 1)
                    need(act, s["pv_ready"], n)
                    nc.scalar.activation(attn[:], weighed[:], ACT.Square).then_inc(s["attn_done"], 1)
                if real(n + 1):
                    act.wait_ge(s["nt_ready"], n + 2)
                    need(act, s["gate_ready"], n + 1)
                    nc.scalar.copy(n_high[:], misc[:, 0:256]).then_inc(s["nT_high"], 1)

                if isinstance(n, int) and 0 <= n < 2:
                    split_experts_high(nc, act, raw_experts, range(2 * n, 2 * n + 2), weights[0], s["experts_in"], EXPERT_LOADS, s["experts_high"])

            batches(act, body)

        @block.vector
        def _(dve):
            steps = [0]

            def then(instruction):
                steps[0] += 1
                instruction.then_inc(s["setup_steps"], 1)
                dve.wait_ge(s["setup_steps"], steps[0])

            nc.vector.memset(send[:], 0.0)
            then(nc.vector.memset(moments[:], 1.0))
            nc.vector.tensor_copy(counts[:], const[:, C_REGION:C_REGION + E])
            nc.vector.tensor_copy(before_b[:], const[:, C_BEFORE:C_BEFORE + 128])
            nc.vector.tensor_copy(ones_b[:], const[:, C_ONES:C_ONES + 128])
            dve.wait_ge(s["weights_in"], 16 * LOADS)
            nc.vector.tensor_copy(first_row[:], const[:, C_FIRST:C_FIRST + 128])
            nc.vector.tensor_scalar(out_bias[:], mod_col[1][:, GA * B:(GA + 1) * B], col[:, OUT_B:OUT_B + 1], None, ALU.mult)
            for raw, high, low in ((raw_hidden, hid_high, hid_low), (raw_qk, wqk_high, wqk_low), (v_bias, bias_high, bias_low)):
                then(nc.vector.tensor_copy(high[:], raw[:]))
                then(nc.vector.tensor_tensor(low[:], raw[:], high[:].bitcast(F32), ALU.subtract))
            dve.sem_inc(s["split_done"], 1)

            def rows_of(owner):
                return x[:, cols(owner * 256, 256)]

            def statistics(k, kind, owner, source):
                for i in range(2):
                    done = nc.vector.bn_stats(stats[:, 12 * k + 6 * i:12 * k + 6 * i + 6], source[i])
                done.then_inc(s["parts_" + kind], 1)
                wait_apart(dve, s["parts_" + kind], owner + 1, s["passed_dve"])
                for i in range(2):
                    done = nc.vector.bn_aggr(moments[:, 4 * k + 2 * i:4 * k + 2 * i + 2], stats[:, 12 * k + 6 * i:12 * k + 6 * i + 6])
                done.then_inc(s["stats_" + kind], 1)

            def tiles_of_x(owner):
                return [x[:, cols(owner * 256 + i * 128, 128)] for i in range(2)]

            STEPS = 3 + 3 * NEWTON
            two = moments[:].rearrange("p (k two) -> p k two", two=2)

            def guess_step(turn, step):
                need(dve, s["newton_steps"], STEPS * turn + step)
                if step == 0:
                    done = nc.vector.tensor_scalar(var[:], two[:, :, 1], EPS, None, ALU.add)
                elif step == 1:
                    nc.vector.tensor_scalar(neg_half[:], var[:], -0.5, None, ALU.mult)
                    done = nc.vector.tensor_scalar(half_bits[:], var[:].bitcast(mybir.dt.int32), 1, None, ALU.logical_shift_right)
                else:
                    done = nc.vector.tensor_scalar(guess_bits[:], half_bits[:], -1.0, float(0x5F3759DF), ALU.mult, ALU.add)
                done.then_inc(s["newton_steps"], 1)

            def newton_step(turn, k, step):
                dve.wait_ge(s["newton_steps"], STEPS * turn + 3 * (k + 1) + step)
                now = guess[:] if k else guess_bits[:].bitcast(F32)
                if step == 0:
                    done = nc.vector.tensor_tensor(square[:], now, now, ALU.mult)
                elif step == 1:
                    done = nc.vector.tensor_tensor(square[:], square[:], neg_half[:], ALU.mult)
                else:
                    done = nc.vector.scalar_tensor_tensor(rstd[:] if k == NEWTON - 1 else guess[:], square[:], 1.5, now, ALU.add, ALU.mult)
                done.then_inc(s["newton_steps"], 1)

            def body(n):
                turn = n + 4
                if real(n - 2):
                    dve.wait_ge(s["stats_f"], last(n - 2) + 1)
                else:
                    need(dve, s["stats_d"], last(n + 2) + 1)
                    need(dve, s["stats_e"], last(n + 1) + 1)
                for step in range(3):
                    guess_step(turn, step)
                newton_step(turn, 0, 0)
                newton_step(turn, 0, 1)
                newton_step(turn, 0, 2)
                newton_step(turn, 1, 0)
                if real(n):
                    dve.wait_ge(s["qk_done"], n + 1)
                    need(dve, s["sim_ready"], n)
                    nc.vector.tensor_scalar(q[:], qk[:], col[:, GAMMA:GAMMA + 1], col[:, BETA:BETA + 1], ALU.mult, ALU.add)
                newton_step(turn, 1, 1)
                if real(n):
                    nc.vector.tensor_scalar(k_[:], qk[:], col[:, GAMMA + 1:GAMMA + 2], col[:, BETA + 1:BETA + 2], ALU.mult, ALU.add).then_inc(s["q_k_done"], 1)
                newton_step(turn, 1, 2)
                newton_step(turn, 2, 0)
                if real(n + 3):
                    wait_apart(dve, s["x2_done"], n + 4, s["passed_dve"])
                    nc.vector.bn_stats(stats[:, 0:6], tiles_of_x(n + 3)[0])
                newton_step(turn, 2, 1)
                if real(n + 3):
                    nc.vector.bn_stats(stats[:, 6:12], tiles_of_x(n + 3)[1]).then_inc(s["parts_d"], 1)
                need(dve, s["z_f_done"], min(n - 2, B) if isinstance(n, int) else n - 2)
                need(dve, s["z_e_done"], min(n + 1, B) if isinstance(n, int) else n + 1)
                need(dve, s["z_d_done"], min(n + 2, B) if isinstance(n, int) else n + 2)
                newton_step(turn, 2, 2)
                if real(n - 1):
                    dve.wait_ge(s["pv_ready"], n)
                    dve.wait_ge(s["gate_done"], n)
                    need(dve, s["y_ready"], n - 1)
                    nc.vector.tensor_tensor(gated[:, 0:256], pv_bank[:, 0:256], gate[:, 0:256], ALU.mult)
                dve.wait_ge(s["newton_steps"], STEPS * turn + STEPS)
                nc.vector.scalar_tensor_tensor(offset[:], two[:, :, 0], -1.0, rstd[:], ALU.mult, ALU.mult).then_inc(s["newton"], 1)
                if real(n - 1):
                    nc.vector.tensor_tensor(gated[:, 256:512], pv_bank[:, 256:512], gate[:, 256:512], ALU.mult).then_inc(s["gated_done"], 1)
                if real(n + 3):
                    dve.wait_ge(s["parts_d"], n + 4)
                    wait_apart(dve, s["newton"], turn + 1, s["passed_dve"])
                    for i in range(2):
                        done = nc.vector.bn_aggr(moments[:, 2 * i:2 * i + 2], stats[:, 6 * i:6 * i + 6])
                    done.then_inc(s["stats_d"], 1)
                if real(n - 3):
                    dve.wait_ge(s["lg_ready"], n - 2)
                    nc.vector.tensor_tensor(logits[:].rearrange("p (i e) -> p i e", e=8), yt_bank[:, 0:16].rearrange("p (i e) -> p i e", e=8),
                                            router_bias[:].unsqueeze(1).broadcast_to([128, 2, 8]), ALU.add).then_inc(s["logits_done"], 1)
                    wait_apart(dve, s["logits_done"], n - 2, s["passed_dve"])
                    for i in range(2):
                        done = nc.vector.max(top[:, i * 8:i * 8 + 8], logits[:, i * 8:i * 8 + 8])
                    done.then_inc(s["top_done"], 1)
                if real(n - 3):
                    wait_apart(dve, s["top_done"], n - 2, s["passed_dve"])
                    for i in range(2):
                        nc.vector.max_index(top_at[:, i * 8:i * 8 + 8], top[:, i * 8:i * 8 + 8], logits[:, i * 8:i * 8 + 8])
                    for i in range(2):
                        done = nc.vector.tensor_scalar(shifted[:, cols((2 * (n - 3) + i) * E, E)], logits[:, i * 8:i * 8 + 8], top[:, i * 8:i * 8 + 1], None, ALU.subtract)
                    done.then_inc(s["top_at_done"], 1)
                    dve.wait_ge(s["top_at_done"], n - 2)
                    nc.vector.tensor_copy(expert[:], top_at[:].rearrange("p (i e) -> p i e", e=8)[:, :, 0]).then_inc(s["expert_done"], 1)
                    dve.wait_ge(s["expert_done"], n - 2)
                    for i in range(2):
                        done = nc.vector.tensor_scalar(hot[:, i * 8:i * 8 + 8], const[:, C_INDEX:C_INDEX + E], expert[:, i:i + 1], None, ALU.is_equal)
                    done.then_inc(s["hot_done"], 1)
                    dve.wait_ge(s["hot_done"], n - 2)
                    need(dve, s["rk_ready"], n - 3)
                    nc.vector.tensor_copy(hot_b[:], hot[:]).then_inc(s["hot_ready"], 1)
                if real(n):
                    dve.wait_ge(s["sim_ready"], n + 1)
                    need(dve, s["attn_done"], n)
                    nc.vector.scalar_tensor_tensor(weighed[:], sim_bank[:, 0:384], 0.0, const[:, C_CAUSAL:C_CAUSAL + 384], ALU.max, ALU.mult).then_inc(s["weighed_done"], 1)
                if real(n - 3):
                    dve.wait_ge(s["rk_ready"], n - 2)
                    nc.vector.tensor_tensor(place[:].rearrange("p (i e) -> p i e", e=8), yt_bank[:, 0:16].rearrange("p (i e) -> p i e", e=8),
                                            counts[:].unsqueeze(1).broadcast_to([128, 2, 8]), ALU.add).then_inc(s["place_made"], 1)
                    dve.wait_ge(s["place_made"], n - 2)
                    nc.vector.tensor_tensor(counts[:], yt_bank[:, 16:24], counts[:], ALU.add).then_inc(s["rk_taken"], 1)
                    nc.vector.tensor_tensor(picked[:], place[:], hot[:], ALU.mult).then_inc(s["picked_done"], 1)
                    dve.wait_ge(s["picked_done"], n - 2)
                    nc.vector.tensor_reduce(place_f[:], picked[:].rearrange("p (i e) -> p i e", e=8), AX.X, ALU.add).then_inc(s["place_summed"], 1)
                    dve.wait_ge(s["place_summed"], n - 2)
                    need(dve, sent_done, 32 * (n - 3))
                    nc.vector.tensor_copy(send[:].bitcast(U32).rearrange("p (i w) -> p i w", w=SENT)[:, :, TOKEN], token[:, cols(2 * (n - 3), 2)])
                    nc.vector.tensor_copy(rows_now[:], place_f[:]).then_inc(s["place_done"], 1)
                if real(n + 2):
                    dve.wait_ge(s["h_done"], n + 3)
                    statistics(1, "e", n + 2, [h[:, i * 128:i * 128 + 128] for i in range(2)])
                if real(n - 1):
                    dve.wait_ge(s["yt_ready"], n)
                    dve.wait_ge(s["x_h_done"], n)
                    nc.vector.tensor_tensor(rows_of(n - 1), yt_bank[:, 0:256], rows_of(n - 1), ALU.add).then_inc(s["x3_done"], 1)
                if real(n + 1):
                    dve.wait_ge(s["nT_high"], n + 2)
                    nc.vector.tensor_tensor(n_low[:], misc[:, 0:256], n_high[:].bitcast(F32), ALU.subtract).then_inc(s["nT_split"], 1)
                if real(n - 1):
                    wait_apart(dve, s["x3_done"], n, s["passed_dve"])
                    statistics(2, "f", n - 1, tiles_of_x(n - 1))

            batches(dve, body)

        @block.gpsimd
        def _(pool):
            def over_tiles(row):
                return row.unsqueeze(1).broadcast_to([128, 2, D])

            def tiles(buffer):
                return buffer.rearrange("p (i d) -> p i d", d=D)

            def affine(source, scale, shift, to, scaled, done, count):
                nc.gpsimd.tensor_tensor(to, tiles(source), over_tiles(scale), ALU.mult).then_inc(s[scaled], 1)
                pool.wait_ge(s[scaled], count)
                nc.gpsimd.tensor_tensor(to, to, over_tiles(shift), ALU.add).then_inc(s[done], 1)

            sent_rows = send[:].rearrange("p (i w) -> p i w", w=SENT)[:, :, 0:D]

            def body(n):
                if real(n + 3):
                    pool.wait_ge(s["got_in"], 16 * (n + 4))
                    pool.wait_ge(s["mod_d_in"], 16 * (n + 4))
                    nc.gpsimd.tensor_tensor(tiles(got[:]), tiles(got[:]), over_tiles(mod_d[:]), ALU.mult).then_inc(s["x2_gated"], 1)
                    pool.wait_ge(s["x2_gated"], n + 4)
                    now = x[:, cols((n + 3) * 256, 256)]
                    nc.gpsimd.tensor_tensor(now, got[:], now, ALU.add).then_inc(s["x2_done"], 1)
                if real(n - 3):
                    pool.wait_ge(s["z_f_done"], n - 2)
                    pool.wait_ge(s["mod_f_in"], 16 * (n - 2))
                    need(pool, sent_done, 32 * (n - 3))
                    need(pool, s["ht_ready"], n - 3)
                    affine(z_f[:], mod_f[:, D:2 * D], mod_f[:, 0:D], sent_rows, "send_scaled", "send_done", n - 2)
                if real(n + 1):
                    pool.wait_ge(s["h_done"], n + 2)
                    pool.wait_ge(s["mod_g_in"], 16 * (n + 2))
                    need(pool, s["x_h_done"], n + 1)
                    nc.gpsimd.tensor_tensor(tiles(gh[:]), tiles(h[:]), over_tiles(mod_g[:]), ALU.mult).then_inc(s["gh_done"], 1)
                    pool.wait_ge(s["gh_done"], n + 2)
                    now = x[:, cols((n + 1) * 256, 256)]
                    nc.gpsimd.tensor_tensor(now, now, gh[:], ALU.add).then_inc(s["x_h_done"], 1)
                if real(n + 2):
                    pool.wait_ge(s["z_d_done"], n + 3)
                    pool.wait_ge(s["mod_h_in"], 16 * (n + 3))
                    need(pool, s["z_e_done"], n + 2)
                    need(pool, s["gh_done"], last(n + 1) + 1)
                    affine(z_d[:], mod_h[:, CA * D:(CA + 1) * D], mod_h[:, SA * D:(SA + 1) * D], tiles(h[:]), "h_scaled", "h_done", n + 3)
                if real(n + 1):
                    pool.wait_ge(s["z_e_done"], n + 2)
                    need(pool, s["nt_ready"], n + 1)
                    affine(z_e[:], ln_row[:, 0:D], ln_row[:, D:2 * D], tiles(normed_rows[:]), "n_scaled", "n_done", n + 2)
                if real(n - 3):
                    wait_apart(pool, s["place_done"], n - 2, s["passed_pool"])
                    for i in range(2):
                        nc.gpsimd.indirect_dma_start(sent, bass.IndirectOffsetOnAxis(ap=rows_now[:, i:i + 1], axis=0), send[:, i * SENT:(i + 1) * SENT], None).then_inc(sent_done, 16)

                if isinstance(n, int) and 0 <= n < 2:
                    split_experts_low(nc, pool, raw_experts, range(2 * n, 2 * n + 2), weights[0], weights[1], s["experts_high"])

            batches(pool, body)
            pool.wait_ge(sent_done, 32 * B)

        ctx_block.close()
        clear(nc, used)


def combine(nc, out, x, mod_row, back, shifted):
    ctx = ExitStack()
    with ctx:
        def sb(name, columns, kind=F32, rows=128):
            return ctx.enter_context(nc.sbuf_tensor("f_" + name, [rows, columns], kind))

        def sem(name):
            return ctx.enter_context(nc.semaphore("f_" + name))

        weight, exped, total = sb("weight", TILES), sb("exped", TILES * E), sb("total", TILES)
        got = [sb(f"got{n}", 2 * D) for n in range(4)]
        gate = [sb(f"gate{n}", D) for n in range(4)]
        result = [sb(f"result{n}", 2 * D) for n in range(4)]
        s = {n: sem(n) for n in "weighted result_done exp_done summed weight_done".split()}
        got_in = [sem(f"got_in{n}") for n in range(4)]
        gate_in = [sem(f"gate_in{n}") for n in range(4)]
        stored = [sem(f"stored{n}") for n in range(4)]
        out_rows = out.rearrange("b (i p) d -> b p i d", p=128)
        block = ctx.enter_context(nc.Block())

        def batches(engine, body):
            turns(engine, body, B, 4, 3, 3)

        @block.sync
        def _(sp):
            def body(n, k, i):
                if real(n + 3):
                    m = (k + 3) % 4
                    need(sp, s["result_done"], n)
                    sp.dma_start(got[m][:].rearrange("p (i d) -> p i d", d=D), back[cols((n + 3) * 256, 256), :].rearrange("(i p) d -> p i d", p=128)).then_inc(got_in[m], 16)
                    sp.dma_start(gate[m][:], mod_row[cols(n + 3, 1), GB * D:6 * D].broadcast_to([128, D])).then_inc(gate_in[m], 16)

            batches(sp, body)

        @block.vector
        def _(dve):
            def body(n, k, i):
                if real(n):
                    dve.wait_ge(got_in[k], 16 * (i + 1))
                    dve.wait_ge(gate_in[k], 16 * (i + 1))
                    for j in range(2):
                        mine = got[k][:, j * D:(j + 1) * D]
                        done = nc.vector.scalar_tensor_tensor(mine, mine, weight[:, cols(2 * n + j, 1)], gate[k][:], ALU.mult, ALU.mult)
                    done.then_inc(s["weighted"], 1)
                    dve.wait_ge(s["weighted"], n + 1)
                    need(dve, stored[k], 16 * i)
                    nc.vector.tensor_tensor(result[k][:], got[k][:], x[:, cols(n * 256, 256)], ALU.add).then_inc(s["result_done"], 1)

            dve.wait_ge(s["exp_done"], 1)
            nc.vector.tensor_reduce(total[:], exped[:].rearrange("p (t e) -> p t e", e=E), AX.X, ALU.add).then_inc(s["summed"], 1)
            dve.wait_ge(s["summed"], 1)
            nc.vector.reciprocal(weight[:], total[:]).then_inc(s["weight_done"], 1)
            dve.wait_ge(s["weight_done"], 1)
            batches(dve, body)

        @block.scalar
        def _(act):
            nc.scalar.activation(exped[:], shifted[:], ACT.Exp).then_inc(s["exp_done"], 1)

            def body(n, k, i):
                if real(n):
                    act.wait_ge(s["result_done"], n + 1)
                    act.dma_start(out_rows[cols(n, 1)].squeeze(0), result[k][:].rearrange("p (i d) -> p i d", d=D)).then_inc(stored[k], 16)

            batches(act, body)
            for k in range(4):
                act.wait_ge(stored[k], 16 * (B // 4))


INPUTS = ["L0_attn_x", "L0_attn_Wqkv", "L0_attn_Wout", "L0_ffn_ln_w", "L0_ffn_ln_b", "L0_ffn_router_w", "L0_ffn_gate_w", "L0_ffn_up_w",
          "L0_ffn_down_w", "L0_ffn_sh_gate", "L0_ffn_sh_up", "L0_ffn_sh_down", "L0_wmod", "L1_attn_ln_g", "L1_attn_ln_b", "L1_attn_W_hidden",
          "L1_attn_b_hidden", "L1_attn_W_qk", "L1_attn_b_qk", "L1_attn_os_gamma", "L1_attn_os_beta", "L1_attn_W_out", "L1_attn_b_out",
          "L1_ffn_Wr", "L1_ffn_br", "L1_ffn_W1", "L1_ffn_b1", "L1_ffn_W2", "L1_ffn_b2", "L1_wmod"]


def kernel(**inputs):
    import numpy as np
    import concourse.bacc as bacc
    from concourse import mybir as m
    from concourse.bass_utils import run_bass_kernel_spmd as run

    nc = bacc.Bacc("TRN2", target_bir_lowering=False, num_devices=1)
    arrays = {name: np.ascontiguousarray(inputs[name]) for name in INPUTS}
    arrays["c0T"] = np.ascontiguousarray(np.asarray(inputs["L0_c"]).T)
    arrays["c1T"] = np.ascontiguousarray(np.asarray(inputs["L1_c"]).T)
    arrays["consts"] = constants()
    t = {name: nc.dram_tensor("in_" + name, a.shape, m.dt.from_np(a.dtype), kind="ExternalInput").ap() for name, a in arrays.items()}
    out = nc.dram_tensor("out", [B, S, D], F32, kind="ExternalOutput").ap()
    program(nc, t, out)
    r = run(nc, [{"in_" + name: a for name, a in arrays.items()}], core_ids=[0])
    return r.results[0]["out"]
```
